# Optimizing a Trainium2 kernel written in Bass

```python
import numpy as np
import jax
import jax.numpy as jnp

def _softmax(x, axis=-1):
    return jax.nn.softmax(x, axis=axis)

def _gelu(x):
    return jax.nn.gelu(x, approximate=True)

def _silu(x):
    return jax.nn.silu(x)

def _sigmoid(x):
    return jax.nn.sigmoid(x)

def _layernorm(x, axis=-1, eps=1e-05):
    m = jnp.mean(x, axis=axis, keepdims=True)
    v = jnp.var(x, axis=axis, keepdims=True)
    return (x - m) / jnp.sqrt(v + eps)

def _scatter_add(tgt, idx, src, axis=0):
    return tgt.at[idx].add(src)

def _segment_sum(src, seg, n):
    return jax.ops.segment_sum(src, seg, n)
kernel_name = 'mk_hybrid_d1_jaxref_r8_ef65d2'

def setup_inputs(seed: int=0):
    np.random.seed(seed)
    _w = jnp.asarray

    def _L0_attn_a_setup():
        import jax, jax.numpy as jnp
        import numpy as np
        EMBED_DIM = 128
        NUM_HEADS = 16
        HEAD_DIM = EMBED_DIM // NUM_HEADS
        SCALE = HEAD_DIM ** (-0.5)
        B, N = (2, 256)
        key = jax.random.key(seed)
        k1, k2, k3 = jax.random.split(key, 3)
        x = jax.random.normal(k1, (B, N, EMBED_DIM), dtype=jnp.float32)
        w_qkv = jax.random.normal(k2, (EMBED_DIM, 3 * EMBED_DIM), dtype=jnp.float32) * EMBED_DIM ** (-0.5)
        b_qkv = jnp.zeros((3 * EMBED_DIM,), dtype=jnp.float32)
        w_proj = jax.random.normal(k3, (EMBED_DIM, EMBED_DIM), dtype=jnp.float32) * EMBED_DIM ** (-0.5)
        b_proj = jnp.zeros((EMBED_DIM,), dtype=jnp.float32)
        return {'x': x, 'w_qkv': w_qkv, 'b_qkv': b_qkv, 'w_proj': w_proj, 'b_proj': b_proj}
    _L0_attn_a_in = _L0_attn_a_setup()

    def _L0_attn_b_setup():
        import jax, jax.numpy as jnp
        import numpy as np
        B, T, D, H, R = (4, 512, 128, 16, 32)
        DH = D // H
        key = jax.random.key(seed)
        ks = jax.random.split(key, 5)
        s = 0.02
        return {'x': jax.random.normal(ks[0], (B, T, D), dtype=jnp.float32), 'Wq': jax.random.normal(ks[1], (D, D), dtype=jnp.float32) * s, 'bq': jnp.zeros((D,), dtype=jnp.float32), 'Wd': jax.random.normal(ks[2], (D, R), dtype=jnp.float32) * s, 'bd': jnp.zeros((R,), dtype=jnp.float32), 'Wu': jax.random.normal(ks[3], (R, 2 * D), dtype=jnp.float32) * s, 'bu': jnp.zeros((2 * D,), dtype=jnp.float32), 'Wo': jax.random.normal(ks[4], (D, D), dtype=jnp.float32) * s, 'bo': jnp.zeros((D,), dtype=jnp.float32)}
    _L0_attn_b_in = _L0_attn_b_setup()

    def _L0_ffn_setup():
        import jax, jax.numpy as jnp
        import numpy as np
        DIM = 128
        DEPTH = 2
        HEADS = 8
        DIM_HEAD = 64
        WINDOW = 64
        INNER = HEADS * DIM_HEAD
        HID = int(DIM * 4 * 2 / 3)
        B, N = (2, 1024)
        QK_SCALE = 8.0

        def shift_token(t):
            t1, t2 = jnp.split(t, 2, axis=-1)
            t2 = jnp.pad(t2, ((0, 0), (1, 0), (0, 0)))[:, :-1]
            return jnp.concatenate([t1, t2], axis=-1)

        def l2norm(t):
            return t / jnp.clip(jnp.linalg.norm(t, axis=-1, keepdims=True), 1e-12)

        def rotate_half(x):
            x1, x2 = jnp.split(x, 2, axis=-1)
            return jnp.concatenate([-x2, x1], axis=-1)

        def rotary_xpos(q, k):
            n = q.shape[-2]
            half_idx = jnp.arange(0, DIM_HEAD, 2, dtype=jnp.float32)
            inv_freq = 1.0 / 10000.0 ** (half_idx / DIM_HEAD)
            t = jnp.arange(n, dtype=jnp.float32)
            freqs = t[:, None] * inv_freq[None, :]
            freqs = jnp.concatenate([freqs, freqs], axis=-1)
            base = (half_idx + 0.4 * DIM_HEAD) / (1.4 * DIM_HEAD)
            power = (t - n // 2) / float(WINDOW // 2)
            scale = base[None, :] ** power[:, None]
            scale = jnp.concatenate([scale, scale], axis=-1)
            cos, sin = (jnp.cos(freqs), jnp.sin(freqs))
            q = q * cos * scale + rotate_half(q) * sin * scale
            k = k * cos / scale + rotate_half(k) * sin / scale
            return (q, k)

        def local_attention(q, k, v):
            b, h, n, d = q.shape
            w = n // WINDOW
            bq = q.reshape(b, h, w, WINDOW, d) * QK_SCALE
            bk = k.reshape(b, h, w, WINDOW, d)
            bv = v.reshape(b, h, w, WINDOW, d)

            def look_around(t):
                p = jnp.pad(t, ((0, 0), (0, 0), (1, 0), (0, 0), (0, 0)))
                return jnp.concatenate([p[:, :, :w], p[:, :, 1:]], axis=3)
            bk, bv = (look_around(bk), look_around(bv))
            bt = jnp.arange(n).reshape(w, WINDOW)
            btp = jnp.pad(bt, ((1, 0), (0, 0)), constant_values=-1)
            btk = jnp.concatenate([btp[:w], btp[1:]], axis=1)
            sim = jnp.einsum('bhwid,bhwjd->bhwij', bq, bk)
            i = bt[:, :, None]
            j = btk[:, None, :]
            mask = (i < j) | (i > j + WINDOW) | (j == -1)
            sim = jnp.where(mask, -jnp.finfo(sim.dtype).max, sim)
            attn = jax.nn.softmax(sim, axis=-1)
            out = jnp.einsum('bhwij,bhwjd->bhwid', attn, bv)
            return out.reshape(b, h, n, d)

        def _layer(x, wqkv, qs, ksc, wo, lg, lb, w1, b1, w2, b2):
            b, n, _ = x.shape
            h = shift_token(x)
            qkv = h @ wqkv
            q, k, v = jnp.split(qkv, 3, axis=-1)
            to_heads = lambda t: t.reshape(b, n, HEADS, DIM_HEAD).transpose(0, 2, 1, 3)
            q, k, v = (to_heads(q), to_heads(k), to_heads(v))
            q = l2norm(q) * qs
            k = l2norm(k) * ksc
            q, k = rotary_xpos(q, k)
            o = local_attention(q, k, v)
            o = o.transpose(0, 2, 1, 3).reshape(b, n, INNER)
            x = x + o @ wo
            h = shift_token(x)
            mu = h.mean(-1, keepdims=True)
            var = h.var(-1, keepdims=True)
            h = (h - mu) / jnp.sqrt(var + 1e-05) * lg + lb
            h = h @ w1 + b1
            a, g = jnp.split(h, 2, axis=-1)
            h = a * jax.nn.gelu(g, approximate=False)
            x = x + h @ w2 + b2
            return x
        key = jax.random.key(seed)
        ks = jax.random.split(key, 6)
        return {'x': jax.random.normal(ks[0], (B, N, DIM), jnp.float32), 'wqkv': jax.random.normal(ks[1], (DEPTH, DIM, 3 * INNER), jnp.float32) * 0.02, 'q_scale': jnp.ones((DEPTH, DIM_HEAD), jnp.float32), 'k_scale': jnp.ones((DEPTH, DIM_HEAD), jnp.float32), 'wo': jax.random.normal(ks[2], (DEPTH, INNER, DIM), jnp.float32) * 0.02, 'ln_g': jnp.ones((DEPTH, DIM), jnp.float32), 'ln_b': jnp.zeros((DEPTH, DIM), jnp.float32), 'w1': jax.random.normal(ks[3], (DEPTH, DIM, 2 * HID), jnp.float32) * 0.02, 'b1': jnp.zeros((DEPTH, 2 * HID), jnp.float32), 'w2': jax.random.normal(ks[4], (DEPTH, HID, DIM), jnp.float32) * 0.02, 'b2': jnp.zeros((DEPTH, DIM), jnp.float32)}
    _L0_ffn_in = _L0_ffn_setup()
    _d = {'L0_attn_a_x': _L0_attn_a_in['x'], 'L0_attn_a_w_qkv': _L0_attn_a_in['w_qkv'], 'L0_attn_a_b_qkv': _L0_attn_a_in['b_qkv'], 'L0_attn_a_w_proj': _L0_attn_a_in['w_proj'], 'L0_attn_a_b_proj': _L0_attn_a_in['b_proj'], 'L0_attn_b_Wq': _L0_attn_b_in['Wq'], 'L0_attn_b_bq': _L0_attn_b_in['bq'], 'L0_attn_b_Wd': _L0_attn_b_in['Wd'], 'L0_attn_b_bd': _L0_attn_b_in['bd'], 'L0_attn_b_Wu': _L0_attn_b_in['Wu'], 'L0_attn_b_bu': _L0_attn_b_in['bu'], 'L0_attn_b_Wo': _L0_attn_b_in['Wo'], 'L0_attn_b_bo': _L0_attn_b_in['bo'], 'L0_ffn_wqkv': _L0_ffn_in['wqkv'], 'L0_ffn_q_scale': _L0_ffn_in['q_scale'], 'L0_ffn_k_scale': _L0_ffn_in['k_scale'], 'L0_ffn_wo': _L0_ffn_in['wo'], 'L0_ffn_ln_g': _L0_ffn_in['ln_g'], 'L0_ffn_ln_b': _L0_ffn_in['ln_b'], 'L0_ffn_w1': _L0_ffn_in['w1'], 'L0_ffn_b1': _L0_ffn_in['b1'], 'L0_ffn_w2': _L0_ffn_in['w2'], 'L0_ffn_b2': _L0_ffn_in['b2']}
    _x0 = _d['L0_attn_a_x']
    _d['L0_attn_a_x'] = jax.random.normal(jax.random.fold_in(jax.random.key(seed), 1), (4, 512, 128), dtype=_x0.dtype)
    del _x0
    return _d

def reference(L0_attn_a_x, L0_attn_a_w_qkv, L0_attn_a_b_qkv, L0_attn_a_w_proj, L0_attn_a_b_proj, L0_attn_b_Wq, L0_attn_b_bq, L0_attn_b_Wd, L0_attn_b_bd, L0_attn_b_Wu, L0_attn_b_bu, L0_attn_b_Wo, L0_attn_b_bo, L0_ffn_wqkv, L0_ffn_q_scale, L0_ffn_k_scale, L0_ffn_wo, L0_ffn_ln_g, L0_ffn_ln_b, L0_ffn_w1, L0_ffn_b1, L0_ffn_w2, L0_ffn_b2):

    def _L0_attn_a_ref(x, w_qkv, b_qkv, w_proj, b_proj):
        import jax, jax.numpy as jnp
        import numpy as np
        EMBED_DIM = 128
        NUM_HEADS = 16
        HEAD_DIM = EMBED_DIM // NUM_HEADS
        SCALE = HEAD_DIM ** (-0.5)
        B, N = (2, 256)
        b, n, c = x.shape
        qkv = x @ w_qkv + b_qkv
        qkv = qkv.reshape(b, n, 3, NUM_HEADS, HEAD_DIM)
        qkv = jnp.transpose(qkv, (2, 0, 3, 1, 4))
        q, k, v = (qkv[0], qkv[1], qkv[2])
        attn = jnp.einsum('bhnd,bhmd->bhnm', q, k) * SCALE
        attn = jax.nn.softmax(attn, axis=-1)
        out = jnp.einsum('bhnm,bhmd->bhnd', attn, v)
        out = jnp.transpose(out, (0, 2, 1, 3)).reshape(b, n, c)
        return out @ w_proj + b_proj

    def _L0_attn_b_ref(x, Wq, bq, Wd, bd, Wu, bu, Wo, bo):
        import jax, jax.numpy as jnp
        import numpy as np
        B, T, D, H, R = (4, 512, 128, 16, 32)
        DH = D // H
        b, t = (x.shape[0], x.shape[1])
        q = (x @ Wq + bq).reshape(b, t, H, DH)
        kv = ((x @ Wd + bd) @ Wu + bu).reshape(b, t, H, 2 * DH)
        k, v = (kv[..., :DH], kv[..., DH:])
        q = jax.nn.elu(q) + 1.0
        k = jax.nn.elu(k) + 1.0
        context = jnp.einsum('bthd,bthe->bhde', k, v)
        out = jnp.einsum('bthd,bhde->bthe', q, context)
        k_sum = k.sum(axis=1)
        z = 1.0 / (jnp.einsum('bthd,bhd->bth', q, k_sum) + 1e-06)
        out = out * z[..., None]
        return out.reshape(b, t, D) @ Wo + bo

    def _L0_ffn_ref(x, wqkv, q_scale, k_scale, wo, ln_g, ln_b, w1, b1, w2, b2):
        import jax, jax.numpy as jnp
        import numpy as np
        DIM = 128
        DEPTH = 2
        HEADS = 8
        DIM_HEAD = 64
        WINDOW = 64
        INNER = HEADS * DIM_HEAD
        HID = int(DIM * 4 * 2 / 3)
        B, N = (2, 1024)
        QK_SCALE = 8.0

        def shift_token(t):
            t1, t2 = jnp.split(t, 2, axis=-1)
            t2 = jnp.pad(t2, ((0, 0), (1, 0), (0, 0)))[:, :-1]
            return jnp.concatenate([t1, t2], axis=-1)

        def l2norm(t):
            return t / jnp.clip(jnp.linalg.norm(t, axis=-1, keepdims=True), 1e-12)

        def rotate_half(x):
            x1, x2 = jnp.split(x, 2, axis=-1)
            return jnp.concatenate([-x2, x1], axis=-1)

        def rotary_xpos(q, k):
            n = q.shape[-2]
            half_idx = jnp.arange(0, DIM_HEAD, 2, dtype=jnp.float32)
            inv_freq = 1.0 / 10000.0 ** (half_idx / DIM_HEAD)
            t = jnp.arange(n, dtype=jnp.float32)
            freqs = t[:, None] * inv_freq[None, :]
            freqs = jnp.concatenate([freqs, freqs], axis=-1)
            base = (half_idx + 0.4 * DIM_HEAD) / (1.4 * DIM_HEAD)
            power = (t - n // 2) / float(WINDOW // 2)
            scale = base[None, :] ** power[:, None]
            scale = jnp.concatenate([scale, scale], axis=-1)
            cos, sin = (jnp.cos(freqs), jnp.sin(freqs))
            q = q * cos * scale + rotate_half(q) * sin * scale
            k = k * cos / scale + rotate_half(k) * sin / scale
            return (q, k)

        def local_attention(q, k, v):
            b, h, n, d = q.shape
            w = n // WINDOW
            bq = q.reshape(b, h, w, WINDOW, d) * QK_SCALE
            bk = k.reshape(b, h, w, WINDOW, d)
            bv = v.reshape(b, h, w, WINDOW, d)

            def look_around(t):
                p = jnp.pad(t, ((0, 0), (0, 0), (1, 0), (0, 0), (0, 0)))
                return jnp.concatenate([p[:, :, :w], p[:, :, 1:]], axis=3)
            bk, bv = (look_around(bk), look_around(bv))
            bt = jnp.arange(n).reshape(w, WINDOW)
            btp = jnp.pad(bt, ((1, 0), (0, 0)), constant_values=-1)
            btk = jnp.concatenate([btp[:w], btp[1:]], axis=1)
            sim = jnp.einsum('bhwid,bhwjd->bhwij', bq, bk)
            i = bt[:, :, None]
            j = btk[:, None, :]
            mask = (i < j) | (i > j + WINDOW) | (j == -1)
            sim = jnp.where(mask, -jnp.finfo(sim.dtype).max, sim)
            attn = jax.nn.softmax(sim, axis=-1)
            out = jnp.einsum('bhwij,bhwjd->bhwid', attn, bv)
            return out.reshape(b, h, n, d)

        def _layer(x, wqkv, qs, ksc, wo, lg, lb, w1, b1, w2, b2):
            b, n, _ = x.shape
            h = shift_token(x)
            qkv = h @ wqkv
            q, k, v = jnp.split(qkv, 3, axis=-1)
            to_heads = lambda t: t.reshape(b, n, HEADS, DIM_HEAD).transpose(0, 2, 1, 3)
            q, k, v = (to_heads(q), to_heads(k), to_heads(v))
            q = l2norm(q) * qs
            k = l2norm(k) * ksc
            q, k = rotary_xpos(q, k)
            o = local_attention(q, k, v)
            o = o.transpose(0, 2, 1, 3).reshape(b, n, INNER)
            x = x + o @ wo
            h = shift_token(x)
            mu = h.mean(-1, keepdims=True)
            var = h.var(-1, keepdims=True)
            h = (h - mu) / jnp.sqrt(var + 1e-05) * lg + lb
            h = h @ w1 + b1
            a, g = jnp.split(h, 2, axis=-1)
            h = a * jax.nn.gelu(g, approximate=False)
            x = x + h @ w2 + b2
            return x
        for l in range(DEPTH):
            x = _layer(x, wqkv[l], q_scale[l], k_scale[l], wo[l], ln_g[l], ln_b[l], w1[l], b1[l], w2[l], b2[l])
        return x
    x = L0_attn_a_x
    x = x + _L0_attn_a_ref(_layernorm(x, axis=-1), L0_attn_a_w_qkv, L0_attn_a_b_qkv, L0_attn_a_w_proj, L0_attn_a_b_proj)
    x = x + _L0_ffn_ref(_layernorm(x, axis=-1), L0_ffn_wqkv, L0_ffn_q_scale, L0_ffn_k_scale, L0_ffn_wo, L0_ffn_ln_g, L0_ffn_ln_b, L0_ffn_w1, L0_ffn_b1, L0_ffn_w2, L0_ffn_b2)
    x = x + _L0_attn_b_ref(_layernorm(x, axis=-1), L0_attn_b_Wq, L0_attn_b_bq, L0_attn_b_Wd, L0_attn_b_bd, L0_attn_b_Wu, L0_attn_b_bu, L0_attn_b_Wo, L0_attn_b_bo)
    x = x + _L0_ffn_ref(_layernorm(x, axis=-1), L0_ffn_wqkv, L0_ffn_q_scale, L0_ffn_k_scale, L0_ffn_wo, L0_ffn_ln_g, L0_ffn_ln_b, L0_ffn_w1, L0_ffn_b1, L0_ffn_w2, L0_ffn_b2)
    return x

_drawn_inputs = setup_inputs


def setup_inputs(seed=0):
    import zlib

    import numpy as np

    out = dict(_drawn_inputs(seed))
    spreads = {'L0_attn_a_b_qkv': (0.0, 0.1),
     'L0_attn_a_b_proj': (0.0, 0.1),
     'L0_attn_b_bq': (0.0, 2.0),
     'L0_attn_b_bd': (0.0, 0.8),
     'L0_attn_b_bu': (0.0, 0.714),
     'L0_attn_b_bo': (0.0, 0.355),
     'L0_ffn_q_scale': (1.0, 0.6),
     'L0_ffn_k_scale': (1.0, 0.6),
     'L0_ffn_ln_g': (1.0, 0.6),
     'L0_ffn_ln_b': (0.0, 0.8),
     'L0_ffn_b1': (0.0, 0.8),
     'L0_ffn_b2': (0.0, 0.1)}
    factors = {'L0_attn_b_Wq': 26.051,
     'L0_attn_b_Wd': 8.0,
     'L0_attn_b_Wu': 8.0,
     'L0_attn_b_Wo': 5.178,
     'L0_ffn_w1': 3.74,
     'L0_ffn_w2': 3.676}
    for name, (base, spread) in spreads.items():
        noise = np.random.default_rng([zlib.crc32(name.encode()), seed]).standard_normal(out[name].shape)
        drawn = base * np.exp(spread * noise) if base else spread * noise
        out[name] = jnp.asarray(drawn.astype(out[name].dtype))
    for name, factor in factors.items():
        out[name] = (out[name] * factor).astype(out[name].dtype)
    return out
```

```python
from contextlib import ExitStack

import numpy as np

import concourse.bass as bass
from concourse import mybir

F32 = mybir.dt.float32
BF16 = mybir.dt.bfloat16
ACT = mybir.ActivationFunctionType
ALU = mybir.AluOpType
AX_X = mybir.AxisListType.X

P = 128
T = 512
NB = 2
BANKS = 8

HA, DA = 16, 8
SLOTS = 9
GUARD_ROW = SLOTS * DA
LAG = 2
HW, DW, WIN = 8, 64, 64
PAIRS = HW // 2
SPAN = P + WIN
HID = 341
HID_BLOCKS = [(0, 128), (128, 128), (256, HID - 256)]
MASKED = -1e30
LN_EPS = 1e-5

_WIDTHS = [("ident", P), ("mean", P), ("cosq", T), ("sinq", T), ("cosk", T), ("sink", T),
           ("pick_num", 4 * P), ("pick_den", 4 * P), ("head_sum", 32), ("spread", 4 * P),
           ("block8", 2 * P), ("ones", DW)]
CONST = {}
_at = 0
for _name, _w in _WIDTHS:
    CONST[_name] = (_at, _at + _w)
    _at += _w
CONST_COLS = _at
CONSTB = {"ident": (0, P), "minus1": (P, 2 * P), "mask_first": (2 * P, 2 * P + SPAN),
          "mask_q": (2 * P + SPAN, 2 * P + 2 * SPAN), "mask_k": (2 * P + 2 * SPAN, 2 * P + 3 * SPAN)}
CONSTB_COLS = 2 * P + 3 * SPAN


def constants():
    c = np.zeros((P, CONST_COLS), np.float32)

    def col(name):
        a, b = CONST[name]
        return c[:, a:b]

    r = np.arange(P)
    col("ident")[:] = np.eye(P)
    col("mean")[:] = 1.0 / P
    half = np.arange(0, DW, 2, dtype=np.float32)
    inv_freq = (1.0 / np.float32(10000.0) ** (half / DW)).astype(np.float32)
    t = np.arange(T, dtype=np.float32)
    freqs = t[:, None] * inv_freq[None, :]
    base = (half + np.float32(0.4 * DW)) / np.float32(1.4 * DW)
    scale = base[None, :] ** ((t - T // 2) / np.float32(WIN // 2))[:, None]
    freqs, scale = (np.concatenate([a, a], -1).T for a in (freqs, scale))
    cos, sin = np.cos(freqs), np.sin(freqs)
    sin = sin * np.where(np.arange(DW) < DW // 2, -1, 1)[:, None]
    for name, table in (("cosq", cos * scale), ("sinq", sin * scale), ("cosk", cos / scale), ("sink", sin / scale)):
        col(name)[:] = np.concatenate([table, table], 0)
    for g in range(4):
        for j in range(4):
            for d in range(DA):
                out = g * P + DA * (4 * g + j) + d
                col("pick_num")[32 * j + d, out] = 1
                col("pick_den")[32 * j + DA, out] = 1
        col("spread")[32 * g, g * P:g * P + DW] = 1
        col("spread")[32 * g + 16, g * P + DW:g * P + P] = 1
    col("head_sum")[:] = (r[:, None] // DW) == (np.arange(32)[None, :] // 16)
    same = (r[:, None] // DA) == (r[None, :] // DA)
    col("block8")[:] = np.concatenate([same, same], 1)
    col("ones")[:] = 1
    b = np.zeros((P, CONSTB_COLS), np.float32)
    b[:, 0:P] = np.eye(P)
    b[:, P:2 * P] = -1
    x = np.arange(SPAN)[None, :]
    far = r[:, None] + WIN - x
    b[:, 2 * P:2 * P + SPAN] = np.where((far >= 0) & (far <= WIN) & (x >= WIN), 0, MASKED)
    b[:, 2 * P + SPAN:2 * P + 2 * SPAN] = np.where((far >= 0) & (far <= WIN), 0, MASKED)
    far = x - r[:, None]
    b[:, 2 * P + 2 * SPAN:] = np.where((far >= 0) & (far <= WIN), 0, MASKED)
    return c, b


class Kept:
    pass


class Phase:

    def __init__(self, nc, label):
        self.nc, self.label, self.held, self.ctx = nc, label, {}, ExitStack()

    def __call__(self, name):
        if name not in self.held:
            self.held[name] = self.ctx.enter_context(self.nc.semaphore(f"{self.label}_{name}"))
        return self.held[name]

    def close(self):
        numbers = sorted(x.num for x in self.held.values())
        start = 0
        for i in range(1, len(numbers) + 1):
            if i == len(numbers) or numbers[i] != numbers[i - 1] + 1:
                self.nc.gpsimd.sem_clear(range(numbers[start], numbers[i - 1] + 1))
                start = i
        self.nc.all_engine_barrier(sem_only=True)
        self.ctx.close()


def build(nc, a, out):
    x_d = a["L0_attn_a_x"]
    B = x_d.shape[0]
    with ExitStack() as top:
        def sb(name, shape, dt=F32, ctx=top):
            return ctx.enter_context(nc.sbuf_tensor(name, shape, dt))

        psum = top.enter_context(nc.psum_tensor("psum", [P, BANKS, T], F32))
        const = sb("const", [P, CONST_COLS])
        constb = sb("constb", [P, CONSTB_COLS], BF16)
        X = sb("X", [P, NB, T])
        Y = sb("Y", [P, NB, T])
        H = sb("H", [P, NB, T])
        eps = sb("eps", [P, 1])
        wa = sb("wa", [P, 3 * P])
        wpa = sb("wpa", [P, P])
        bqk = sb("bqk", [P, 3])
        bpa = sb("bpa", [P, 1])
        wq_b = sb("wq_b", [P, P])
        bq_b = sb("bq_b", [P, 1])
        wd_b = sb("wd_b", [P, 32])
        bd_b = sb("bd_b", [32, 1])
        wu_b = sb("wu_b", [33, 2 * P])
        wo_b = sb("wo_b", [P, P])
        bo_b = sb("bo_b", [P, 1])
        wqkv = sb("wqkv", [P, 3 * T])
        wo = sb("wo", [P, PAIRS, P])
        w1 = sb("w1", [P, 2 * HID])
        w2 = sb("w2", [P, 3, P])
        b1 = sb("b1", [P, 6])
        vecs = sb("vecs", [P, 3])
        qks = sb("qks", [P, 4])

        def cst(name, lo=0, n=None):
            s, e = CONST[name]
            return const[:, s + lo:e if n is None else s + lo + n]

        def cstb(name, lo=0, n=None):
            s, e = CONSTB[name]
            return constb[:, s + lo:e if n is None else s + lo + n]

        ident, mean_w = cst("ident"), cst("mean")

        def load_layer(sp, layer, sem):
            def row(name):
                return a[name][bass.ds(layer, 1)]
            n = 0
            for dst, src in (
                (w1[:, :], row("L0_ffn_w1").rearrange("a p n -> (a p) n")),
                (w2[:, 0:2, :], row("L0_ffn_w2")[:, 0:256, :].rearrange("a (c p) n -> p (a c) n", p=P)),
                (w2[0:HID - 256, 2, :], row("L0_ffn_w2")[:, 256:HID, :].rearrange("a p n -> (a p) n")),
                *((b1[0:w, 3 * part + i:3 * part + i + 1],
                   row("L0_ffn_b1")[:, HID * part + lo:HID * part + lo + w].rearrange("a (p c) -> (a p) c", c=1))
                  for part in range(2) for i, (lo, w) in enumerate(HID_BLOCKS)),
                (vecs[:, 0:1], row("L0_ffn_ln_g").rearrange("a (p c) -> (a p) c", c=1)),
                (vecs[:, 1:2], row("L0_ffn_ln_b").rearrange("a (p c) -> (a p) c", c=1)),
                (vecs[:, 2:3], row("L0_ffn_b2").rearrange("a (p c) -> (a p) c", c=1)),
            ):
                sp.dma_start(dst, src).then_inc(sem, 16)
                n += 16
            return n

        def load_layer_attention(sp, layer, sem):
            def row(name):
                return a[name][bass.ds(layer, 1)]
            n = 0
            pieces = [(wqkv[:, :], row("L0_ffn_wqkv").rearrange("a p n -> (a p) n")),
                      (wo[:, :, :], row("L0_ffn_wo").rearrange("a (c p) n -> p (a c) n", p=P))]
            for at, name in ((0, "L0_ffn_q_scale"), (1, "L0_ffn_k_scale")):
                v = row(name).rearrange("a (p c) -> (a p) c", c=1)
                for h in range(2):
                    pieces.append((qks[DW * h:DW * h + DW, at:at + 1], v))
                    for s in range(2):
                        dst = DW * h + 32 * s
                        pieces.append((qks[dst:dst + 32, at + 2:at + 3], v[32 * (1 - s):32 * (1 - s) + 32, :]))
            for dst, src in pieces:
                sp.dma_start(dst, src).then_inc(sem, 16)
                n += 16
            return n

        parts_d = nc.dram_tensor("parts", [NB, 2, 3, P, T], BF16).ap()
        minus_ones = nc.dram_tensor("minus_ones", [1, HA, T], BF16).ap()
        s = Phase(nc, "load")
        casting = ExitStack()
        constb_f = casting.enter_context(nc.sbuf_tensor("constb_f", [P, CONSTB_COLS], F32))
        minus = casting.enter_context(nc.sbuf_tensor("minus", [HA, T], BF16))
        block = nc.Block()
        with block:
            @block.vector
            def _(dve):
                nc.vector.memset(minus[:, :], -1.0).then_inc(s("minus"), 1)
                dve.wait_ge(s("tables"), 16)
                nc.vector.tensor_copy(constb[:, :], constb_f[:, :]).then_inc(s("tables_cast"), 1)

            @block.sync
            def _(sp):
                n = 0
                sp.dma_start(constb_f[:, :], a["constb"]).then_inc(s("tables"), 16)
                sp.wait_ge(s("minus"), 1)
                sp.dma_start(minus_ones[0], minus[:, :]).then_inc(s("loaded"), 16)
                n += 16
                wu = a["L0_attn_b_Wu"].rearrange("r (h c d) -> c r h d", c=2, d=DA)
                bu = a["L0_attn_b_bu"].rearrange("(o h c d) -> c o h d", o=1, c=2, d=DA)

                def column(v):
                    return v.rearrange("(p c) -> p c", c=1)
                for dst, src in (
                    (const[:, :], a["const"]),
                    (wa[:, :], a["L0_attn_a_w_qkv"]), (wpa[:, :], a["L0_attn_a_w_proj"]),
                    *((bqk[:, i:i + 1], column(a["L0_attn_a_b_qkv"][P * i:P * i + P])) for i in range(3)),
                    (bpa[:, :], column(a["L0_attn_a_b_proj"])),
                    (wq_b[:, :], a["L0_attn_b_Wq"]), (bq_b[:, :], column(a["L0_attn_b_bq"])),
                    (wd_b[:, :], a["L0_attn_b_Wd"]), (bd_b[:, :], column(a["L0_attn_b_bd"])),
                    (wu_b[0:32, 0:P].rearrange("r (h d) -> r h d", d=DA), wu[0]),
                    (wu_b[0:32, P:2 * P].rearrange("r (h d) -> r h d", d=DA), wu[1]),
                    (wu_b[32:33, 0:P].rearrange("r (h d) -> r h d", d=DA), bu[0]),
                    (wu_b[32:33, P:2 * P].rearrange("r (h d) -> r h d", d=DA), bu[1]),
                    (wo_b[:, :], a["L0_attn_b_Wo"]), (bo_b[:, :], column(a["L0_attn_b_bo"])),
                ):
                    sp.dma_start(dst, src).then_inc(s("loaded"), 16)
                    n += 16
                n += load_layer(sp, 0, s("loaded"))
                n += load_layer_attention(sp, 0, s("loaded"))
                sp.wait_ge(s("loaded"), n)

            @block.gpsimd
            def _(pool):
                nc.gpsimd.memset(eps[:, :], LN_EPS).then_inc(s("eps"), 1)
                pool.wait_ge(s("eps"), 1)
        s.close()
        casting.close()

        g = Kept()
        g.psum, g.X, g.Y, g.H, g.eps, g.cst = psum, X, Y, H, eps, cst
        g.cstb, g.ident, g.mean_w, g.x_d, g.wa, g.wpa = cstb, ident, mean_w, x_d, wa, wpa
        g.bqk, g.bpa, g.wq_b, g.bq_b, g.wd_b, g.bd_b = bqk, bpa, wq_b, bq_b, wd_b, bd_b
        g.wu_b, g.wo_b, g.bo_b, g.wqkv, g.wo, g.w1 = wu_b, wo_b, bo_b, wqkv, wo, w1
        g.w2, g.b1, g.vecs, g.qks, g.load_layer, g.load_layer_attention = w2, b1, vecs, qks, load_layer, load_layer_attention
        g.parts_d, g.minus_ones = parts_d, minus_ones
        with nc.Fori(0, B // NB) as pair:
            attention_a(nc, a, g, pair)
            with nc.Fori(0, 2) as layer:
                feed_forward(nc, g, layer, 0)
            attention_b(nc, g)
            with nc.Fori(0, 2) as layer:
                feed_forward(nc, g, layer, 1)
            store(nc, g, out, pair)


def shift_dve(nc, s, g, n):
    nc.vector.tensor_copy(g.H[0:64, n, :], g.Y[0:64, n, :])
    nc.vector.tensor_copy(g.H[64:P, n, 1:T], g.Y[64:P, n, 0:T - 1])
    nc.vector.memset(g.H[64:P, n, 0:1], 0.0).then_inc(s("shifted"), 1)


def attention_a(nc, a, g, pair):
    psum, X, Y, eps, cst, ident, mean_w = g.psum, g.X, g.Y, g.eps, g.cst, g.ident, g.mean_w
    wa, wpa, bqk, bpa, x_d, parts_d = g.wa, g.wpa, g.bqk, g.bpa, g.x_d, g.parts_d
    with ExitStack() as ctx:
        def sb(name, shape, dt=F32):
            return ctx.enter_context(nc.sbuf_tensor(name, shape, dt))

        QS = sb("QS", [P, NB, HA, T], BF16)
        KS = sb("KS", [P, NB, HA, T], BF16)
        VA = sb("VA", [P, NB, 4, HA, 16])
        OC = sb("OC", [P, NB, 4, T])

        with ExitStack() as prep:
            def sp_(name, shape, dt=F32):
                return prep.enter_context(nc.sbuf_tensor(name, shape, dt))
            XT = sp_("XT", [P, NB, 4, P])
            XC = sp_("XC", [P, NB, T])
            SQ = sp_("SQ", [P, NB, T])
            SD = sp_("SD", [P, NB, T])
            RS = sp_("RS", [P, NB, T])
            QF = sp_("QF", [P, NB, 2, T])
            PRT = sp_("PRT", [P, NB, 2, 3, T], BF16)
            R1 = sp_("R1", [P, NB, 2, T])
            s = Phase(nc, "a1")
            block = nc.Block()
            with block:
                @block.sync
                def _(sp):
                    for n in range(NB):
                        src = x_d[bass.ds(pair * NB + n, 1)].rearrange("a (t p) d -> p (a t) d", p=P)
                        sp.dma_start(XT[:, n, :, :], src).then_inc(s(f"x_loaded{n}"), 16)
                    for n in range(NB):
                        for w in range(2):
                            sp.wait_ge(s("split"), 2 * n + w + 1)
                            sp.dma_start(parts_d[n, w].rearrange("c (p) t -> p c t", p=P),
                                         PRT[:, n, w, :, :]).then_inc(s(f"parts_out{n}{w}"), 16)
                    sp.wait_ge(s("stacks_zero"), NB * 3)
                    for n in range(NB):
                        for w, dst in ((0, QS), (1, KS)):
                            sp.wait_ge(s(f"parts_out{n}{w}"), 16)
                            for i in range(3):
                                for j in range(3):
                                    part, slot = (i, 3 * i + j) if w == 0 else (j, 3 * i + j)
                                    src = parts_d[n, w, part].rearrange("(h d) t -> d h t", d=DA)
                                    sp.dma_start(dst[DA * slot:DA * slot + DA, n, :, :], src)\
                                      .then_inc(s("stacked"), 16)
                    for n in range(NB):
                        sp.dma_start(KS[GUARD_ROW:GUARD_ROW + 1, n, :, :],
                                     g.minus_ones).then_inc(s("stacked"), 16)
                    sp.wait_ge(s("stacked"), 16 * (NB * 2 * SLOTS + NB))

                @block.gpsimd
                def _(pool):
                    for n in range(NB):
                        for i, part in enumerate((QS[64:P, n, :, :], KS[64:P, n, :, :], VA[:, n, :, :, :])):
                            nc.gpsimd.memset(part, 0.0).then_inc(s("stacks_zero"), 1)
                            pool.wait_ge(s("stacks_zero"), 3 * n + i + 1)
                    for n in range(NB):
                        nc.gpsimd.memset(VA[:, n, :, :, DA:DA + 1], 1.0).then_inc(s("v_ones"), 1)
                    pool.wait_ge(s("v_ones"), NB)

                @block.tensor
                def _(pe):
                    for n in range(NB):
                        pe.wait_ge(s(f"x_loaded{n}"), 16)
                        for t in range(4):
                            last = nc.tensor.transpose(psum[:, 4 * n, P * t:P * t + P], XT[:, n, t, :], ident)
                        last.then_inc(s("x_turned"), 1)
                    for n in range(NB):
                        pe.wait_ge(s("x_copied"), n + 1)
                        nc.tensor.matmul(psum[:, 4 * n + 1, :], mean_w, X[:, n, :], start=True, stop=True)\
                          .then_inc(s("ln_mean"), 1)
                    for n in range(NB):
                        pe.wait_ge(s("ln_squared"), n + 1)
                        nc.tensor.matmul(psum[:, 4 * n + 2, :], mean_w, SQ[:, n, :], start=True, stop=True)\
                          .then_inc(s("ln_var"), 1)
                    for n in range(NB):
                        pe.wait_ge(s("ln_done"), n + 1)
                        for w in range(2):
                            nc.tensor.matmul(psum[:, 4 * n + w, :], wa[:, P * w:P * w + P], XC[:, n, :],
                                             start=True, stop=True).then_inc(s("qk"), 1)
                        for t in range(4):
                            last = nc.tensor.matmul(psum[:, 4 * n + 3, P * t:P * t + P], XC[:, n, P * t:P * t + P],
                                                    wa[:, 2 * P:3 * P], start=True, stop=True)
                        last.then_inc(s("v"), 1)

                @block.scalar
                def _(act):
                    for n in range(NB):
                        act.wait_ge(s("x_turned"), n + 1)
                        nc.scalar.activation(X[:, n, :], psum[:, 4 * n, :], ACT.Copy).then_inc(s("x_copied"), 1)
                    for n in range(NB):
                        act.wait_ge(s("ln_centered"), n + 1)
                        nc.scalar.activation(SQ[:, n, :], XC[:, n, :], ACT.Square).then_inc(s("ln_squared"), 1)
                    for n in range(NB):
                        act.wait_ge(s("ln_var"), n + 1)
                        nc.scalar.activation(SD[:, n, :], psum[:, 4 * n + 2, :], ACT.Sqrt, bias=eps[:, 0:1])\
                          .then_inc(s("ln_sd"), 1)
                    for n in range(NB):
                        for w in range(2):
                            act.wait_ge(s("qk"), 2 * n + w + 1)
                            nc.scalar.activation(QF[:, n, w, :], psum[:, 4 * n + w, :], ACT.Identity,
                                                 bias=bqk[:, w:w + 1]).then_inc(s("qk_biased"), 1)
                        act.wait_ge(s("v"), n + 1)
                        act.wait_ge(s("v_ones"), NB)
                        nc.scalar.activation(VA[:, n, :, :, 0:DA],
                                             psum[:, 4 * n + 3, :].rearrange("p (t h d) -> p t h d", t=4, d=DA),
                                             ACT.Copy).then_inc(s("v_copied"), 1)

                @block.vector
                def _(dve):
                    for n in range(NB):
                        dve.wait_ge(s("ln_mean"), n + 1)
                        nc.vector.tensor_tensor(XC[:, n, :], X[:, n, :], psum[:, 4 * n + 1, :], ALU.subtract)\
                          .then_inc(s("ln_centered"), 1)
                    for n in range(NB):
                        dve.wait_ge(s("ln_sd"), n + 1)
                        nc.vector.reciprocal(RS[:, n, :], SD[:, n, :]).then_inc(s("ln_recip"), 1)
                        dve.wait_ge(s("ln_recip"), n + 1)
                        nc.vector.tensor_tensor(XC[:, n, :], XC[:, n, :], RS[:, n, :], ALU.mult)\
                          .then_inc(s("ln_done"), 1)
                    for n in range(NB):
                        for w in range(2):
                            i = 2 * n + w
                            dve.wait_ge(s("qk_biased"), i + 1)
                            nc.vector.tensor_copy(PRT[:, n, w, 0, :], QF[:, n, w, :]).then_inc(s("hi"), 1)
                            dve.wait_ge(s("hi"), i + 1)
                            nc.vector.tensor_tensor(R1[:, n, w, :], QF[:, n, w, :], PRT[:, n, w, 0, :],
                                                    ALU.subtract).then_inc(s("rest"), 1)
                            dve.wait_ge(s("rest"), i + 1)
                            nc.vector.tensor_copy(PRT[:, n, w, 1, :], R1[:, n, w, :]).then_inc(s("mid"), 1)
                            dve.wait_ge(s("mid"), i + 1)
                            nc.vector.tensor_tensor(PRT[:, n, w, 2, :], R1[:, n, w, :], PRT[:, n, w, 1, :],
                                                    ALU.subtract).then_inc(s("split"), 1)
            s.close()

        with ExitStack() as main:
            def sm(name, shape, dt=F32):
                return main.enter_context(nc.sbuf_tensor(name, shape, dt))
            PT = sm("PT", [P, 8, 4, T])
            M = sm("M", [P, 4, 2, 4])
            MROW = sm("MROW", [2, 4, T], BF16)
            s = Phase(nc, "a2")
            UNITS = NB * HA // 2
            SLOT = [(2, 3), (4, 5)]
            O_BANK, TURN_BANK = 6, 7

            def where(unit):
                return unit // (HA // 2), 2 * (unit % (HA // 2))

            block = nc.Block()
            with block:
                @block.tensor
                def _(pe):
                    def scores(unit, j):
                        n, h = where(unit)
                        for qt in range(4):
                            i = (2 * unit + j) * 4 + qt
                            if i >= 2:
                                pe.wait_ge(s("maxed"), i - 1)
                            nc.tensor.matmul(psum[:, i % 2, :], QS[0:GUARD_ROW, n, h + j, P * qt:P * qt + P],
                                             KS[0:GUARD_ROW, n, h + j, :], start=True, stop=True)\
                              .then_inc(s("scored"), 1)

                    def turn_maxima(unit):
                        pe.wait_ge(s("maxed"), 8 * (unit + 1))
                        if unit:
                            pe.wait_ge(s("row_made"), unit)
                        for qt in range(4):
                            last = nc.tensor.transpose(psum[0:2, TURN_BANK, P * qt:P * qt + P],
                                                       M[:, unit % 4, :, qt], ident)
                        last.then_inc(s("turned"), 1)

                    def scores_by_key(unit, j):
                        n, h = where(unit)
                        if j == 0:
                            pe.wait_ge(s(f"row_in{unit % 4}"), 32 * (unit // 4 + 1))
                        for kt in range(4):
                            i = (2 * unit + j) * 2 + kt // 2
                            if i >= 2 and kt % 2 == 0:
                                pe.wait_ge(s("exped"), i - 1)
                            last = nc.tensor.matmul(psum[:, SLOT[i % 2][kt % 2], :],
                                                    KS[:, n, h + j, P * kt:P * kt + P],
                                                    QS[:, n, h + j, :], start=True, stop=True)
                            if kt % 2:
                                last.then_inc(s("scored_by_key"), 1)

                    def weighted_sums(group):
                        n, quad = group // 4, group % 4
                        pe.wait_ge(s("exped"), 8 * (group + 1))
                        if group:
                            pe.wait_ge(s("o_copied"), group)
                        else:
                            pe.wait_ge(s("o_zeroed"), 1)
                        for kt in range(4):
                            for j in range(4):
                                h = 4 * quad + j
                                last = nc.tensor.matmul(psum[32 * j:32 * j + 16, O_BANK, :], VA[:, n, kt, h, :],
                                                        PT[:, (4 * group + j) % 8, kt, :],
                                                        start=(kt == 0), stop=(kt == 3))
                        last.then_inc(s("summed"), 1)

                    for u in range(LAG):
                        for j in range(2):
                            scores(u, j)
                    turn_maxima(0)
                    for u in range(UNITS):
                        ahead = u + LAG < UNITS
                        if ahead:
                            scores(u + LAG, 0)
                        scores_by_key(u, 0)
                        if u + 1 < UNITS:
                            turn_maxima(u + 1)
                        if ahead:
                            scores(u + LAG, 1)
                        scores_by_key(u, 1)
                        if u % 2 == 0 and u:
                            weighted_sums(u // 2 - 1)
                    weighted_sums(UNITS // 2 - 1)

                @block.vector
                def _(dve):
                    def make_row(unit):
                        dve.wait_ge(s("turned"), unit + 1)
                        if unit >= 4:
                            dve.wait_ge(s(f"row_in{unit % 4}"), 32 * (unit // 4))
                        nc.vector.tensor_copy(MROW[:, unit % 4, :], psum[0:2, TURN_BANK, :])\
                          .then_inc(s("row_made"), 1)

                    nc.vector.memset(psum[:, O_BANK, :], 0.0).then_inc(s("o_zeroed"), 1)
                    for u in range(UNITS):
                        for j in range(2):
                            for qt in range(4):
                                i = (2 * u + j) * 4 + qt
                                dve.wait_ge(s("scored"), i + 1)
                                if u >= 4 and j == 0 and qt == 0:
                                    dve.wait_ge(s("turned"), u - 3)
                                nc.vector.tensor_reduce(M[:, u % 4, j, qt:qt + 1], psum[:, i % 2, :], AX_X,
                                                        ALU.max).then_inc(s("maxed"), 1)
                            if j == 0 and u >= LAG:
                                make_row(u - 1)
                        if u == LAG - 1:
                            make_row(0)
                    make_row(UNITS - 1)

                @block.sync
                def _(sp):
                    for u in range(UNITS):
                        n, h = where(u)
                        sp.wait_ge(s("row_made"), u + 1)
                        for j in range(2):
                            sp.dma_start(QS[GUARD_ROW:GUARD_ROW + 1, n, h + j, :], MROW[j:j + 1, u % 4, :])\
                              .then_inc(s(f"row_in{u % 4}"), 16)

                @block.scalar
                def _(act):
                    def copy_sums(group):
                        act.wait_ge(s("summed"), group + 1)
                        nc.scalar.activation(OC[:, group // 4, group % 4, :], psum[:, O_BANK, :], ACT.Copy)\
                          .then_inc(s("o_copied"), 1)

                    for u in range(UNITS):
                        for j in range(2):
                            head = 2 * u + j
                            if head >= 8 and head % 4 == 0:
                                act.wait_ge(s("summed"), head // 4 - 1)
                            for half in range(2):
                                i = head * 2 + half
                                act.wait_ge(s("scored_by_key"), i + 1)
                                nc.scalar.activation(PT[:, head % 8, 2 * half:2 * half + 2, :],
                                                     psum[:, SLOT[i % 2][0]:SLOT[i % 2][1] + 1, :], ACT.Exp,
                                                     scale=float(DA) ** -0.5).then_inc(s("exped"), 1)
                        if u % 2 and u > 2:
                            copy_sums(u // 2 - 1)
                    copy_sums(UNITS // 2 - 1)
            s.close()

        with ExitStack() as tail:
            def st(name, shape, dt=F32):
                return tail.enter_context(nc.sbuf_tensor(name, shape, dt))
            RD = st("RD", [P, NB, T])
            ON = st("ON", [P, NB, T])
            bufs = ln_buffers(st)
            s = Phase(nc, "a3")
            block = nc.Block()
            with block:
                @block.tensor
                def _(pe):
                    for n in range(NB):
                        for quad in range(4):
                            nc.tensor.matmul(psum[:, 4 * n, :], cst("pick_den", P * quad, P), OC[:, n, quad, :],
                                             start=(quad == 0), stop=(quad == 3))\
                              .then_inc(s("den"), 1)
                        for quad in range(4):
                            nc.tensor.matmul(psum[:, 4 * n + 1, :], cst("pick_num", P * quad, P), OC[:, n, quad, :],
                                             start=(quad == 0), stop=(quad == 3))\
                              .then_inc(s("num"), 1)
                    for n in range(NB):
                        pe.wait_ge(s("o_ready"), n + 1)
                        nc.tensor.matmul(psum[:, 4 * n + 2, :], wpa[:, :], ON[:, n, :], start=True, stop=True)\
                          .then_inc(s("projected"), 1)
                    norm_pe(nc, pe, s, g, bufs)

                @block.scalar
                def _(act):
                    norm_act(nc, act, s, g, bufs)

                @block.vector
                def _(dve):
                    for n in range(NB):
                        dve.wait_ge(s("den"), 4 * n + 4)
                        nc.vector.reciprocal(RD[:, n, :], psum[:, 4 * n, :]).then_inc(s("rden"), 1)
                        dve.wait_ge(s("num"), 4 * n + 4)
                        dve.wait_ge(s("rden"), n + 1)
                        nc.vector.tensor_tensor(ON[:, n, :], psum[:, 4 * n + 1, :], RD[:, n, :], ALU.mult)\
                          .then_inc(s("o_div"), 1)
                        dve.wait_ge(s("o_div"), n + 1)
                        nc.vector.tensor_scalar(ON[:, n, :], ON[:, n, :], bqk[:, 2:3], None, ALU.add)\
                          .then_inc(s("o_ready"), 1)
                    for n in range(NB):
                        dve.wait_ge(s("projected"), n + 1)
                        nc.vector.scalar_tensor_tensor(out=X[:, n, :], in0=psum[:, 4 * n + 2, :],
                                                       scalar=bpa[:, 0:1], in1=X[:, n, :],
                                                       op0=ALU.add, op1=ALU.add).then_inc(s("x_new"), 1)
                    norm_dve(nc, dve, s, g, bufs)
                    for n in range(NB):
                        dve.wait_ge(s("y_new"), n + 1)
                        shift_dve(nc, s, g, n)
            s.close()


def ln_buffers(alloc):
    return {k: alloc("ln_" + k, [P, NB, T]) for k in ("centered", "squared", "sd", "recip")}


def norm_pe(nc, pe, s, g, b):
    psum, X, mean_w = g.psum, g.X, g.mean_w
    for n in range(NB):
        pe.wait_ge(s("x_new"), n + 1)
        nc.tensor.matmul(psum[:, 4 * n, :], mean_w, X[:, n, :], start=True, stop=True).then_inc(s("ln_mean"), 1)
    for n in range(NB):
        pe.wait_ge(s("ln_squared"), n + 1)
        nc.tensor.matmul(psum[:, 4 * n + 3, :], mean_w, b["squared"][:, n, :], start=True, stop=True)\
          .then_inc(s("ln_var"), 1)


def norm_act(nc, act, s, g, b):
    psum, eps = g.psum, g.eps
    for n in range(NB):
        act.wait_ge(s("ln_centered"), n + 1)
        nc.scalar.activation(b["squared"][:, n, :], b["centered"][:, n, :], ACT.Square).then_inc(s("ln_squared"), 1)
    for n in range(NB):
        act.wait_ge(s("ln_var"), n + 1)
        nc.scalar.activation(b["sd"][:, n, :], psum[:, 4 * n + 3, :], ACT.Sqrt, bias=eps[:, 0:1])\
          .then_inc(s("ln_sd"), 1)


def norm_dve(nc, dve, s, g, b):
    psum, X, Y = g.psum, g.X, g.Y
    for n in range(NB):
        dve.wait_ge(s("ln_mean"), n + 1)
        nc.vector.tensor_tensor(b["centered"][:, n, :], X[:, n, :], psum[:, 4 * n, :], ALU.subtract)\
          .then_inc(s("ln_centered"), 1)
    for n in range(NB):
        dve.wait_ge(s("ln_sd"), n + 1)
        nc.vector.reciprocal(b["recip"][:, n, :], b["sd"][:, n, :]).then_inc(s("ln_recip"), 1)
        dve.wait_ge(s("ln_recip"), n + 1)
        nc.vector.tensor_tensor(Y[:, n, :], b["centered"][:, n, :], b["recip"][:, n, :], ALU.mult)\
          .then_inc(s("y_new"), 1)




def feed_forward(nc, g, layer, call):
    psum, Y, H, eps, cst, cstb = g.psum, g.Y, g.H, g.eps, g.cst, g.cstb
    wqkv, wo, w1, w2, b1, vecs, qks = g.wqkv, g.wo, g.w1, g.w2, g.b1, g.vecs, g.qks
    STEPS = NB * PAIRS
    BLOCKS = 2 * PAIRS

    order = []
    for n in range(NB):
        for blk in range(BLOCKS):
            order += [("main", n, blk), ("rot", n, blk)]
        order += [("ssq", n, 0), ("ssq", n, 1)]
    for n in range(NB):
        order += [("v", n, t) for t in range(4)]
        order += [("spread", n, blk) for blk in range(BLOCKS)]
    order += [("s", 0, j, half) for j in range(2) for half in range(2)]
    for i in range(STEPS):
        if i + 1 < STEPS:
            order += [("s", i + 1, j, half) for j in range(2) for half in range(2)]
        order += [("st", i, j, half) for j in range(2) for half in range(2)]
        if i:
            order += [("o", i - 1), ("den", i - 1)]
    order += [("o", STEPS - 1), ("den", STEPS - 1)]
    for kind in ("wo", "mean", "var"):
        order += [(kind, n) for n in range(NB)]
    for n in range(NB):
        for blk in range(3):
            order += [("gate", n, blk), ("up", n, blk)]
    order += [("w2", n) for n in range(NB)]
    at = {use: i for i, use in enumerate(order)}

    def bank(*use):
        return at[use] % BANKS

    def last_read(use):
        kind, *i = use
        if kind in ("main", "rot"):
            return "rotated", BLOCKS * i[0] + i[1] + 1
        if kind == "ssq":
            return "sd", 2 * i[0] + i[1] + 1
        if kind == "v":
            return "v_copied", 4 * i[0] + i[1] + 1
        if kind == "spread":
            return "qk_ready", BLOCKS * i[0] + i[1] + 1
        if kind in ("s", "st"):
            return "maxed" if kind == "s" else "exped", 4 * i[0] + 2 * i[1] + i[2] + 1
        if kind in ("o", "den"):
            return "o_ready", i[0] + 1
        if kind in ("gate", "up"):
            return "hidden", 3 * i[0] + i[1] + 1
        return {"wo": "y_mid", "mean": "ln_centered", "var": "ln_sd", "w2": "y_new"}[kind], i[0] + 1

    with ExitStack() as ctx:
        def sb(name, shape, dt=F32):
            return ctx.enter_context(nc.sbuf_tensor(f"f{call}_{name}", shape, dt))

        TAB = sb("TAB", [P, 4, T])
        WR = sb("WR", [P, 2 * T])
        QZ = sb("QZ", [P, NB, HW, T])
        QB = sb("QB", [P, NB, HW, T], BF16)
        K = sb("K", [P, NB, PAIRS, T])
        KB = sb("KB", [P, NB, PAIRS, WIN + T], BF16)
        V = sb("V", [P, NB, 4, T])
        O = sb("O", [P, NB, PAIRS, T])
        SQ = sb("SQ", [P, BLOCKS, T])
        R = sb("R", [P, NB, 2, T])
        MIX = sb("MIX", [P, 2, 2, T])
        PT = sb("PT", [P, 4, 4 * SPAN])
        M = sb("M", [P, 4, 4])
        D = SQ[:, 6:8, :].bitcast(BF16).rearrange("p a (h t c) -> p (a h) t c", h=2, t=4)
        RD = MIX[:, 0, :, :]
        F1 = V[:, :, :, :].rearrange("p n t c -> p (n t) c")

        def hidden(n, part, blk):
            return (SQ if n == 0 else F1)[:, 3 * part + blk, :]

        s = Phase(nc, f"f{call}")
        block = nc.Block()
        with block:
            @block.sync
            def _(sp):
                sp.wait_ge(s("v"), 4 * NB)
                sp.wait_ge(s("wo"), NB)
                loads = g.load_layer_attention(sp, 1 - layer, s("next_layer"))
                sp.wait_ge(s("w2"), NB)
                sp.wait_ge(s("y_new"), NB)
                loads += g.load_layer(sp, 1 - layer, s("next_layer"))
                sp.wait_ge(s("next_layer"), loads)

            @block.gpsimd
            def _(pool):
                for n in range(NB):
                    for j in range(2):
                        other = slice(DW * (1 - j), DW * (1 - j) + DW)
                        nc.gpsimd.memset(QZ[other, n, j:HW:2, :], 0.0).then_inc(s("zeroed"), 1)
                        pool.wait_ge(s("zeroed"), 3 * n + j + 1)
                    nc.gpsimd.memset(KB[:, n, :, 0:WIN], 0.0).then_inc(s("zeroed"), 1)
                    pool.wait_ge(s("zeroed"), 3 * n + 3)
                for n in range(NB):
                    for blk in range(BLOCKS):
                        i = BLOCKS * n + blk
                        pool.wait_ge(s("rotated"), i + 1)
                        dst = O[:, n, blk, :] if blk < PAIRS else K[:, n, blk - PAIRS, :]
                        nc.gpsimd.tensor_tensor(dst, MIX[:, i % 2, 0, :], MIX[:, i % 2, 1, :], ALU.add)\
                          .then_inc(s("summed"), 1)
                for i in range(STEPS):
                    for j in range(2):
                        head = 2 * i + j
                        pool.wait_ge(s("maxed"), 2 * head + 2)
                        if head >= 4:
                            pool.wait_ge(s("st"), 2 * (head - 4) + 2)
                        nc.gpsimd.tensor_tensor(
                            D[:, head % 4, :, :],
                            cstb("ident")[:, None, :].to_broadcast([P, 4, P]),
                            M[:, head % 4, :, None].to_broadcast([P, 4, P]), ALU.mult).then_inc(s("diag"), 1)

            @block.tensor
            def _(pe):
                def take(*use):
                    i = at[use]
                    if i >= BANKS:
                        name, value = last_read(order[i - BANKS])
                        pe.wait_ge(s(name), value)
                    return psum[:, i % BANKS, :]

                pe.wait_ge(s("swapped"), 1)
                for n in range(NB):
                    for blk in range(BLOCKS):
                        nc.tensor.matmul(take("main", n, blk), wqkv[:, P * blk:P * blk + P], H[:, n, :],
                                         start=True, stop=True).then_inc(s("main"), 1)
                        nc.tensor.matmul(take("rot", n, blk), WR[:, P * blk:P * blk + P], H[:, n, :],
                                         start=True, stop=True).then_inc(s("rot"), 1)
                    for w in range(2):
                        dst = take("ssq", n, w)
                        pe.wait_ge(s("squared"), BLOCKS * n + PAIRS * (w + 1))
                        for c in range(PAIRS):
                            last = nc.tensor.matmul(dst[32 * c:32 * c + 32, :], cst("head_sum"),
                                                    SQ[:, PAIRS * w + c, :], start=True, stop=True)
                        last.then_inc(s("ssq"), 1)
                for n in range(NB):
                    for t in range(4):
                        nc.tensor.matmul(take("v", n, t), H[:, n, P * t:P * t + P], wqkv[:, 2 * T:3 * T],
                                         start=True, stop=True).then_inc(s("v"), 1)
                    for blk in range(BLOCKS):
                        w, c = blk // PAIRS, blk % PAIRS
                        pe.wait_ge(s("norm_recip"), 2 * n + w + 1)
                        nc.tensor.matmul(take("spread", n, blk), cst("spread", P * c, P), R[:, n, w, :],
                                         start=True, stop=True).then_inc(s("spread"), 1)

                def scores(i):
                    n, c = i // PAIRS, i % PAIRS
                    pe.wait_ge(s("cast"), BLOCKS * n + PAIRS + c + 1)
                    for j in range(2):
                        for half in range(2):
                            dst = take("s", i, j, half)
                            for k in range(2):
                                tile = 2 * half + k
                                part = dst[:, SPAN * k:SPAN * k + SPAN]
                                nc.tensor.matmul(part, QB[:, n, 2 * c + j, P * tile:P * tile + P],
                                                 KB[:, n, c, P * tile:P * tile + SPAN], start=True, stop=False)
                                last = nc.tensor.matmul(part, cstb("ident"), cstb("mask_q" if tile else "mask_first"),
                                                        start=False, stop=True)
                            last.then_inc(s("s"), 1)

                def scores_by_key(i):
                    n, c = i // PAIRS, i % PAIRS
                    for j in range(2):
                        head = 2 * i + j
                        pe.wait_ge(s("diag"), head + 1)
                        for half in range(2):
                            dst = take("st", i, j, half)
                            for k in range(2):
                                tile = 2 * half + k
                                width = min(SPAN, T - P * tile)
                                part = dst[:, SPAN * k:SPAN * k + width]
                                nc.tensor.matmul(part, K[:, n, c, P * tile:P * tile + P],
                                                 QZ[:, n, 2 * c + j, P * tile:P * tile + width],
                                                 start=True, stop=False)
                                nc.tensor.matmul(part, cstb("ident"), cstb("mask_k", 0, width),
                                                 start=False, stop=False)
                                diag = D[:, head % 4, :, :].rearrange("p a b -> p (a b)")
                                last = nc.tensor.matmul(part, cstb("minus1"), diag[:, P * tile:P * tile + width],
                                                        start=False, stop=True)
                            last.then_inc(s("st"), 1)

                def weighted_sums(i):
                    n, c = i // PAIRS, i % PAIRS
                    pe.wait_ge(s("exped"), 4 * i + 4)
                    for kind in ("o", "den"):
                        dst = take(kind, i)
                        for tile in range(4):
                            width = min(SPAN, T - P * tile)
                            for j in range(2):
                                weights = (V[:, n, tile, DW * (2 * c + j):DW * (2 * c + j) + DW] if kind == "o"
                                           else cst("ones"))
                                last = nc.tensor.matmul(
                                    dst[DW * j:DW * j + DW, P * tile:P * tile + width], weights,
                                    PT[:, (2 * i + j) % 4, SPAN * tile:SPAN * tile + width],
                                    start=(tile == 0), stop=(tile == 3), skip_group_check=True)
                        last.then_inc(s(kind), 1)

                scores(0)
                for i in range(STEPS):
                    if i + 1 < STEPS:
                        scores(i + 1)
                    scores_by_key(i)
                    if i:
                        weighted_sums(i - 1)
                weighted_sums(STEPS - 1)

                for n in range(NB):
                    pe.wait_ge(s("o_ready"), PAIRS * (n + 1))
                    dst = take("wo", n)
                    for c in range(PAIRS):
                        last = nc.tensor.matmul(dst, wo[:, c, :], O[:, n, c, :], start=(c == 0),
                                                stop=(c == PAIRS - 1))
                    last.then_inc(s("wo"), 1)
                for n in range(NB):
                    pe.wait_ge(s("shifted"), n + 1)
                    nc.tensor.matmul(take("mean", n), g.mean_w, H[:, n, :], start=True, stop=True)\
                      .then_inc(s("mean"), 1)
                for n in range(NB):
                    pe.wait_ge(s("ln_squared"), n + 1)
                    nc.tensor.matmul(take("var", n), g.mean_w, F1[:, 3 + n, :], start=True, stop=True)\
                      .then_inc(s("var"), 1)
                for n in range(NB):
                    pe.wait_ge(s("ln_done"), n + 1)
                    for blk, (lo, w) in enumerate(HID_BLOCKS):
                        for kind, first in (("gate", HID), ("up", 0)):
                            nc.tensor.matmul(take(kind, n, blk)[0:w, :], w1[:, first + lo:first + lo + w],
                                             H[:, n, :], start=True, stop=True).then_inc(s(kind), 1)
                for n in range(NB):
                    dst = take("w2", n)
                    for blk, (lo, w) in enumerate(HID_BLOCKS):
                        pe.wait_ge(s("hidden"), 3 * n + blk + 1)
                        last = nc.tensor.matmul(dst, w2[0:w, blk, :], hidden(n, 1, blk)[0:w, :],
                                                start=(blk == 0), stop=(blk == 2))
                    last.then_inc(s("w2"), 1)

            @block.scalar
            def _(act):
                for n in range(NB):
                    if n:
                        act.wait_ge(s("ssq"), 2 * n)
                    for blk in range(BLOCKS):
                        act.wait_ge(s("main"), BLOCKS * n + blk + 1)
                        nc.scalar.activation(SQ[:, blk, :], psum[:, bank("main", n, blk), :], ACT.Square)\
                          .then_inc(s("squared"), 1)
                    for w in range(2):
                        act.wait_ge(s("ssq"), 2 * n + w + 1)
                        nc.scalar.activation(R[:, n, w, :], psum[:, bank("ssq", n, w), :], ACT.Sqrt)\
                          .then_inc(s("sd"), 1)
                for n in range(NB):
                    for t in range(4):
                        act.wait_ge(s("v"), 4 * n + t + 1)
                        nc.scalar.activation(V[:, n, t, :], psum[:, bank("v", n, t), :], ACT.Copy)\
                          .then_inc(s("v_copied"), 1)
                for i in range(STEPS):
                    for j in range(2):
                        if i >= 2:
                            act.wait_ge(s("den"), i - 1)
                        for half in range(2):
                            act.wait_ge(s("st"), 4 * i + 2 * j + half + 1)
                            width = SPAN + min(SPAN, T - P * (2 * half + 1))
                            nc.scalar.activation(
                                PT[:, (2 * i + j) % 4, 2 * SPAN * half:2 * SPAN * half + width],
                                psum[:, bank("st", i, j, half), 0:width], ACT.Exp, scale=8.0)\
                              .then_inc(s("exped"), 1)
                for n in range(NB):
                    act.wait_ge(s("ln_centered"), n + 1)
                    nc.scalar.activation(F1[:, 3 + n, :], F1[:, n, :], ACT.Square).then_inc(s("ln_squared"), 1)
                for n in range(NB):
                    act.wait_ge(s("var"), n + 1)
                    nc.scalar.activation(RD[:, n, :], psum[:, bank("var", n), :], ACT.Sqrt,
                                         bias=eps[:, 0:1]).then_inc(s("ln_sd"), 1)
                for n in range(NB):
                    for blk, (_, w) in enumerate(HID_BLOCKS):
                        act.wait_ge(s("gate"), 3 * n + blk + 1)
                        nc.scalar.activation(hidden(n, 0, blk)[0:w, :], psum[0:w, bank("gate", n, blk), :],
                                             ACT.Gelu, bias=b1[0:w, 3 + blk:4 + blk]).then_inc(s("gated"), 1)

            @block.vector
            def _(dve):
                heads = wqkv[:, 0:2 * T].rearrange("p (h s d) -> p h s d", s=2, d=DW // 2)
                swapped = WR[:, :].rearrange("p (h s d) -> p h s d", s=2, d=DW // 2)
                for part in range(2):
                    last = nc.vector.tensor_copy(swapped[:, :, part, :], heads[:, :, 1 - part, :])
                last.then_inc(s("swapped"), 1)
                for i, (name, col) in enumerate((("cosq", 0), ("sinq", 2), ("cosk", 1), ("sink", 3))):
                    nc.vector.tensor_scalar(TAB[:, i, :], cst(name), qks[:, col:col + 1], None, ALU.mult)\
                      .then_inc(s("tables"), 1)
                dve.wait_ge(s("tables"), 4)
                for n in range(NB):
                    for blk in range(BLOCKS):
                        i, w = BLOCKS * n + blk, blk // PAIRS
                        if i >= 2:
                            dve.wait_ge(s("summed"), i - 1)
                        dve.wait_ge(s("squared"), i + 1)
                        nc.vector.tensor_tensor(MIX[:, i % 2, 0, :], psum[:, bank("main", n, blk), :],
                                                TAB[:, 2 * w, :], ALU.mult)
                        dve.wait_ge(s("rot"), i + 1)
                        nc.vector.tensor_tensor(MIX[:, i % 2, 1, :], psum[:, bank("rot", n, blk), :],
                                                TAB[:, 2 * w + 1, :], ALU.mult).then_inc(s("rotated"), 1)
                    for w in range(2):
                        dve.wait_ge(s("sd"), 2 * n + w + 1)
                        nc.vector.tensor_scalar(R[:, n, w, :], R[:, n, w, :], 1e-12, None, ALU.max)\
                          .then_inc(s("clipped"), 1)
                        dve.wait_ge(s("clipped"), 2 * n + w + 1)
                        nc.vector.reciprocal(R[:, n, w, :], R[:, n, w, :]).then_inc(s("norm_recip"), 1)
                dve.wait_ge(s("zeroed"), 3 * NB)
                for n in range(NB):
                    for blk in range(BLOCKS):
                        i, c = BLOCKS * n + blk, blk % PAIRS
                        dve.wait_ge(s("spread"), i + 1)
                        dve.wait_ge(s("summed"), i + 1)
                        r = psum[:, bank("spread", n, blk), :]
                        if blk < PAIRS:
                            nc.vector.tensor_tensor(QZ[0:DW, n, 2 * c, :], O[0:DW, n, c, :], r[0:DW, :], ALU.mult)
                            nc.vector.tensor_tensor(QZ[DW:P, n, 2 * c + 1, :], O[DW:P, n, c, :], r[DW:P, :],
                                                    ALU.mult).then_inc(s("qk_ready"), 1)
                            dve.wait_ge(s("qk_ready"), i + 1)
                            nc.vector.tensor_copy(QB[:, n, 2 * c:2 * c + 2, :], QZ[:, n, 2 * c:2 * c + 2, :])\
                              .then_inc(s("cast"), 1)
                        else:
                            nc.vector.tensor_tensor(K[:, n, c, :], K[:, n, c, :], r, ALU.mult)\
                              .then_inc(s("qk_ready"), 1)
                            dve.wait_ge(s("qk_ready"), i + 1)
                            nc.vector.tensor_copy(KB[:, n, c, WIN:WIN + T], K[:, n, c, :]).then_inc(s("cast"), 1)

                def maxima(i):
                    for j in range(2):
                        head = 2 * i + j
                        if head >= 4:
                            dve.wait_ge(s("diag"), head - 3)
                        for half in range(2):
                            dve.wait_ge(s("s"), 2 * head + half + 1)
                            nc.vector.tensor_reduce(
                                M[:, head % 4, 2 * half:2 * half + 2],
                                psum[:, bank("s", i, j, half), 0:2 * SPAN].rearrange("p (k x) -> p k x", k=2),
                                AX_X, ALU.max).then_inc(s("maxed"), 1)

                def divide(i):
                    n, c = i // PAIRS, i % PAIRS
                    dve.wait_ge(s("den"), i + 1)
                    nc.vector.reciprocal(RD[:, i % 2, :], psum[:, bank("den", i), :]).then_inc(s("den_recip"), 1)
                    dve.wait_ge(s("den_recip"), i + 1)
                    nc.vector.tensor_tensor(O[:, n, c, :], psum[:, bank("o", i), :], RD[:, i % 2, :],
                                            ALU.mult).then_inc(s("o_ready"), 1)

                maxima(0)
                for i in range(STEPS):
                    if i + 1 < STEPS:
                        maxima(i + 1)
                    if i >= 1:
                        divide(i - 1)
                divide(STEPS - 1)

                for n in range(NB):
                    dve.wait_ge(s("wo"), n + 1)
                    nc.vector.tensor_tensor(Y[:, n, :], psum[:, bank("wo", n), :], Y[:, n, :], ALU.add)\
                      .then_inc(s("y_mid"), 1)
                    dve.wait_ge(s("y_mid"), n + 1)
                    shift_dve(nc, s, g, n)
                for n in range(NB):
                    dve.wait_ge(s("mean"), n + 1)
                    nc.vector.tensor_tensor(F1[:, n, :], H[:, n, :], psum[:, bank("mean", n), :], ALU.subtract)\
                      .then_inc(s("ln_centered"), 1)
                for n in range(NB):
                    dve.wait_ge(s("ln_sd"), n + 1)
                    nc.vector.reciprocal(RD[:, n, :], RD[:, n, :]).then_inc(s("ln_recip"), 1)
                    dve.wait_ge(s("ln_recip"), n + 1)
                    nc.vector.scalar_tensor_tensor(out=H[:, n, :], in0=F1[:, n, :], scalar=vecs[:, 0:1],
                                                   in1=RD[:, n, :], op0=ALU.mult, op1=ALU.mult)\
                      .then_inc(s("ln_scaled"), 1)
                    dve.wait_ge(s("ln_scaled"), n + 1)
                    nc.vector.tensor_scalar(H[:, n, :], H[:, n, :], vecs[:, 1:2], None, ALU.add)\
                      .then_inc(s("ln_done"), 1)
                for n in range(NB):
                    for blk, (_, w) in enumerate(HID_BLOCKS):
                        dve.wait_ge(s("up"), 3 * n + blk + 1)
                        dve.wait_ge(s("gated"), 3 * n + blk + 1)
                        nc.vector.scalar_tensor_tensor(
                            out=hidden(n, 1, blk)[0:w, :], in0=psum[0:w, bank("up", n, blk), :],
                            scalar=b1[0:w, blk:blk + 1], in1=hidden(n, 0, blk)[0:w, :],
                            op0=ALU.add, op1=ALU.mult).then_inc(s("hidden"), 1)
                for n in range(NB):
                    dve.wait_ge(s("w2"), n + 1)
                    nc.vector.scalar_tensor_tensor(out=Y[:, n, :], in0=psum[:, bank("w2", n), :],
                                                   scalar=vecs[:, 2:3], in1=Y[:, n, :],
                                                   op0=ALU.add, op1=ALU.add).then_inc(s("y_new"), 1)
                    dve.wait_ge(s("y_new"), n + 1)
                    shift_dve(nc, s, g, n)
        s.close()


def attention_b(nc, g):
    psum, X, Y, cst = g.psum, g.X, g.Y, g.cst
    with ExitStack() as ctx:
        def sb(name, shape, dt=F32):
            return ctx.enter_context(nc.sbuf_tensor("b_" + name, shape, dt))

        first = ln_buffers(lambda name, *rest: sb("1" + name, *rest))
        second = ln_buffers(lambda name, *rest: sb("2" + name, *rest))
        Q = sb("Q", [P, NB, T])
        NEG = sb("NEG", [P, NB, T])
        E = sb("E", [P, NB, T])
        LAT = sb("LAT", [33, NB, T])
        KT = sb("KT", [P, NB, 4, P])
        NEGK = sb("NEGK", [P, NB, 4, P])
        EK = sb("EK", [P, NB, 4, P])
        VT = sb("VT", [P, NB, 4, 2 * P])
        CTX = sb("CTX", [P, NB, 2 * P])
        DEN = sb("DEN", [P, NB, T])
        ON = sb("ON", [P, NB, T])
        s = Phase(nc, "b1")
        block = nc.Block()
        with block:
            @block.gpsimd
            def _(pool):
                for n in range(NB):
                    nc.gpsimd.memset(LAT[32:33, n, :], 1.0).then_inc(s("ones"), 1)
                    pool.wait_ge(s("ones"), 2 * n + 1)
                    nc.gpsimd.memset(VT[:, n, :, P:2 * P], 1.0).then_inc(s("ones"), 1)
                    pool.wait_ge(s("ones"), 2 * n + 2)

            @block.tensor
            def _(pe):
                norm_pe(nc, pe, s, g, first)
                for n in range(NB):
                    pe.wait_ge(s("y_new"), n + 1)
                    nc.tensor.matmul(psum[:, 4 * n, :], g.wq_b[:, :], Y[:, n, :], start=True, stop=True)\
                      .then_inc(s("q"), 1)
                    nc.tensor.matmul(psum[0:32, 4 * n + 1, :], g.wd_b[:, :], Y[:, n, :], start=True, stop=True)\
                      .then_inc(s("latent"), 1)
                pe.wait_ge(s("ones"), 2 * NB)
                for n in range(NB):
                    pe.wait_ge(s("latent_ready"), n + 1)
                    for t in range(4):
                        last = nc.tensor.matmul(psum[:, 4 * n + 2 + t // 2, 256 * (t % 2):256 * (t % 2) + 256],
                                                LAT[:, n, P * t:P * t + P], g.wu_b[:, :], start=True, stop=True)
                        if t % 2:
                            last.then_inc(s("kv"), 1)
                for n in range(NB):
                    pe.wait_ge(s("k_ready"), 2 * n + 2)
                    pe.wait_ge(s("v_ready"), 2 * n + 2)
                    pe.wait_ge(s("q_ready"), n + 1)
                    for t in range(4):
                        last = nc.tensor.matmul(psum[:, 4 * n, 0:2 * P], KT[:, n, t, :], VT[:, n, t, :],
                                                start=(t == 0), stop=(t == 3))
                    last.then_inc(s("context"), 1)
                for n in range(NB):
                    pe.wait_ge(s("context_ready"), n + 1)
                    nc.tensor.matmul(psum[:, 4 * n + 2, :], CTX[:, n, P:2 * P], Q[:, n, :], start=True, stop=True)\
                      .then_inc(s("den"), 1)
                    nc.tensor.matmul(psum[:, 4 * n + 1, :], CTX[:, n, 0:P], Q[:, n, :], start=True, stop=True)\
                      .then_inc(s("num"), 1)
                for n in range(NB):
                    pe.wait_ge(s("o_ready"), n + 1)
                    nc.tensor.matmul(psum[:, 4 * n, :], g.wo_b[:, :], ON[:, n, :], start=True, stop=True)\
                      .then_inc(s("projected"), 1)

            @block.scalar
            def _(act):
                norm_act(nc, act, s, g, first)
                for n in range(NB):
                    act.wait_ge(s("latent"), n + 1)
                    nc.scalar.activation(LAT[0:32, n, :], psum[0:32, 4 * n + 1, :], ACT.Identity,
                                         bias=g.bd_b[:, 0:1]).then_inc(s("latent_ready"), 1)
                for n in range(NB):
                    act.wait_ge(s("q_neg"), n + 1)
                    nc.scalar.activation(E[:, n, :], NEG[:, n, :], ACT.Exp).then_inc(s("q_exp"), 1)
                for n in range(NB):
                    for half in range(2):
                        i = 2 * n + half
                        act.wait_ge(s("k_neg"), i + 1)
                        pair_ = psum[:, 4 * n + 2 + half, :].rearrange("p (t x) -> p t x", t=2)
                        nc.scalar.activation(VT[:, n, 2 * half:2 * half + 2, 0:P], pair_[:, :, P:2 * P],
                                             ACT.Copy).then_inc(s("v_ready"), 1)
                        nc.scalar.activation(EK[:, n, 2 * half:2 * half + 2, :],
                                             NEGK[:, n, 2 * half:2 * half + 2, :], ACT.Exp)\
                          .then_inc(s("k_exp"), 1)

            @block.vector
            def _(dve):
                for n in range(NB):
                    nc.vector.tensor_tensor(X[:, n, :], X[:, n, :], Y[:, n, :], ALU.add).then_inc(s("x_new"), 1)
                dve.wait_ge(s("x_new"), NB)
                norm_dve(nc, dve, s, g, first)
                for n in range(NB):
                    dve.wait_ge(s("q"), n + 1)
                    nc.vector.tensor_scalar(NEG[:, n, :], psum[:, 4 * n, :], g.bq_b[:, 0:1], 0.0,
                                            ALU.add, ALU.min).then_inc(s("q_neg"), 1)
                    nc.vector.tensor_scalar(Q[:, n, :], psum[:, 4 * n, :], g.bq_b[:, 0:1], 0.0,
                                            ALU.add, ALU.max).then_inc(s("q_pos"), 1)
                    dve.wait_ge(s("q_pos"), n + 1)
                    dve.wait_ge(s("q_exp"), n + 1)
                    nc.vector.tensor_tensor(Q[:, n, :], Q[:, n, :], E[:, n, :], ALU.add).then_inc(s("q_ready"), 1)
                for n in range(NB):
                    for half in range(2):
                        i = 2 * n + half
                        dve.wait_ge(s("kv"), i + 1)
                        pair_ = psum[:, 4 * n + 2 + half, :].rearrange("p (t x) -> p t x", t=2)
                        nc.vector.tensor_scalar(NEGK[:, n, 2 * half:2 * half + 2, :], pair_[:, :, 0:P], 0.0, None,
                                                ALU.min).then_inc(s("k_neg"), 1)
                    for half in range(2):
                        i = 2 * n + half
                        pair_ = psum[:, 4 * n + 2 + half, :].rearrange("p (t x) -> p t x", t=2)
                        dve.wait_ge(s("k_exp"), i + 1)
                        nc.vector.scalar_tensor_tensor(out=KT[:, n, 2 * half:2 * half + 2, :],
                                                       in0=pair_[:, :, 0:P], scalar=0.0,
                                                       in1=EK[:, n, 2 * half:2 * half + 2, :],
                                                       op0=ALU.max, op1=ALU.add).then_inc(s("k_ready"), 1)
                for n in range(NB):
                    dve.wait_ge(s("context"), n + 1)
                    nc.vector.tensor_tensor(CTX[:, n, :], psum[:, 4 * n, 0:2 * P], cst("block8"), ALU.mult)\
                      .then_inc(s("context_ready"), 1)
                for n in range(NB):
                    dve.wait_ge(s("den"), n + 1)
                    nc.vector.tensor_scalar(DEN[:, n, :], psum[:, 4 * n + 2, :], 1e-6, None, ALU.add)\
                      .then_inc(s("den_ready"), 1)
                    dve.wait_ge(s("den_ready"), n + 1)
                    nc.vector.reciprocal(DEN[:, n, :], DEN[:, n, :]).then_inc(s("den_recip"), 1)
                    dve.wait_ge(s("den_recip"), n + 1)
                    dve.wait_ge(s("num"), n + 1)
                    nc.vector.tensor_tensor(ON[:, n, :], psum[:, 4 * n + 1, :], DEN[:, n, :], ALU.mult)\
                      .then_inc(s("o_ready"), 1)
                for n in range(NB):
                    dve.wait_ge(s("projected"), n + 1)
                    nc.vector.scalar_tensor_tensor(out=X[:, n, :], in0=psum[:, 4 * n, :], scalar=g.bo_b[:, 0:1],
                                                   in1=X[:, n, :], op0=ALU.add, op1=ALU.add).then_inc(s("x_out"), 1)
        s.close()
        s = Phase(nc, "b2")
        block = nc.Block()
        with block:
            @block.tensor
            def _(pe):
                norm_pe(nc, pe, s, g, second)

            @block.scalar
            def _(act):
                norm_act(nc, act, s, g, second)

            @block.vector
            def _(dve):
                for n in range(NB):
                    nc.vector.engine_nop().then_inc(s("x_new"), 1)
                norm_dve(nc, dve, s, g, second)
                for n in range(NB):
                    dve.wait_ge(s("y_new"), n + 1)
                    shift_dve(nc, s, g, n)
        s.close()


def store(nc, g, out, pair):
    psum, X, Y = g.psum, g.X, g.Y
    with ExitStack() as ctx:
        OUT = ctx.enter_context(nc.sbuf_tensor("OUT", [P, NB, 4, P], F32))
        s = Phase(nc, "out")
        block = nc.Block()
        with block:
            @block.vector
            def _(dve):
                for n in range(NB):
                    nc.vector.tensor_tensor(X[:, n, :], X[:, n, :], Y[:, n, :], ALU.add).then_inc(s("x_new"), 1)

            @block.tensor
            def _(pe):
                for n in range(NB):
                    pe.wait_ge(s("x_new"), n + 1)
                    for t in range(4):
                        last = nc.tensor.transpose(psum[:, n, P * t:P * t + P], X[:, n, P * t:P * t + P], g.ident)
                    last.then_inc(s("turned"), 1)

            @block.scalar
            def _(act):
                for n in range(NB):
                    act.wait_ge(s("turned"), n + 1)
                    nc.scalar.activation(OUT[:, n, :, :].rearrange("p t d -> p (t d)"), psum[:, n, :], ACT.Copy)\
                      .then_inc(s("copied"), 1)

            @block.sync
            def _(sp):
                for n in range(NB):
                    sp.wait_ge(s("copied"), n + 1)
                    dst = out[bass.ds(pair * NB + n, 1)].rearrange("a (t p) d -> p (a t) d", p=P)
                    sp.dma_start(dst, OUT[:, n, :, :]).then_inc(s("stored"), 16)
                sp.wait_ge(s("stored"), 16 * NB)
        s.close()


def kernel(**inputs):
    import concourse.bacc as bacc
    from concourse.bass_utils import run_bass_kernel_spmd

    nc = bacc.Bacc("TRN2", target_bir_lowering=False, num_devices=1)
    arrays = {name: np.ascontiguousarray(a) for name, a in inputs.items()}
    c, b = constants()
    arrays["const"] = c
    arrays["constb"] = b
    args = {name: nc.dram_tensor(name + "_dram", a.shape, mybir.dt.from_np(a.dtype), kind="ExternalInput").ap()
            for name, a in arrays.items()}
    shape = inputs["L0_attn_a_x"].shape
    out = nc.dram_tensor("out_dram", shape, F32, kind="ExternalOutput").ap()
    build(nc, args, out)
    r = run_bass_kernel_spmd(nc, [{name + "_dram": a for name, a in arrays.items()}], core_ids=[0])
    return r.results[0]["out_dram"]
```

```python
from contextlib import ExitStack

import numpy as np

import concourse.bass as bass
from concourse import mybir

F32 = mybir.dt.float32
F32R = mybir.dt.float32r
BF16 = mybir.dt.bfloat16
ACT = mybir.ActivationFunctionType
ALU = mybir.AluOpType
AX_X = mybir.AxisListType.X

P = 128
T = 512
NB = 2
BANKS = 8

HA, DA = 16, 8
RUNS = [(0, 2), (0, 1), (0, 0), (1, 2), (2, 2)]
SLOTS = 9
GUARD_ROW = SLOTS * DA
LAG = 3
HW, DW, WIN = 8, 64, 64
PAIRS = HW // 2
SPAN = P + WIN
HID = 341
HID_BLOCKS = [(0, 128), (128, 128), (256, HID - 256)]
MASKED = -1e30
LN_EPS = 1e-5
EXP_AND_LN = "natural_log_exp_and_others"

_WIDTHS = [("ident", P), ("mean", P), ("cosq", T), ("sinq", T), ("cosk", T), ("sink", T),
           ("pick_num", 4 * P), ("pick_den", 4 * P), ("head_sum", 64), ("block8", 2 * P), ("ones", DW)]
CONST = {}
_at = 0
for _name, _w in _WIDTHS:
    CONST[_name] = (_at, _at + _w)
    _at += _w
CONST_COLS = _at
CONSTB = {"ident": (0, P), "minus1": (P, 2 * P), "mask_first": (2 * P, 2 * P + SPAN),
          "mask_q": (2 * P + SPAN, 2 * P + 2 * SPAN), "mask_k": (2 * P + 2 * SPAN, 2 * P + 3 * SPAN)}
CONSTB_COLS = 2 * P + 3 * SPAN
SPREAD_COLS = 8 * P


def constants():
    c = np.zeros((P, CONST_COLS), np.float32)

    def col(name):
        a, b = CONST[name]
        return c[:, a:b]

    r = np.arange(P)
    col("ident")[:] = np.eye(P)
    col("mean")[:] = 1.0 / P
    half = np.arange(0, DW, 2, dtype=np.float32)
    inv_freq = (1.0 / np.float32(10000.0) ** (half / DW)).astype(np.float32)
    t = np.arange(T, dtype=np.float32)
    freqs = t[:, None] * inv_freq[None, :]
    base = (half + np.float32(0.4 * DW)) / np.float32(1.4 * DW)
    scale = base[None, :] ** ((t - T // 2) / np.float32(WIN // 2))[:, None]
    freqs, scale = (np.concatenate([a, a], -1).T for a in (freqs, scale))
    cos, sin = np.cos(freqs), np.sin(freqs)
    sin = sin * np.where(np.arange(DW) < DW // 2, -1, 1)[:, None]
    for name, table in (("cosq", cos * scale), ("sinq", sin * scale), ("cosk", cos / scale), ("sink", sin / scale)):
        col(name)[:] = np.concatenate([table, table], 0)
    for g in range(4):
        for j in range(4):
            for d in range(DA):
                out = g * P + DA * (4 * g + j) + d
                col("pick_num")[32 * j + d, out] = 1
                col("pick_den")[32 * j + DA, out] = 1
    col("head_sum")[:] = np.concatenate([(r[:, None] // DW + 2 * w) == (np.arange(32)[None, :] // 8)
                                         for w in range(2)], 1)
    same = (r[:, None] // DA) == (r[None, :] // DA)
    col("block8")[:] = np.concatenate([same, same], 1)
    col("ones")[:] = 1
    b = np.zeros((P, CONSTB_COLS + SPREAD_COLS), np.float32)
    for i in range(16):
        b[8 * i, CONSTB_COLS + DW * i:CONSTB_COLS + DW * i + DW] = 1
    b[:, 0:P] = np.eye(P)
    b[:, P:2 * P] = -1
    x = np.arange(SPAN)[None, :]
    far = r[:, None] + WIN - x
    b[:, 2 * P:2 * P + SPAN] = np.where((far >= 0) & (far <= WIN) & (x >= WIN), 0, MASKED)
    b[:, 2 * P + SPAN:2 * P + 2 * SPAN] = np.where((far >= 0) & (far <= WIN), 0, MASKED)
    far = x - r[:, None]
    b[:, 2 * P + 2 * SPAN:CONSTB_COLS] = np.where((far >= 0) & (far <= WIN), 0, MASKED)
    return c, b


class Kept:
    pass


class Phase:

    def __init__(self, nc, label):
        self.nc, self.label, self.held, self.ctx = nc, label, {}, ExitStack()

    def __call__(self, name):
        if name not in self.held:
            self.held[name] = self.ctx.enter_context(self.nc.semaphore(f"{self.label}_{name}"))
        return self.held[name]

    def close(self):
        numbers = sorted(x.num for x in self.held.values())
        start = 0
        for i in range(1, len(numbers) + 1):
            if i == len(numbers) or numbers[i] != numbers[i - 1] + 1:
                self.nc.gpsimd.sem_clear(range(numbers[start], numbers[i - 1] + 1))
                start = i
        self.nc.all_engine_barrier(sem_only=True)
        self.ctx.close()


def build(nc, a, out):
    x_d = a["L0_attn_a_x"]
    B = x_d.shape[0]
    with ExitStack() as top:
        def sb(name, shape, dt=F32, ctx=top):
            return ctx.enter_context(nc.sbuf_tensor(name, shape, dt))

        psum = top.enter_context(nc.psum_tensor("psum", [P, BANKS, T], F32))
        const = sb("const", [P, CONST_COLS])
        constb = sb("constb", [P, CONSTB_COLS], BF16)
        spread_w = sb("spread_w", [P, SPREAD_COLS], F32R)
        X = sb("X", [P, NB, T])
        Y = sb("Y", [P, NB, T])
        H = sb("H", [P, NB, T])
        eps = sb("eps", [P, 1])
        wa = sb("wa", [P, 3 * P])
        wpa = sb("wpa", [P, P])
        bqk = sb("bqk", [P, 3])
        bpa = sb("bpa", [P, 1])
        wq_b = sb("wq_b", [P, P])
        bq_b = sb("bq_b", [P, 1])
        wd_b = sb("wd_b", [P, 32])
        bd_b = sb("bd_b", [32, 1])
        wu_b = sb("wu_b", [33, 2 * P])
        wo_b = sb("wo_b", [P, P])
        bo_b = sb("bo_b", [P, 1])
        wqkv = sb("wqkv", [P, 3 * T])
        wo = sb("wo", [P, PAIRS, P])
        w1 = sb("w1", [P, 2 * HID])
        w2 = sb("w2", [P, 3, P])
        b1 = sb("b1", [P, 6])
        vecs = sb("vecs", [P, 3])
        qks = sb("qks", [P, 4])

        def cst(name, lo=0, n=None):
            s, e = CONST[name]
            return const[:, s + lo:e if n is None else s + lo + n]

        def cstb(name, lo=0, n=None):
            s, e = CONSTB[name]
            return constb[:, s + lo:e if n is None else s + lo + n]

        ident, mean_w = cst("ident"), cst("mean")

        def load_layer(sp, layer, sem):
            def row(name):
                return a[name][bass.ds(layer, 1)]
            n = 0
            for dst, src in (
                (wo[:, :, :], row("L0_ffn_wo").rearrange("a (c p) n -> p (a c) n", p=P)),
                (w1[:, :], row("L0_ffn_w1").rearrange("a p n -> (a p) n")),
                (w2[:, 0:2, :], row("L0_ffn_w2")[:, 0:256, :].rearrange("a (c p) n -> p (a c) n", p=P)),
                (w2[0:HID - 256, 2, :], row("L0_ffn_w2")[:, 256:HID, :].rearrange("a p n -> (a p) n")),
                *((b1[0:w, 3 * part + i:3 * part + i + 1],
                   row("L0_ffn_b1")[:, HID * part + lo:HID * part + lo + w].rearrange("a (p c) -> (a p) c", c=1))
                  for part in range(2) for i, (lo, w) in enumerate(HID_BLOCKS)),
                (vecs[:, 0:1], row("L0_ffn_ln_g").rearrange("a (p c) -> (a p) c", c=1)),
                (vecs[:, 1:2], row("L0_ffn_ln_b").rearrange("a (p c) -> (a p) c", c=1)),
                (vecs[:, 2:3], row("L0_ffn_b2").rearrange("a (p c) -> (a p) c", c=1)),
            ):
                sp.dma_start(dst, src).then_inc(sem, 16)
                n += 16
            return n

        def layer_attention_weights(layer):
            def row(name):
                return a[name][bass.ds(layer, 1)]
            pieces = [(wqkv[:, :], row("L0_ffn_wqkv").rearrange("a p n -> (a p) n"))]
            for at, name in ((0, "L0_ffn_q_scale"), (1, "L0_ffn_k_scale")):
                v = row(name).rearrange("a (p c) -> (a p) c", c=1)
                for h in range(2):
                    pieces.append((qks[DW * h:DW * h + DW, at:at + 1], v))
                    for s in range(2):
                        dst = DW * h + 32 * s
                        pieces.append((qks[dst:dst + 32, at + 2:at + 3], v[32 * (1 - s):32 * (1 - s) + 32, :]))
            return pieces

        def column(v):
            return v.rearrange("(p c) -> p c", c=1)

        def attention_b_weights():
            wu = a["L0_attn_b_Wu"].rearrange("r (h c d) -> c r h d", c=2, d=DA)
            bu = a["L0_attn_b_bu"].rearrange("(o h c d) -> c o h d", o=1, c=2, d=DA)
            return [(wq_b[:, :], a["L0_attn_b_Wq"]), (bq_b[:, :], column(a["L0_attn_b_bq"])),
                    (wd_b[:, :], a["L0_attn_b_Wd"]), (bd_b[:, :], column(a["L0_attn_b_bd"])),
                    (wu_b[0:32, 0:P].rearrange("r (h d) -> r h d", d=DA), wu[0]),
                    (wu_b[0:32, P:2 * P].rearrange("r (h d) -> r h d", d=DA), wu[1]),
                    (wu_b[32:33, 0:P].rearrange("r (h d) -> r h d", d=DA), bu[0]),
                    (wu_b[32:33, P:2 * P].rearrange("r (h d) -> r h d", d=DA), bu[1]),
                    (wo_b[:, :], a["L0_attn_b_Wo"]), (bo_b[:, :], column(a["L0_attn_b_bo"]))]

        parts_d = nc.dram_tensor("parts", [NB, 2, HA, 3, DA, T], BF16).ap()
        minus_ones = nc.dram_tensor("minus_ones", [1, HA, T], BF16).ap()
        s = Phase(nc, "load")
        casting = ExitStack()
        constb_f = casting.enter_context(nc.sbuf_tensor("constb_f", [P, CONSTB_COLS + SPREAD_COLS], F32))
        minus = casting.enter_context(nc.sbuf_tensor("minus", [HA, T], BF16))
        block = nc.Block()
        with block:
            @block.vector
            def _(dve):
                nc.vector.memset(minus[:, :], -1.0).then_inc(s("minus"), 1)
                dve.wait_ge(s("tables"), 16)
                nc.vector.tensor_copy(constb[:, :], constb_f[:, 0:CONSTB_COLS]).then_inc(s("tables_cast"), 1)
                nc.vector.tensor_copy(spread_w[:, :], constb_f[:, CONSTB_COLS:]).then_inc(s("tables_cast"), 1)

            @block.sync
            def _(sp):
                n = 0
                sp.dma_start(constb_f[:, :], a["constb"]).then_inc(s("tables"), 16)
                sp.wait_ge(s("minus"), 1)
                sp.dma_start(minus_ones[0], minus[:, :]).then_inc(s("loaded"), 16)
                n += 16
                for dst, src in (
                    (const[:, :], a["const"]),
                    (wa[:, :], a["L0_attn_a_w_qkv"]), (wpa[:, :], a["L0_attn_a_w_proj"]),
                    *((bqk[:, i:i + 1], column(a["L0_attn_a_b_qkv"][P * i:P * i + P])) for i in range(3)),
                    (bpa[:, :], column(a["L0_attn_a_b_proj"])),
                ):
                    sp.dma_start(dst, src).then_inc(s("loaded"), 16)
                    n += 16
                sp.wait_ge(s("loaded"), n)

            @block.gpsimd
            def _(pool):
                nc.gpsimd.memset(eps[:, :], LN_EPS).then_inc(s("eps"), 1)
                pool.wait_ge(s("eps"), 1)
        s.close()
        casting.close()

        g = Kept()
        g.psum, g.X, g.Y, g.H, g.eps, g.cst = psum, X, Y, H, eps, cst
        g.cstb, g.ident, g.mean_w, g.x_d, g.wa, g.wpa = cstb, ident, mean_w, x_d, wa, wpa
        g.bqk, g.bpa, g.wq_b, g.bq_b, g.wd_b, g.bd_b = bqk, bpa, wq_b, bq_b, wd_b, bd_b
        g.wu_b, g.wo_b, g.bo_b, g.wqkv, g.wo, g.w1 = wu_b, wo_b, bo_b, wqkv, wo, w1
        g.w2, g.b1, g.vecs, g.qks, g.load_layer = w2, b1, vecs, qks, load_layer
        g.attention_b_weights, g.layer_attention_weights = attention_b_weights, layer_attention_weights
        g.parts_d, g.minus_ones, g.spread_w = parts_d, minus_ones, spread_w
        g.LATE_WEIGHTS = 16 * 13
        with nc.Fori(0, B // NB) as pair:
            attention_a(nc, a, g, pair)
            with nc.Fori(0, 2) as layer:
                feed_forward(nc, g, layer, 0)
            attention_b(nc, g)
            with nc.Fori(0, 2) as layer:
                feed_forward(nc, g, layer, 1)
            store(nc, g, out, pair)


def shift_dve(nc, s, g, n):
    nc.vector.tensor_copy(g.H[0:64, n, :], g.Y[0:64, n, :])
    nc.vector.tensor_copy(g.H[64:P, n, 1:T], g.Y[64:P, n, 0:T - 1])
    nc.vector.memset(g.H[64:P, n, 0:1], 0.0).then_inc(s("shifted"), 1)


def attention_a(nc, a, g, pair):
    psum, X, Y, eps, cst, ident, mean_w = g.psum, g.X, g.Y, g.eps, g.cst, g.ident, g.mean_w
    wa, wpa, bqk, bpa, x_d, parts_d = g.wa, g.wpa, g.bqk, g.bpa, g.x_d, g.parts_d
    with ExitStack() as ctx:
        def sb(name, shape, dt=F32):
            return ctx.enter_context(nc.sbuf_tensor(name, shape, dt))

        QS = sb("QS", [P, NB, HA, T], BF16)
        KS = sb("KS", [P, NB, HA, T], BF16)
        VA = sb("VA", [P, NB, 4, HA, 16])
        OC = sb("OC", [P, NB, 4, T])

        with ExitStack() as prep:
            def sp_(name, shape, dt=F32):
                return prep.enter_context(nc.sbuf_tensor(name, shape, dt))
            XT = sp_("XT", [P, NB, 4, P])
            XC = sp_("XC", [P, NB, T])
            SQ = sp_("SQ", [P, NB, T])
            SD = sp_("SD", [P, NB, T])
            RS = sp_("RS", [P, NB, T])
            QF = sp_("QF", [P, NB, 2, T])
            PRT = sp_("PRT", [P, NB, 2, 3, T], BF16)
            R1 = sp_("R1", [P, NB, 2, T])
            s = Phase(nc, "a1")
            block = nc.Block()
            with block:
                @block.sync
                def _(sp):
                    for n in range(NB):
                        src = x_d[bass.ds(pair * NB + n, 1)].rearrange("a (t p) d -> p (a t) d", p=P)
                        sp.dma_start(XT[:, n, :, :], src).then_inc(s(f"x_loaded{n}"), 16)
                    for n in range(NB):
                        for w in range(2):
                            for part in range(3):
                                sp.wait_ge(s(("hi", "mid", "split")[part]), 2 * n + w + 1)
                                place = part if w == 0 else 2 - part
                                sp.dma_start(parts_d[n, w, :, place], PRT[:, n, w, part, :])\
                                  .then_inc(s(f"parts_out{n}"), 16)
                        sp.wait_ge(s(f"parts_out{n}"), 6 * 16)
                        for w, stack in ((0, QS), (1, KS)):
                            slot = 0
                            for first, last in RUNS:
                                rows = DA * (last - first + 1)
                                if DA * slot + rows > 64 and w == 0 and n == 0:
                                    sp.wait_ge(s("stacks_zero"), NB)
                                lo = first if w == 0 else 2 - last
                                src = parts_d[n, w, :, lo:lo + last - first + 1].rearrange("h c d t -> (c d) h t")
                                sp.dma_start(stack[DA * slot:DA * slot + rows, n, :, :], src)\
                                  .then_inc(s("stacked"), 16)
                                slot += last - first + 1
                        sp.dma_start(KS[GUARD_ROW:GUARD_ROW + 1, n, :, :],
                                     g.minus_ones).then_inc(s("stacked"), 16)
                    sp.wait_ge(s("stacked"), 16 * NB * (2 * len(RUNS) + 1))

                @block.gpsimd
                def _(pool):
                    for i, stack in enumerate((QS, KS)):
                        rows = stack[64:P, :, :, :].rearrange("p n h t -> p (n h t)").bitcast(F32)
                        nc.gpsimd.memset(rows, 0.0).then_inc(s("stacks_zero"), 1)
                        pool.wait_ge(s("stacks_zero"), i + 1)
                    for n in range(NB):
                        nc.gpsimd.memset(VA[:, n, :, :, :], 0.0).then_inc(s("v_zero"), 1)
                        pool.wait_ge(s("v_zero"), n + 1)
                    for n in range(NB):
                        nc.gpsimd.memset(VA[:, n, :, :, DA:DA + 1], 1.0).then_inc(s("v_ones"), 1)
                    pool.wait_ge(s("v_ones"), NB)

                @block.tensor
                def _(pe):
                    for n in range(NB):
                        pe.wait_ge(s(f"x_loaded{n}"), 16)
                        for t in range(4):
                            last = nc.tensor.transpose(psum[:, 4 * n, P * t:P * t + P], XT[:, n, t, :], ident)
                        last.then_inc(s("x_turned"), 1)
                    for n in range(NB):
                        pe.wait_ge(s("x_copied"), n + 1)
                        nc.tensor.matmul(psum[:, 4 * n + 1, :], mean_w, X[:, n, :], start=True, stop=True)\
                          .then_inc(s("ln_mean"), 1)
                    for n in range(NB):
                        pe.wait_ge(s("ln_squared"), n + 1)
                        nc.tensor.matmul(psum[:, 4 * n + 2, :], mean_w, SQ[:, n, :], start=True, stop=True)\
                          .then_inc(s("ln_var"), 1)
                    for n in range(NB):
                        pe.wait_ge(s("ln_done"), n + 1)
                        for w in range(2):
                            nc.tensor.matmul(psum[:, 4 * n + w, :], wa[:, P * w:P * w + P], XC[:, n, :],
                                             start=True, stop=True).then_inc(s("qk"), 1)
                        for t in range(4):
                            last = nc.tensor.matmul(psum[:, 4 * n + 3, P * t:P * t + P], XC[:, n, P * t:P * t + P],
                                                    wa[:, 2 * P:3 * P], start=True, stop=True)
                        last.then_inc(s("v"), 1)

                @block.scalar
                def _(act):
                    for n in range(NB):
                        act.wait_ge(s("x_turned"), n + 1)
                        nc.scalar.activation(X[:, n, :], psum[:, 4 * n, :], ACT.Copy).then_inc(s("x_copied"), 1)
                    for n in range(NB):
                        act.wait_ge(s("ln_centered"), n + 1)
                        nc.scalar.activation(SQ[:, n, :], XC[:, n, :], ACT.Square).then_inc(s("ln_squared"), 1)
                    for n in range(NB):
                        act.wait_ge(s("ln_var"), n + 1)
                        nc.scalar.activation(SD[:, n, :], psum[:, 4 * n + 2, :], ACT.Sqrt, bias=eps[:, 0:1])\
                          .then_inc(s("ln_sd"), 1)
                    for n in range(NB):
                        for w in range(2):
                            act.wait_ge(s("qk"), 2 * n + w + 1)
                            nc.scalar.activation(QF[:, n, w, :], psum[:, 4 * n + w, :], ACT.Identity,
                                                 bias=bqk[:, w:w + 1]).then_inc(s("qk_biased"), 1)
                        act.wait_ge(s("v"), n + 1)
                        act.wait_ge(s("v_ones"), NB)
                        nc.scalar.activation(VA[:, n, :, :, 0:DA],
                                             psum[:, 4 * n + 3, :].rearrange("p (t h d) -> p t h d", t=4, d=DA),
                                             ACT.Copy).then_inc(s("v_copied"), 1)

                @block.vector
                def _(dve):
                    for n in range(NB):
                        dve.wait_ge(s("ln_mean"), n + 1)
                        nc.vector.tensor_tensor(XC[:, n, :], X[:, n, :], psum[:, 4 * n + 1, :], ALU.subtract)\
                          .then_inc(s("ln_centered"), 1)
                    for n in range(NB):
                        dve.wait_ge(s("ln_sd"), n + 1)
                        nc.vector.reciprocal(RS[:, n, :], SD[:, n, :]).then_inc(s("ln_recip"), 1)
                        dve.wait_ge(s("ln_recip"), n + 1)
                        nc.vector.tensor_tensor(XC[:, n, :], XC[:, n, :], RS[:, n, :], ALU.mult)\
                          .then_inc(s("ln_done"), 1)
                    for n in range(NB):
                        for w in range(2):
                            i = 2 * n + w
                            dve.wait_ge(s("qk_biased"), i + 1)
                            nc.vector.tensor_copy(PRT[:, n, w, 0, :], QF[:, n, w, :]).then_inc(s("hi"), 1)
                            dve.wait_ge(s("hi"), i + 1)
                            nc.vector.tensor_tensor(R1[:, n, w, :], QF[:, n, w, :], PRT[:, n, w, 0, :],
                                                    ALU.subtract).then_inc(s("rest"), 1)
                            dve.wait_ge(s("rest"), i + 1)
                            nc.vector.tensor_copy(PRT[:, n, w, 1, :], R1[:, n, w, :]).then_inc(s("mid"), 1)
                            dve.wait_ge(s("mid"), i + 1)
                            nc.vector.tensor_tensor(PRT[:, n, w, 2, :], R1[:, n, w, :], PRT[:, n, w, 1, :],
                                                    ALU.subtract).then_inc(s("split"), 1)
            s.close()

        with ExitStack() as main:
            def sm(name, shape, dt=F32):
                return main.enter_context(nc.sbuf_tensor(name, shape, dt))
            PT = sm("PT", [P, 8, 4, T])
            M = sm("M", [P, 4, 2, 4])
            MROW = sm("MROW", [2, 4, T], BF16)
            s = Phase(nc, "a2")
            UNITS = NB * HA // 2
            SLOT = [(2, 3), (4, 5)]
            O_BANK = 6
            TURN_AFTER = 2

            ring = []
            for u in range(UNITS + 1):
                for k in range(8):
                    if k == TURN_AFTER and u:
                        ring.append(("row", u - 1))
                    if u < UNITS:
                        ring.append(("tile", 8 * u + k))
            at = {use: i for i, use in enumerate(ring)}

            def bank(*use):
                return (0, 1, 7)[at[use] % 3]

            def where(unit):
                return unit // (HA // 2), 2 * (unit % (HA // 2))

            block = nc.Block()
            with block:
                @block.tensor
                def _(pe):
                    def take(*use):
                        if at[use] >= 3:
                            kind, i = ring[at[use] - 3]
                            pe.wait_ge(s("maxed" if kind == "tile" else "row_made"), i + 1)
                        return bank(*use)

                    def scores(unit, k):
                        n, h = where(unit)
                        qt = k % 4
                        nc.tensor.matmul(psum[:, take("tile", 8 * unit + k), :],
                                         QS[:, n, h + k // 4, P * qt:P * qt + P],
                                         KS[:, n, h + k // 4, :], start=True, stop=True)\
                          .then_inc(s("scored"), 1)

                    def turn_maxima(unit):
                        dst = take("row", unit)
                        pe.wait_ge(s("maxed"), 8 * (unit + 1))
                        for qt in range(4):
                            last = nc.tensor.transpose(psum[0:2, dst, P * qt:P * qt + P],
                                                       M[:, unit % 4, :, qt], ident)
                        last.then_inc(s("turned"), 1)

                    def scores_by_key(unit, k):
                        n, h = where(unit)
                        j, kt = k // 4, k % 4
                        if k == 0:
                            pe.wait_ge(s(f"row_in{unit % 4}"), 32 * (unit // 4 + 1))
                        i = (2 * unit + j) * 2 + kt // 2
                        if i >= 2 and kt % 2 == 0:
                            pe.wait_ge(s("exped"), i - 1)
                        last = nc.tensor.matmul(psum[:, SLOT[i % 2][kt % 2], :],
                                                KS[:, n, h + j, P * kt:P * kt + P],
                                                QS[:, n, h + j, :], start=True, stop=True)
                        if kt % 2:
                            last.then_inc(s("scored_by_key"), 1)

                    def weighted_sums(group, kt):
                        n, quad = group // 4, group % 4
                        if kt == 0:
                            pe.wait_ge(s("exped"), 8 * (group + 1))
                            if group:
                                pe.wait_ge(s("o_copied"), group)
                            else:
                                pe.wait_ge(s("o_zeroed"), 1)
                        for j in range(4):
                            last = nc.tensor.matmul(psum[32 * j:32 * j + 16, O_BANK, :],
                                                    VA[:, n, kt, 4 * quad + j, :], PT[:, (4 * group + j) % 8, kt, :],
                                                    start=(kt == 0), stop=(kt == 3))
                        if kt == 3:
                            last.then_inc(s("summed"), 1)

                    for u in range(LAG):
                        for k in range(8):
                            if k == TURN_AFTER and u:
                                turn_maxima(u - 1)
                            scores(u, k)
                    for u in range(UNITS):
                        for k in range(8):
                            if k == TURN_AFTER and u + LAG <= UNITS:
                                turn_maxima(u + LAG - 1)
                            if u + LAG < UNITS:
                                scores(u + LAG, k)
                            scores_by_key(u, k)
                            if k % 4 == 3 and u >= 2:
                                weighted_sums(u // 2 - 1, 2 * (u % 2) + k // 4)
                    for kt in range(4):
                        weighted_sums(UNITS // 2 - 1, kt)

                @block.vector
                def _(dve):
                    nc.vector.memset(psum[:, O_BANK, :], 0.0).then_inc(s("o_zeroed"), 1)
                    for u in range(UNITS):
                        for k in range(8):
                            i = 8 * u + k
                            dve.wait_ge(s("scored"), i + 1)
                            if u >= 4 and k == 0:
                                dve.wait_ge(s("turned"), u - 3)
                            nc.vector.tensor_reduce(M[:, u % 4, k // 4, k % 4:k % 4 + 1],
                                                    psum[:, bank("tile", i), :], AX_X, ALU.max)\
                              .then_inc(s("maxed"), 1)

                @block.sync
                def _(sp):
                    pieces = g.layer_attention_weights(0) + g.attention_b_weights()
                    todo = list(pieces)
                    for u in range(UNITS):
                        n, h = where(u)
                        sp.wait_ge(s("row_made"), u + 1)
                        for j in range(2):
                            sp.dma_start(QS[GUARD_ROW:GUARD_ROW + 1, n, h + j, :], MROW[j:j + 1, u % 4, :])\
                              .then_inc(s(f"row_in{u % 4}"), 16)
                        for dst, src in todo[:3]:
                            sp.dma_start(dst, src).then_inc(s("weights"), 16)
                        todo = todo[3:]
                    assert not todo
                    sp.wait_ge(s("weights"), 16 * len(pieces))

                @block.scalar
                def _(act):
                    def copy_sums(group):
                        act.wait_ge(s("summed"), group + 1)
                        nc.scalar.activation(OC[:, group // 4, group % 4, :], psum[:, O_BANK, :], ACT.Copy)\
                          .then_inc(s("o_copied"), 1)

                    def make_row(unit):
                        act.wait_ge(s("turned"), unit + 1)
                        if unit >= 4:
                            act.wait_ge(s(f"row_in{unit % 4}"), 32 * (unit // 4))
                        nc.scalar.activation(MROW[:, unit % 4, :], psum[0:2, bank("row", unit), :], ACT.Copy)\
                          .then_inc(s("row_made"), 1)

                    for u in range(LAG - 1):
                        make_row(u)
                    for u in range(UNITS):
                        for half in range(4):
                            head = 2 * u + half // 2
                            if head >= 8 and head % 4 == 0 and half % 2 == 0:
                                act.wait_ge(s("summed"), head // 4 - 1)
                            i = 4 * u + half
                            act.wait_ge(s("scored_by_key"), i + 1)
                            nc.scalar.activation(PT[:, head % 8, 2 * (half % 2):2 * (half % 2) + 2, :],
                                                 psum[:, SLOT[i % 2][0]:SLOT[i % 2][1] + 1, :], ACT.Exp,
                                                 scale=float(DA) ** -0.5).then_inc(s("exped"), 1)
                            if half == 0 and u + LAG <= UNITS:
                                make_row(u + LAG - 1)
                        if u % 2 and u > 2:
                            copy_sums(u // 2 - 1)
                    copy_sums(UNITS // 2 - 1)
            s.close()

        with ExitStack() as tail:
            def st(name, shape, dt=F32):
                return tail.enter_context(nc.sbuf_tensor(name, shape, dt))
            RD = st("RD", [P, NB, T])
            ON = st("ON", [P, NB, T])
            bufs = ln_buffers(st)
            s = Phase(nc, "a3")
            block = nc.Block()
            with block:
                @block.tensor
                def _(pe):
                    for n in range(NB):
                        for quad in range(4):
                            nc.tensor.matmul(psum[:, 4 * n, :], cst("pick_den", P * quad, P), OC[:, n, quad, :],
                                             start=(quad == 0), stop=(quad == 3))\
                              .then_inc(s("den"), 1)
                        for quad in range(4):
                            nc.tensor.matmul(psum[:, 4 * n + 1, :], cst("pick_num", P * quad, P), OC[:, n, quad, :],
                                             start=(quad == 0), stop=(quad == 3))\
                              .then_inc(s("num"), 1)
                    for n in range(NB):
                        pe.wait_ge(s("o_ready"), n + 1)
                        nc.tensor.matmul(psum[:, 4 * n + 2, :], wpa[:, :], ON[:, n, :], start=True, stop=True)\
                          .then_inc(s("projected"), 1)
                    norm_pe(nc, pe, s, g, bufs)

                @block.scalar
                def _(act):
                    norm_act(nc, act, s, g, bufs)

                @block.vector
                def _(dve):
                    for n in range(NB):
                        dve.wait_ge(s("den"), 4 * n + 4)
                        nc.vector.reciprocal(RD[:, n, :], psum[:, 4 * n, :]).then_inc(s("rden"), 1)
                        dve.wait_ge(s("num"), 4 * n + 4)
                        dve.wait_ge(s("rden"), n + 1)
                        nc.vector.tensor_tensor(ON[:, n, :], psum[:, 4 * n + 1, :], RD[:, n, :], ALU.mult)\
                          .then_inc(s("o_div"), 1)
                        dve.wait_ge(s("o_div"), n + 1)
                        nc.vector.tensor_scalar(ON[:, n, :], ON[:, n, :], bqk[:, 2:3], None, ALU.add)\
                          .then_inc(s("o_ready"), 1)
                    for n in range(NB):
                        dve.wait_ge(s("projected"), n + 1)
                        nc.vector.scalar_tensor_tensor(out=X[:, n, :], in0=psum[:, 4 * n + 2, :],
                                                       scalar=bpa[:, 0:1], in1=X[:, n, :],
                                                       op0=ALU.add, op1=ALU.add).then_inc(s("x_new"), 1)
                    norm_dve(nc, dve, s, g, bufs)
                    for n in range(NB):
                        dve.wait_ge(s("y_new"), n + 1)
                        shift_dve(nc, s, g, n)
            s.close()


def ln_buffers(alloc):
    return {k: alloc("ln_" + k, [P, NB, T]) for k in ("centered", "squared", "sd", "recip")}


def norm_pe(nc, pe, s, g, b):
    psum, X, mean_w = g.psum, g.X, g.mean_w
    for n in range(NB):
        pe.wait_ge(s("x_new"), n + 1)
        nc.tensor.matmul(psum[:, 4 * n, :], mean_w, X[:, n, :], start=True, stop=True).then_inc(s("ln_mean"), 1)
    for n in range(NB):
        pe.wait_ge(s("ln_squared"), n + 1)
        nc.tensor.matmul(psum[:, 4 * n + 3, :], mean_w, b["squared"][:, n, :], start=True, stop=True)\
          .then_inc(s("ln_var"), 1)


def norm_act(nc, act, s, g, b):
    psum, eps = g.psum, g.eps
    for n in range(NB):
        act.wait_ge(s("ln_centered"), n + 1)
        nc.scalar.activation(b["squared"][:, n, :], b["centered"][:, n, :], ACT.Square).then_inc(s("ln_squared"), 1)
    for n in range(NB):
        act.wait_ge(s("ln_var"), n + 1)
        nc.scalar.activation(b["sd"][:, n, :], psum[:, 4 * n + 3, :], ACT.Sqrt, bias=eps[:, 0:1])\
          .then_inc(s("ln_sd"), 1)


def norm_dve(nc, dve, s, g, b):
    psum, X, Y = g.psum, g.X, g.Y
    for n in range(NB):
        dve.wait_ge(s("ln_mean"), n + 1)
        nc.vector.tensor_tensor(b["centered"][:, n, :], X[:, n, :], psum[:, 4 * n, :], ALU.subtract)\
          .then_inc(s("ln_centered"), 1)
    for n in range(NB):
        dve.wait_ge(s("ln_sd"), n + 1)
        nc.vector.reciprocal(b["recip"][:, n, :], b["sd"][:, n, :]).then_inc(s("ln_recip"), 1)
        dve.wait_ge(s("ln_recip"), n + 1)
        nc.vector.tensor_tensor(Y[:, n, :], b["centered"][:, n, :], b["recip"][:, n, :], ALU.mult)\
          .then_inc(s("y_new"), 1)




def feed_forward_schedule():
    def each(stage, n, items):
        return [(stage, n, i) for i in items]

    plan = each("project", 0, range(6)) + [("ssq", 0, 0)] + each("project", 0, (6, 7)) + [("ssq", 0, 1)]
    plan += each("value", 0, range(4)) + [("norm", 0)] + each("project", 1, (0, 1))
    plan += each("spread", 0, (0, 1)) + [("project", 1, 2), ("scores", 0), ("spread", 0, 2)]
    plan += [("scores", 1), ("project", 1, 3), ("by_key", 0), ("spread", 0, 3)]
    plan += [("scores", 2), ("project", 1, 4), ("by_key", 1), ("project", 1, 5), ("sums", 0), ("divide", 0)]
    plan += [("scores", 3), ("ssq", 1, 0), ("project", 1, 6), ("project", 1, 7), ("ssq", 1, 1), ("norm", 1),
             ("by_key", 2), ("sums", 1), ("divide", 1)]
    plan += each("value", 1, range(4)) + [("spread", 1, 0), ("by_key", 3), ("spread", 1, 1), ("scores", 4),
                                          ("sums", 2), ("divide", 2)]
    plan += [("scores", 5), ("spread", 1, 2), ("by_key", 4), ("sums", 3), ("divide", 3)]
    plan += [("scores", 6), ("spread", 1, 3), ("by_key", 5), ("wo", 0), ("sums", 4), ("divide", 4)]
    plan += [("scores", 7), ("mean", 0), ("by_key", 6), ("sums", 5), ("var", 0), ("divide", 5)]
    plan += [("by_key", 7), ("scale", 0), ("sums", 6), ("divide", 6), ("sums", 7)] + each("w1", 0, (0, 1))
    plan += [("divide", 7), ("wo", 1), ("w1", 0, 2), ("mean", 1), ("w2", 0), ("var", 1), ("scale", 1)]
    plan += each("w1", 1, range(3)) + [("w2", 1)]
    return plan


def feed_forward(nc, g, layer, call):
    psum, Y, H, eps, cst, cstb = g.psum, g.Y, g.H, g.eps, g.cst, g.cstb
    wqkv, wo, w1, w2, b1, vecs, qks = g.wqkv, g.wo, g.w1, g.w2, g.b1, g.vecs, g.qks
    BLOCKS = 2 * PAIRS
    SQUARES = 6
    plan = feed_forward_schedule()

    order = []
    for stage, *i in plan:
        if stage == "project":
            order += [("main", *i), ("rot", *i)]
        elif stage == "ssq" and i[1] == 0:
            order += [("ssq", i[0])]
        elif stage in ("value", "wo", "mean", "var", "w2"):
            order += [(stage, *i)]
        elif stage == "spread":
            order += [("spread", i[0], 2 * i[1] + w) for w in range(2)]
        elif stage in ("scores", "by_key"):
            order += [(stage, *i, j, half) for j in range(2) for half in range(2)]
        elif stage == "sums":
            order += [("den", *i), ("num", *i)]
        elif stage == "w1":
            order += [("gate", *i), ("up", *i)]
    at = {use: i for i, use in enumerate(order)}

    def bank(*use):
        return at[use] % BANKS

    def last_read(use):
        kind, *i = use
        if kind in ("main", "rot"):
            return "rotated", BLOCKS * i[0] + i[1] + 1
        if kind == "value":
            return "v_copied", 4 * i[0] + i[1] + 1
        if kind == "spread":
            return "qk_ready", BLOCKS * i[0] + i[1] + 1
        if kind in ("scores", "by_key"):
            return "maxed" if kind == "scores" else "exped", 4 * i[0] + 2 * i[1] + i[2] + 1
        if kind in ("gate", "up"):
            return "hidden", 3 * i[0] + i[1] + 1
        return {"ssq": "sd", "den": "den_refined", "num": "o_ready", "wo": "y_mid", "mean": "ln_centered",
                "var": "ln_sd", "w2": "y_new"}[kind], i[0] + 1

    with ExitStack() as ctx:
        def sb(name, shape, dt=F32):
            return ctx.enter_context(nc.sbuf_tensor(f"f{call}_{name}", shape, dt))

        WR = sb("WR", [P, 2 * T])
        QZ = sb("QZ", [P, NB, HW, T])
        QB = sb("QB", [P, NB, HW, T], BF16)
        K = sb("K", [P, NB, PAIRS, T])
        KB = sb("KB", [P, NB, PAIRS, WIN + T], BF16)
        V = sb("V", [P, NB, 4, T])
        O = sb("O", [P, NB, PAIRS, T])
        SQ = sb("SQ", [P, SQUARES, T])
        R = sb("R", [P, T])
        RH = sb("RH", [P, T], F32R)
        RL = sb("RL", [P, T], F32R)
        MIX = sb("MIX", [P, 2, 2, T])
        PT = sb("PT", [P, 4, 4 * SPAN])
        M = sb("M", [P, 4, 4])
        D = sb("D", [P, 4, 4, P], BF16)
        RD = sb("RD", [P, 2, T])

        def centered(n):
            return K[:, n, 0, :]

        def ln_squared(n):
            return K[:, n, 1, :]

        def ln_sd(n):
            return K[:, n, 2, :]

        def hidden(n, part, blk):
            return QZ[:, n, 3 * part + blk, :]

        s = Phase(nc, f"f{call}")
        block = nc.Block()
        with block:
            @block.sync
            def _(sp):
                loads = g.load_layer(sp, layer, s("weights"))
                assert loads == g.LATE_WEIGHTS
                sp.wait_ge(s("value"), 4 * NB)
                sp.wait_ge(s("swapped"), 1)
                sp.wait_ge(s("rotated"), BLOCKS * NB)
                pieces = g.layer_attention_weights(1 - layer)
                for dst, src in pieces:
                    sp.dma_start(dst, src).then_inc(s("next_layer"), 16)
                sp.wait_ge(s("next_layer"), 16 * len(pieces))

            @block.gpsimd
            def _(pool):
                for n in range(NB):
                    for j in range(2):
                        other = slice(DW * (1 - j), DW * (1 - j) + DW)
                        nc.gpsimd.memset(QZ[other, n, j:HW:2, :], 0.0).then_inc(s("zeroed"), 1)
                        pool.wait_ge(s("zeroed"), 3 * n + j + 1)
                    nc.gpsimd.memset(KB[:, n, :, 0:WIN], 0.0).then_inc(s("zeroed"), 1)
                    pool.wait_ge(s("zeroed"), 3 * n + 3)
                for stage, *i in plan:
                    if stage == "project":
                        n, b = i
                        pool.wait_ge(s("rotated"), BLOCKS * n + b + 1)
                        dst = K[:, n, b // 2, :] if b % 2 else O[:, n, b // 2, :]
                        nc.gpsimd.tensor_tensor(dst, MIX[:, b % 2, 0, :], MIX[:, b % 2, 1, :], ALU.add)\
                          .then_inc(s("rotation_added"), 1)
                    elif stage == "scores":
                        for j in range(2):
                            head = 2 * i[0] + j
                            pool.wait_ge(s("maxed"), 2 * head + 2)
                            if head >= 4:
                                pool.wait_ge(s("by_key"), 2 * (head - 4) + 2)
                            nc.gpsimd.tensor_tensor(
                                D[:, head % 4, :, :],
                                cstb("ident")[:, None, :].to_broadcast([P, 4, P]),
                                M[:, head % 4, :, None].to_broadcast([P, 4, P]), ALU.mult).then_inc(s("diag"), 1)

            @block.tensor
            def _(pe):
                def take(*use):
                    i = at[use]
                    if i >= BANKS:
                        name, value = last_read(order[i - BANKS])
                        pe.wait_ge(s(name), value)
                    return psum[:, i % BANKS, :]

                def project(n, b):
                    col = P * (PAIRS * (b % 2) + b // 2)
                    nc.tensor.matmul(take("main", n, b), wqkv[:, col:col + P], H[:, n, :],
                                     start=True, stop=True).then_inc(s("main"), 1)
                    if n == 0 and b == 0:
                        pe.wait_ge(s("swapped"), 1)
                    nc.tensor.matmul(take("rot", n, b), WR[:, col:col + P], H[:, n, :],
                                     start=True, stop=True).then_inc(s("rot"), 1)

                def ssq(n, part):
                    if part == 0:
                        take("ssq", n)
                        blocks = range(0, SQUARES)
                    else:
                        blocks = range(SQUARES, BLOCKS)
                    dst = psum[:, bank("ssq", n), :]
                    pe.wait_ge(s("squared"), BLOCKS * n + blocks[-1] + 1)
                    for w in range(2):
                        for b in blocks:
                            if b % 2 == w:
                                c = b // 2
                                last = nc.tensor.matmul(dst[32 * c:32 * c + 32, :], cst("head_sum", 32 * w, 32),
                                                        SQ[:, b % SQUARES, :], start=(w == 0), stop=(w == 1))
                    last.then_inc(s("ssq"), 1)

                def value(n, t):
                    nc.tensor.matmul(take("value", n, t), H[:, n, P * t:P * t + P], wqkv[:, 2 * T:3 * T],
                                     start=True, stop=True).then_inc(s("value"), 1)

                def spread(n, c):
                    pe.wait_ge(s("norm_split"), n + 1)
                    for w in range(2):
                        dst = take("spread", n, 2 * c + w)
                        rows = g.spread_w[:, P * (2 * c + w):P * (2 * c + w) + P]
                        nc.tensor.matmul(dst, rows, RH[:, :], start=True, stop=False)
                        nc.tensor.matmul(dst, rows, RL[:, :], start=False, stop=True).then_inc(s("spread"), 1)

                def scores(i):
                    n, c = i // PAIRS, i % PAIRS
                    pe.wait_ge(s("cast"), BLOCKS * n + 2 * c + 2)
                    for j in range(2):
                        for half in range(2):
                            dst = take("scores", i, j, half)
                            for k in range(2):
                                tile = 2 * half + k
                                part = dst[:, SPAN * k:SPAN * k + SPAN]
                                nc.tensor.matmul(part, QB[:, n, 2 * c + j, P * tile:P * tile + P],
                                                 KB[:, n, c, P * tile:P * tile + SPAN], start=True, stop=False)
                                last = nc.tensor.matmul(part, cstb("ident"), cstb("mask_q" if tile else "mask_first"),
                                                        start=False, stop=True)
                            last.then_inc(s("scores"), 1)

                def by_key(i):
                    n, c = i // PAIRS, i % PAIRS
                    for j in range(2):
                        head = 2 * i + j
                        pe.wait_ge(s("diag"), head + 1)
                        for half in range(2):
                            dst = take("by_key", i, j, half)
                            for k in range(2):
                                tile = 2 * half + k
                                width = min(SPAN, T - P * tile)
                                part = dst[:, SPAN * k:SPAN * k + width]
                                nc.tensor.matmul(part, K[:, n, c, P * tile:P * tile + P],
                                                 QZ[:, n, 2 * c + j, P * tile:P * tile + width],
                                                 start=True, stop=False)
                                nc.tensor.matmul(part, cstb("ident"), cstb("mask_k", 0, width),
                                                 start=False, stop=False)
                                diag = D[:, head % 4, :, :].rearrange("p a b -> p (a b)")
                                last = nc.tensor.matmul(part, cstb("minus1"), diag[:, P * tile:P * tile + width],
                                                        start=False, stop=True)
                            last.then_inc(s("by_key"), 1)

                def sums(i):
                    n, c = i // PAIRS, i % PAIRS
                    pe.wait_ge(s("exped"), 4 * i + 4)
                    for kind in ("den", "num"):
                        dst = take(kind, i)
                        for tile in range(4):
                            width = min(SPAN, T - P * tile)
                            for j in range(2):
                                weights = (V[:, n, tile, DW * (2 * c + j):DW * (2 * c + j) + DW] if kind == "num"
                                           else cst("ones"))
                                last = nc.tensor.matmul(
                                    dst[DW * j:DW * j + DW, P * tile:P * tile + width], weights,
                                    PT[:, (2 * i + j) % 4, SPAN * tile:SPAN * tile + width],
                                    start=(tile == 0), stop=(tile == 3), skip_group_check=True)
                        last.then_inc(s(kind), 1)

                for stage, *i in plan:
                    if stage == "project":
                        project(*i)
                    elif stage == "ssq":
                        ssq(*i)
                    elif stage == "value":
                        value(*i)
                    elif stage == "spread":
                        spread(*i)
                    elif stage == "scores":
                        scores(*i)
                    elif stage == "by_key":
                        by_key(*i)
                    elif stage == "sums":
                        sums(*i)
                    elif stage == "wo":
                        n = i[0]
                        pe.wait_ge(s("weights"), g.LATE_WEIGHTS)
                        pe.wait_ge(s("o_ready"), PAIRS * (n + 1))
                        dst = take("wo", n)
                        for c in range(PAIRS):
                            last = nc.tensor.matmul(dst, wo[:, c, :], O[:, n, c, :], start=(c == 0),
                                                    stop=(c == PAIRS - 1))
                        last.then_inc(s("wo"), 1)
                    elif stage == "mean":
                        n = i[0]
                        pe.wait_ge(s("shifted"), n + 1)
                        nc.tensor.matmul(take("mean", n), g.mean_w, H[:, n, :], start=True, stop=True)\
                          .then_inc(s("mean"), 1)
                    elif stage == "var":
                        n = i[0]
                        pe.wait_ge(s("ln_squared"), n + 1)
                        nc.tensor.matmul(take("var", n), g.mean_w, ln_squared(n), start=True, stop=True)\
                          .then_inc(s("var"), 1)
                    elif stage == "w1":
                        n, blk = i
                        lo, w = HID_BLOCKS[blk]
                        pe.wait_ge(s("ln_done"), n + 1)
                        for kind, first in (("gate", HID), ("up", 0)):
                            nc.tensor.matmul(take(kind, n, blk)[0:w, :], w1[:, first + lo:first + lo + w],
                                             H[:, n, :], start=True, stop=True).then_inc(s(kind), 1)
                    elif stage == "w2":
                        n = i[0]
                        dst = take("w2", n)
                        for blk, (lo, w) in enumerate(HID_BLOCKS):
                            pe.wait_ge(s("hidden"), 3 * n + blk + 1)
                            last = nc.tensor.matmul(dst, w2[0:w, blk, :], hidden(n, 1, blk)[0:w, :],
                                                    start=(blk == 0), stop=(blk == 2))
                        last.then_inc(s("w2"), 1)

            @block.scalar
            def _(act):
                for stage, *i in plan:
                    if stage == "project":
                        n, b = i
                        act.wait_ge(s("main"), BLOCKS * n + b + 1)
                        if n or b >= SQUARES:
                            act.wait_ge(s("ssq"), 2 * n + 1 if b >= SQUARES else 2 * n)
                        nc.scalar.activation(SQ[:, b % SQUARES, :], psum[:, bank("main", n, b), :], ACT.Square)\
                          .then_inc(s("squared"), 1)
                    elif stage == "ssq" and i[1] == 1:
                        n = i[0]
                        act.wait_ge(s("ssq"), 2 * n + 2)
                        if n:
                            act.wait_ge(s("norm_split"), n)
                        nc.scalar.activation(R[:, :], psum[:, bank("ssq", n), :], ACT.Sqrt).then_inc(s("sd"), 1)
                        nc.scalar.preload_act_table_set(EXP_AND_LN)
                    elif stage == "value":
                        n, t = i
                        act.wait_ge(s("value"), 4 * n + t + 1)
                        nc.scalar.activation(V[:, n, t, :], psum[:, bank("value", n, t), :], ACT.Copy)\
                          .then_inc(s("v_copied"), 1)
                    elif stage == "by_key":
                        i = i[0]
                        for j in range(2):
                            if i >= 2:
                                act.wait_ge(s("num"), i - 1)
                            for half in range(2):
                                act.wait_ge(s("by_key"), 4 * i + 2 * j + half + 1)
                                width = SPAN + min(SPAN, T - P * (2 * half + 1))
                                nc.scalar.activation(
                                    PT[:, (2 * i + j) % 4, 2 * SPAN * half:2 * SPAN * half + width],
                                    psum[:, bank("by_key", i, j, half), 0:width], ACT.Exp, scale=8.0)\
                                  .then_inc(s("exped"), 1)
                    elif stage == "sums":
                        i = i[0]
                        act.wait_ge(s("den"), i + 1)
                        if i >= 2:
                            act.wait_ge(s("o_ready"), i - 1)
                        nc.scalar.activation(RD[:, i % 2, :], psum[:, bank("den", i), :], ACT.Ln)\
                          .then_inc(s("den_log"), 1)
                        act.wait_ge(s("den_log"), i + 1)
                        nc.scalar.activation(RD[:, i % 2, :], RD[:, i % 2, :], ACT.Exp, scale=-1.0)\
                          .then_inc(s("den_recip"), 1)
                    elif stage == "mean":
                        n = i[0]
                        act.wait_ge(s("ln_centered"), n + 1)
                        nc.scalar.activation(ln_squared(n), centered(n), ACT.Square).then_inc(s("ln_squared"), 1)
                    elif stage == "var":
                        n = i[0]
                        act.wait_ge(s("var"), n + 1)
                        nc.scalar.activation(ln_sd(n), psum[:, bank("var", n), :], ACT.Sqrt,
                                             bias=eps[:, 0:1]).then_inc(s("ln_sd"), 1)
                        if n == 0:
                            nc.scalar.preload_act_table_set(EXP_AND_LN)
                    elif stage == "w1":
                        n, blk = i
                        w = HID_BLOCKS[blk][1]
                        act.wait_ge(s("weights"), g.LATE_WEIGHTS)
                        act.wait_ge(s("gate"), 3 * n + blk + 1)
                        nc.scalar.activation(hidden(n, 0, blk)[0:w, :], psum[0:w, bank("gate", n, blk), :],
                                             ACT.Gelu, bias=b1[0:w, 3 + blk:4 + blk]).then_inc(s("gated"), 1)

            @block.vector
            def _(dve):
                heads = wqkv[:, 0:2 * T].rearrange("p (h s d) -> p h s d", s=2, d=DW // 2)
                swapped = WR[:, :].rearrange("p (h s d) -> p h s d", s=2, d=DW // 2)
                for part in range(2):
                    last = nc.vector.tensor_copy(swapped[:, :, part, :], heads[:, :, 1 - part, :])
                last.then_inc(s("swapped"), 1)

                def rotate(n, b):
                    i, w = BLOCKS * n + b, b % 2
                    if i >= 2:
                        dve.wait_ge(s("rotation_added"), i - 1)
                    dve.wait_ge(s("squared"), i + 1)
                    nc.vector.scalar_tensor_tensor(
                        out=MIX[:, b % 2, 0, :], in0=psum[:, bank("main", n, b), :], scalar=qks[:, w:w + 1],
                        in1=cst("cosk" if w else "cosq"), op0=ALU.mult, op1=ALU.mult)
                    dve.wait_ge(s("rot"), i + 1)
                    nc.vector.scalar_tensor_tensor(
                        out=MIX[:, b % 2, 1, :], in0=psum[:, bank("rot", n, b), :], scalar=qks[:, w + 2:w + 3],
                        in1=cst("sink" if w else "sinq"), op0=ALU.mult, op1=ALU.mult).then_inc(s("rotated"), 1)

                def norm(n):
                    dve.wait_ge(s("sd"), n + 1)
                    nc.vector.tensor_scalar(R[:, :], R[:, :], 1e-12, None, ALU.max).then_inc(s("clipped"), 1)
                    dve.wait_ge(s("clipped"), n + 1)
                    nc.vector.reciprocal(R[:, :], R[:, :]).then_inc(s("norm_recip"), 1)
                    dve.wait_ge(s("norm_recip"), n + 1)
                    if n:
                        dve.wait_ge(s("spread"), BLOCKS * n)
                    nc.vector.tensor_copy(RH[:, :], R[:, :]).then_inc(s("norm_high"), 1)
                    dve.wait_ge(s("norm_high"), n + 1)
                    nc.vector.tensor_tensor(RL[:, :], R[:, :], RH[:, :].bitcast(F32), ALU.subtract)\
                      .then_inc(s("norm_split"), 1)

                def normalise(n, c):
                    for w in range(2):
                        i = BLOCKS * n + 2 * c + w
                        dve.wait_ge(s("spread"), i + 1)
                        dve.wait_ge(s("rotation_added"), i + 1)
                        if i == 0:
                            dve.wait_ge(s("zeroed"), 3 * NB)
                        r = psum[:, bank("spread", n, 2 * c + w), :]
                        if w == 0:
                            nc.vector.tensor_tensor(QZ[0:DW, n, 2 * c, :], O[0:DW, n, c, :], r[0:DW, :], ALU.mult)
                            nc.vector.tensor_tensor(QZ[DW:P, n, 2 * c + 1, :], O[DW:P, n, c, :], r[DW:P, :],
                                                    ALU.mult).then_inc(s("qk_ready"), 1)
                            dve.wait_ge(s("qk_ready"), i + 1)
                            nc.vector.tensor_copy(QB[:, n, 2 * c:2 * c + 2, :], QZ[:, n, 2 * c:2 * c + 2, :])\
                              .then_inc(s("cast"), 1)
                        else:
                            nc.vector.tensor_tensor(K[:, n, c, :], K[:, n, c, :], r, ALU.mult)\
                              .then_inc(s("qk_ready"), 1)
                            dve.wait_ge(s("qk_ready"), i + 1)
                            nc.vector.tensor_copy(KB[:, n, c, WIN:WIN + T], K[:, n, c, :]).then_inc(s("cast"), 1)

                def maxima(i):
                    for j in range(2):
                        head = 2 * i + j
                        if head >= 4:
                            dve.wait_ge(s("diag"), head - 3)
                        for half in range(2):
                            dve.wait_ge(s("scores"), 2 * head + half + 1)
                            nc.vector.tensor_reduce(
                                M[:, head % 4, 2 * half:2 * half + 2],
                                psum[:, bank("scores", i, j, half), 0:2 * SPAN].rearrange("p (k x) -> p k x", k=2),
                                AX_X, ALU.max).then_inc(s("maxed"), 1)

                def divide(i):
                    n, c = i // PAIRS, i % PAIRS
                    dve.wait_ge(s("den_recip"), i + 1)
                    nc.vector.tensor_tensor(O[:, n, c, :], psum[:, bank("den", i), :], RD[:, i % 2, :],
                                            ALU.mult).then_inc(s("den_refined"), 1)
                    dve.wait_ge(s("den_refined"), i + 1)
                    nc.vector.scalar_tensor_tensor(out=RD[:, i % 2, :], in0=O[:, n, c, :], scalar=-2.0,
                                                   in1=RD[:, i % 2, :], op0=ALU.add, op1=ALU.mult)\
                      .then_inc(s("minus_recip"), 1)
                    dve.wait_ge(s("minus_recip"), i + 1)
                    dve.wait_ge(s("num"), i + 1)
                    nc.vector.tensor_tensor(O[:, n, c, :], psum[:, bank("num", i), :], RD[:, i % 2, :],
                                            ALU.mult).then_inc(s("o_ready"), 1)

                for stage, *i in plan:
                    if stage == "project":
                        rotate(*i)
                    elif stage == "norm":
                        norm(*i)
                    elif stage == "spread":
                        normalise(*i)
                    elif stage == "scores":
                        maxima(*i)
                    elif stage == "divide":
                        divide(*i)
                    elif stage == "wo":
                        n = i[0]
                        dve.wait_ge(s("wo"), n + 1)
                        nc.vector.tensor_tensor(Y[:, n, :], Y[:, n, :], psum[:, bank("wo", n), :], ALU.subtract)\
                          .then_inc(s("y_mid"), 1)
                        dve.wait_ge(s("y_mid"), n + 1)
                        shift_dve(nc, s, g, n)
                    elif stage == "mean":
                        n = i[0]
                        dve.wait_ge(s("mean"), n + 1)
                        nc.vector.tensor_tensor(centered(n), H[:, n, :], psum[:, bank("mean", n), :], ALU.subtract)\
                          .then_inc(s("ln_centered"), 1)
                    elif stage == "scale":
                        n = i[0]
                        dve.wait_ge(s("weights"), g.LATE_WEIGHTS)
                        dve.wait_ge(s("ln_sd"), n + 1)
                        nc.vector.reciprocal(ln_sd(n), ln_sd(n)).then_inc(s("ln_recip"), 1)
                        dve.wait_ge(s("ln_recip"), n + 1)
                        nc.vector.scalar_tensor_tensor(out=H[:, n, :], in0=centered(n), scalar=vecs[:, 0:1],
                                                       in1=ln_sd(n), op0=ALU.mult, op1=ALU.mult)\
                          .then_inc(s("ln_scaled"), 1)
                        dve.wait_ge(s("ln_scaled"), n + 1)
                        nc.vector.tensor_scalar(H[:, n, :], H[:, n, :], vecs[:, 1:2], None, ALU.add)\
                          .then_inc(s("ln_done"), 1)
                    elif stage == "w1":
                        n, blk = i
                        w = HID_BLOCKS[blk][1]
                        dve.wait_ge(s("up"), 3 * n + blk + 1)
                        dve.wait_ge(s("gated"), 3 * n + blk + 1)
                        nc.vector.scalar_tensor_tensor(
                            out=hidden(n, 1, blk)[0:w, :], in0=psum[0:w, bank("up", n, blk), :],
                            scalar=b1[0:w, blk:blk + 1], in1=hidden(n, 0, blk)[0:w, :],
                            op0=ALU.add, op1=ALU.mult).then_inc(s("hidden"), 1)
                    elif stage == "w2":
                        n = i[0]
                        dve.wait_ge(s("w2"), n + 1)
                        nc.vector.scalar_tensor_tensor(out=Y[:, n, :], in0=psum[:, bank("w2", n), :],
                                                       scalar=vecs[:, 2:3], in1=Y[:, n, :],
                                                       op0=ALU.add, op1=ALU.add).then_inc(s("y_new"), 1)
                        dve.wait_ge(s("y_new"), n + 1)
                        shift_dve(nc, s, g, n)
        s.close()


def attention_b(nc, g):
    psum, X, Y, cst = g.psum, g.X, g.Y, g.cst
    with ExitStack() as ctx:
        def sb(name, shape, dt=F32):
            return ctx.enter_context(nc.sbuf_tensor("b_" + name, shape, dt))

        first = ln_buffers(lambda name, *rest: sb("1" + name, *rest))
        second = ln_buffers(lambda name, *rest: sb("2" + name, *rest))
        Q = sb("Q", [P, NB, T])
        NEG = sb("NEG", [P, NB, T])
        E = sb("E", [P, NB, T])
        LAT = sb("LAT", [33, NB, T])
        KT = sb("KT", [P, NB, 4, P])
        NEGK = sb("NEGK", [P, NB, 4, P])
        EK = sb("EK", [P, NB, 4, P])
        VT = sb("VT", [P, NB, 4, 2 * P])
        CTX = sb("CTX", [P, NB, 2 * P])
        DEN = sb("DEN", [P, NB, T])
        ON = sb("ON", [P, NB, T])
        s = Phase(nc, "b1")
        block = nc.Block()
        with block:
            @block.gpsimd
            def _(pool):
                for n in range(NB):
                    nc.gpsimd.memset(LAT[32:33, n, :], 1.0).then_inc(s("ones"), 1)
                    pool.wait_ge(s("ones"), 2 * n + 1)
                    nc.gpsimd.memset(VT[:, n, :, P:2 * P], 1.0).then_inc(s("ones"), 1)
                    pool.wait_ge(s("ones"), 2 * n + 2)

            @block.tensor
            def _(pe):
                norm_pe(nc, pe, s, g, first)
                for n in range(NB):
                    pe.wait_ge(s("y_new"), n + 1)
                    nc.tensor.matmul(psum[:, 4 * n, :], g.wq_b[:, :], Y[:, n, :], start=True, stop=True)\
                      .then_inc(s("q"), 1)
                    nc.tensor.matmul(psum[0:32, 4 * n + 1, :], g.wd_b[:, :], Y[:, n, :], start=True, stop=True)\
                      .then_inc(s("latent"), 1)
                pe.wait_ge(s("ones"), 2 * NB)
                for n in range(NB):
                    pe.wait_ge(s("latent_ready"), n + 1)
                    for t in range(4):
                        last = nc.tensor.matmul(psum[:, 4 * n + 2 + t // 2, 256 * (t % 2):256 * (t % 2) + 256],
                                                LAT[:, n, P * t:P * t + P], g.wu_b[:, :], start=True, stop=True)
                        if t % 2:
                            last.then_inc(s("kv"), 1)
                for n in range(NB):
                    pe.wait_ge(s("k_ready"), 2 * n + 2)
                    pe.wait_ge(s("v_ready"), 2 * n + 2)
                    pe.wait_ge(s("q_ready"), n + 1)
                    for t in range(4):
                        last = nc.tensor.matmul(psum[:, 4 * n, 0:2 * P], KT[:, n, t, :], VT[:, n, t, :],
                                                start=(t == 0), stop=(t == 3))
                    last.then_inc(s("context"), 1)
                for n in range(NB):
                    pe.wait_ge(s("context_ready"), n + 1)
                    nc.tensor.matmul(psum[:, 4 * n + 2, :], CTX[:, n, P:2 * P], Q[:, n, :], start=True, stop=True)\
                      .then_inc(s("den"), 1)
                    nc.tensor.matmul(psum[:, 4 * n + 1, :], CTX[:, n, 0:P], Q[:, n, :], start=True, stop=True)\
                      .then_inc(s("num"), 1)
                for n in range(NB):
                    pe.wait_ge(s("o_ready"), n + 1)
                    nc.tensor.matmul(psum[:, 4 * n, :], g.wo_b[:, :], ON[:, n, :], start=True, stop=True)\
                      .then_inc(s("projected"), 1)

            @block.scalar
            def _(act):
                norm_act(nc, act, s, g, first)
                for n in range(NB):
                    act.wait_ge(s("latent"), n + 1)
                    nc.scalar.activation(LAT[0:32, n, :], psum[0:32, 4 * n + 1, :], ACT.Identity,
                                         bias=g.bd_b[:, 0:1]).then_inc(s("latent_ready"), 1)
                for n in range(NB):
                    act.wait_ge(s("q_neg"), n + 1)
                    nc.scalar.activation(E[:, n, :], NEG[:, n, :], ACT.Exp).then_inc(s("q_exp"), 1)
                for n in range(NB):
                    for half in range(2):
                        i = 2 * n + half
                        act.wait_ge(s("k_neg"), i + 1)
                        pair_ = psum[:, 4 * n + 2 + half, :].rearrange("p (t x) -> p t x", t=2)
                        nc.scalar.activation(VT[:, n, 2 * half:2 * half + 2, 0:P], pair_[:, :, P:2 * P],
                                             ACT.Copy).then_inc(s("v_ready"), 1)
                        nc.scalar.activation(EK[:, n, 2 * half:2 * half + 2, :],
                                             NEGK[:, n, 2 * half:2 * half + 2, :], ACT.Exp)\
                          .then_inc(s("k_exp"), 1)

            @block.vector
            def _(dve):
                for n in range(NB):
                    nc.vector.tensor_tensor(X[:, n, :], X[:, n, :], Y[:, n, :], ALU.add).then_inc(s("x_new"), 1)
                dve.wait_ge(s("x_new"), NB)
                norm_dve(nc, dve, s, g, first)
                for n in range(NB):
                    dve.wait_ge(s("q"), n + 1)
                    nc.vector.tensor_scalar(NEG[:, n, :], psum[:, 4 * n, :], g.bq_b[:, 0:1], 0.0,
                                            ALU.add, ALU.min).then_inc(s("q_neg"), 1)
                    nc.vector.tensor_scalar(Q[:, n, :], psum[:, 4 * n, :], g.bq_b[:, 0:1], 0.0,
                                            ALU.add, ALU.max).then_inc(s("q_pos"), 1)
                    dve.wait_ge(s("q_pos"), n + 1)
                    dve.wait_ge(s("q_exp"), n + 1)
                    nc.vector.tensor_tensor(Q[:, n, :], Q[:, n, :], E[:, n, :], ALU.add).then_inc(s("q_ready"), 1)
                for n in range(NB):
                    for half in range(2):
                        i = 2 * n + half
                        dve.wait_ge(s("kv"), i + 1)
                        pair_ = psum[:, 4 * n + 2 + half, :].rearrange("p (t x) -> p t x", t=2)
                        nc.vector.tensor_scalar(NEGK[:, n, 2 * half:2 * half + 2, :], pair_[:, :, 0:P], 0.0, None,
                                                ALU.min).then_inc(s("k_neg"), 1)
                    for half in range(2):
                        i = 2 * n + half
                        pair_ = psum[:, 4 * n + 2 + half, :].rearrange("p (t x) -> p t x", t=2)
                        dve.wait_ge(s("k_exp"), i + 1)
                        nc.vector.scalar_tensor_tensor(out=KT[:, n, 2 * half:2 * half + 2, :],
                                                       in0=pair_[:, :, 0:P], scalar=0.0,
                                                       in1=EK[:, n, 2 * half:2 * half + 2, :],
                                                       op0=ALU.max, op1=ALU.add).then_inc(s("k_ready"), 1)
                for n in range(NB):
                    dve.wait_ge(s("context"), n + 1)
                    nc.vector.tensor_tensor(CTX[:, n, :], psum[:, 4 * n, 0:2 * P], cst("block8"), ALU.mult)\
                      .then_inc(s("context_ready"), 1)
                for n in range(NB):
                    dve.wait_ge(s("den"), n + 1)
                    nc.vector.tensor_scalar(DEN[:, n, :], psum[:, 4 * n + 2, :], 1e-6, None, ALU.add)\
                      .then_inc(s("den_ready"), 1)
                    dve.wait_ge(s("den_ready"), n + 1)
                    nc.vector.reciprocal(DEN[:, n, :], DEN[:, n, :]).then_inc(s("den_recip"), 1)
                    dve.wait_ge(s("den_recip"), n + 1)
                    dve.wait_ge(s("num"), n + 1)
                    nc.vector.tensor_tensor(ON[:, n, :], psum[:, 4 * n + 1, :], DEN[:, n, :], ALU.mult)\
                      .then_inc(s("o_ready"), 1)
                for n in range(NB):
                    dve.wait_ge(s("projected"), n + 1)
                    nc.vector.scalar_tensor_tensor(out=X[:, n, :], in0=psum[:, 4 * n, :], scalar=g.bo_b[:, 0:1],
                                                   in1=X[:, n, :], op0=ALU.add, op1=ALU.add).then_inc(s("x_out"), 1)
        s.close()
        s = Phase(nc, "b2")
        block = nc.Block()
        with block:
            @block.tensor
            def _(pe):
                norm_pe(nc, pe, s, g, second)

            @block.scalar
            def _(act):
                norm_act(nc, act, s, g, second)

            @block.vector
            def _(dve):
                for n in range(NB):
                    nc.vector.engine_nop().then_inc(s("x_new"), 1)
                norm_dve(nc, dve, s, g, second)
                for n in range(NB):
                    dve.wait_ge(s("y_new"), n + 1)
                    shift_dve(nc, s, g, n)
        s.close()


def store(nc, g, out, pair):
    psum, X, Y = g.psum, g.X, g.Y
    with ExitStack() as ctx:
        OUT = ctx.enter_context(nc.sbuf_tensor("OUT", [P, NB, 4, P], F32))
        s = Phase(nc, "out")
        block = nc.Block()
        with block:
            @block.vector
            def _(dve):
                for n in range(NB):
                    nc.vector.tensor_tensor(X[:, n, :], X[:, n, :], Y[:, n, :], ALU.add).then_inc(s("x_new"), 1)

            @block.tensor
            def _(pe):
                for n in range(NB):
                    pe.wait_ge(s("x_new"), n + 1)
                    for t in range(4):
                        last = nc.tensor.transpose(psum[:, n, P * t:P * t + P], X[:, n, P * t:P * t + P], g.ident)
                    last.then_inc(s("turned"), 1)

            @block.scalar
            def _(act):
                for n in range(NB):
                    act.wait_ge(s("turned"), n + 1)
                    nc.scalar.activation(OUT[:, n, :, :].rearrange("p t d -> p (t d)"), psum[:, n, :], ACT.Copy)\
                      .then_inc(s("copied"), 1)

            @block.sync
            def _(sp):
                for n in range(NB):
                    sp.wait_ge(s("copied"), n + 1)
                    dst = out[bass.ds(pair * NB + n, 1)].rearrange("a (t p) d -> p (a t) d", p=P)
                    sp.dma_start(dst, OUT[:, n, :, :]).then_inc(s("stored"), 16)
                sp.wait_ge(s("stored"), 16 * NB)
        s.close()


def kernel(**inputs):
    import concourse.bacc as bacc
    from concourse.bass_utils import run_bass_kernel_spmd

    nc = bacc.Bacc("TRN2", target_bir_lowering=False, num_devices=1)
    arrays = {name: np.ascontiguousarray(a) for name, a in inputs.items()}
    c, b = constants()
    arrays["const"] = c
    arrays["constb"] = b
    args = {name: nc.dram_tensor(name + "_dram", a.shape, mybir.dt.from_np(a.dtype), kind="ExternalInput").ap()
            for name, a in arrays.items()}
    shape = inputs["L0_attn_a_x"].shape
    out = nc.dram_tensor("out_dram", shape, F32, kind="ExternalOutput").ap()
    build(nc, args, out)
    r = run_bass_kernel_spmd(nc, [{name + "_dram": a for name, a in arrays.items()}], core_ids=[0])
    return r.results[0]["out_dram"]
```

```python
from contextlib import ExitStack

import numpy as np

import concourse.bass as bass
from concourse import mybir

F32 = mybir.dt.float32
F32R = mybir.dt.float32r
BF16 = mybir.dt.bfloat16
ACT = mybir.ActivationFunctionType
ALU = mybir.AluOpType
AX_X = mybir.AxisListType.X

P = 128
T = 512
NB = 2
BANKS = 8

HA, DA = 16, 8
RUNS = [(0, 2), (0, 1), (0, 0), (1, 2), (2, 2)]
SLOTS = 9
ROWS = 2
VCOLS = 12
GUARD_ROW = SLOTS * DA
LAG = 3
HW, DW, WIN = 8, 64, 64
PAIRS = HW // 2
SPAN = P + WIN
HID = 341
HID_BLOCKS = [(0, 128), (128, 128), (256, HID - 256)]
MASKED = -1e30
LN_EPS = 1e-5
EXP_AND_LN, SQRT, GELU = "natural_log_exp_and_others", "sqrt_and_others", "gelu_and_others"

_WIDTHS = [("ident", P), ("center", P), ("mean", 1), ("head_sum", 64), ("block8", P + HA), ("ones", P),
           ("cosq", T), ("sinq", T), ("cosk", T), ("sink", T)]
CONST = {}
_at = 0
for _name, _w in _WIDTHS:
    CONST[_name] = (_at, _at + _w)
    _at += _w
CONST_COLS = _at
TABLES = CONST["cosq"][0]
CONSTB = {"ident": (0, P), "minus1": (P, 2 * P), "mask_first": (2 * P, 2 * P + SPAN),
          "mask_q": (2 * P + SPAN, 2 * P + 2 * SPAN), "mask_k": (2 * P + 2 * SPAN, 2 * P + 3 * SPAN)}
CONSTB_COLS = 2 * P + 3 * SPAN
SPREAD_COLS = 8 * P


def constants():
    c = np.zeros((P, CONST_COLS), np.float32)

    def col(name):
        a, b = CONST[name]
        return c[:, a:b]

    r = np.arange(P)
    col("ident")[:] = np.eye(P)
    col("mean")[:] = 1.0 / P
    col("center")[:] = np.eye(P) - 1.0 / P
    half = np.arange(0, DW, 2, dtype=np.float32)
    inv_freq = (1.0 / np.float32(10000.0) ** (half / DW)).astype(np.float32)
    t = np.arange(T, dtype=np.float32)
    freqs = t[:, None] * inv_freq[None, :]
    base = (half + np.float32(0.4 * DW)) / np.float32(1.4 * DW)
    scale = base[None, :] ** ((t - T // 2) / np.float32(WIN // 2))[:, None]
    freqs, scale = (np.concatenate([a, a], -1).T for a in (freqs, scale))
    cos, sin = np.cos(freqs), np.sin(freqs)
    sin = sin * np.where(np.arange(DW) < DW // 2, -1, 1)[:, None]
    for name, table in (("cosq", cos * scale), ("sinq", sin * scale), ("cosk", cos / scale), ("sink", sin / scale)):
        col(name)[:] = np.concatenate([table, table], 0)
    col("head_sum")[:] = np.concatenate([(r[:, None] // DW + 2 * w) == (np.arange(32)[None, :] // 8)
                                         for w in range(2)], 1)
    col("block8")[:] = np.concatenate([(r[:, None] // DA) == (r[None, :] // DA),
                                       (r[:, None] // DA) == np.arange(HA)[None, :]], 1)
    col("ones")[:] = 1
    b = np.zeros((P, CONSTB_COLS + SPREAD_COLS), np.float32)
    for i in range(16):
        b[8 * i, CONSTB_COLS + DW * i:CONSTB_COLS + DW * i + DW] = 1
    b[:, 0:P] = np.eye(P)
    b[:, P:2 * P] = -1
    x = np.arange(SPAN)[None, :]
    far = r[:, None] + WIN - x
    b[:, 2 * P:2 * P + SPAN] = np.where((far >= 0) & (far <= WIN) & (x >= WIN), 0, MASKED)
    b[:, 2 * P + SPAN:2 * P + 2 * SPAN] = np.where((far >= 0) & (far <= WIN), 0, MASKED)
    far = x - r[:, None]
    b[:, 2 * P + 2 * SPAN:CONSTB_COLS] = np.where((far >= 0) & (far <= WIN), 0, MASKED)
    return c, b


class Kept:
    pass


class Phase:

    def __init__(self, nc, label):
        self.nc, self.label, self.held, self.ctx = nc, label, {}, ExitStack()

    def __call__(self, name):
        if name not in self.held:
            self.held[name] = self.ctx.enter_context(self.nc.semaphore(f"{self.label}_{name}"))
        return self.held[name]

    def close(self):
        numbers = sorted(x.num for x in self.held.values())
        start = 0
        for i in range(1, len(numbers) + 1):
            if i == len(numbers) or numbers[i] != numbers[i - 1] + 1:
                self.nc.gpsimd.sem_clear(range(numbers[start], numbers[i - 1] + 1))
                start = i
        self.nc.all_engine_barrier(sem_only=True)
        self.ctx.close()


def build(nc, a, out):
    x_d = a["L0_attn_a_x"]
    B = x_d.shape[0]
    with ExitStack() as top:
        def sb(name, shape, dt=F32, ctx=top):
            return ctx.enter_context(nc.sbuf_tensor(name, shape, dt))

        psum = top.enter_context(nc.psum_tensor("psum", [P, BANKS, T], F32))
        const = sb("const", [P, CONST_COLS])
        constb = sb("constb", [P, CONSTB_COLS], BF16)
        spread_w = sb("spread_w", [P, SPREAD_COLS], F32R)
        X = sb("X", [P, NB, T])
        Y = sb("Y", [P, NB, T])
        HH = sb("HH", [P, NB, T], F32R)
        HL = sb("HL", [P, NB, T], F32R)
        eps = sb("eps", [P, 1])
        wa = sb("wa", [P, 3 * P])
        wpa = sb("wpa", [P, P])
        bqk = sb("bqk", [P, 3])
        bpa = sb("bpa", [P, 1])
        wq_b = sb("wq_b", [P, P])
        bq_b = sb("bq_b", [P, 1])
        wd_b = sb("wd_b", [P, 32])
        bd_b = sb("bd_b", [32, 1])
        wu_b = sb("wu_b", [33, 2 * P])
        wo_b = sb("wo_b", [P, P])
        bo_b = sb("bo_b", [P, 1])
        wqkv_h = sb("wqkv_h", [P, 3 * T], F32R)
        wqkv_l = sb("wqkv_l", [P, 3 * T], F32R)
        wo = sb("wo", [P, PAIRS, P])
        w1 = sb("w1", [P, 2 * HID])
        w2 = sb("w2", [P, 3, P])
        b1 = sb("b1", [P, 6])
        vecs = sb("vecs", [P, 3])
        qks = sb("qks", [P, 4])

        def cst(name, lo=0, n=None):
            s, e = CONST[name]
            return const[:, s + lo:e if n is None else s + lo + n]

        def cstb(name, lo=0, n=None):
            s, e = CONSTB[name]
            return constb[:, s + lo:e if n is None else s + lo + n]

        ident = cst("ident")

        def load_layer(sp, layer, sem):
            def row(name):
                return a[name][bass.ds(layer, 1)]
            n = 0
            for dst, src in (
                (wo[:, :, :], row("L0_ffn_wo").rearrange("a (c p) n -> p (a c) n", p=P)),
                (w1[:, :], row("L0_ffn_w1").rearrange("a p n -> (a p) n")),
                (w2[:, 0:2, :], row("L0_ffn_w2")[:, 0:256, :].rearrange("a (c p) n -> p (a c) n", p=P)),
                (w2[0:HID - 256, 2, :], row("L0_ffn_w2")[:, 256:HID, :].rearrange("a p n -> (a p) n")),
                *((b1[0:w, 3 * part + i:3 * part + i + 1],
                   row("L0_ffn_b1")[:, HID * part + lo:HID * part + lo + w].rearrange("a (p c) -> (a p) c", c=1))
                  for part in range(2) for i, (lo, w) in enumerate(HID_BLOCKS)),
                (vecs[:, 0:1], row("L0_ffn_ln_g").rearrange("a (p c) -> (a p) c", c=1)),
                (vecs[:, 1:2], row("L0_ffn_ln_b").rearrange("a (p c) -> (a p) c", c=1)),
                (vecs[:, 2:3], row("L0_ffn_b2").rearrange("a (p c) -> (a p) c", c=1)),
            ):
                sp.dma_start(dst, src).then_inc(sem, 16)
                n += 16
            return n

        def wqkv_of(layer):
            return a["L0_ffn_wqkv"][bass.ds(layer, 1)].rearrange("a p n -> (a p) n")

        def attention_scales(layer):
            def row(name):
                return a[name][bass.ds(layer, 1)]
            pieces = []
            for at, name in ((0, "L0_ffn_q_scale"), (1, "L0_ffn_k_scale")):
                v = row(name).rearrange("a (p c) -> (a p) c", c=1)
                for h in range(2):
                    pieces.append((qks[DW * h:DW * h + DW, at:at + 1], v))
                    for s in range(2):
                        dst = DW * h + 32 * s
                        pieces.append((qks[dst:dst + 32, at + 2:at + 3], v[32 * (1 - s):32 * (1 - s) + 32, :]))
            return pieces

        def column(v):
            return v.rearrange("(p c) -> p c", c=1)

        def tables_and_weights_b():
            wu = a["L0_attn_b_Wu"].rearrange("r (h c d) -> c r h d", c=2, d=DA)
            bu = a["L0_attn_b_bu"].rearrange("(o h c d) -> c o h d", o=1, c=2, d=DA)
            return [(const[:, TABLES:], a["const"][:, TABLES:]),
                    (wq_b[:, :], a["L0_attn_b_Wq"]), (bq_b[:, :], column(a["L0_attn_b_bq"])),
                    (wd_b[:, :], a["L0_attn_b_Wd"]), (bd_b[:, :], column(a["L0_attn_b_bd"])),
                    (wu_b[0:32, 0:P].rearrange("r (h d) -> r h d", d=DA), wu[0]),
                    (wu_b[0:32, P:2 * P].rearrange("r (h d) -> r h d", d=DA), wu[1]),
                    (wu_b[32:33, 0:P].rearrange("r (h d) -> r h d", d=DA), bu[0]),
                    (wu_b[32:33, P:2 * P].rearrange("r (h d) -> r h d", d=DA), bu[1]),
                    (wo_b[:, :], a["L0_attn_b_Wo"]), (bo_b[:, :], column(a["L0_attn_b_bo"]))]

        parts_d = nc.dram_tensor("parts", [NB, 2, HA, 3, DA, T], BF16).ap()
        minus_ones = nc.dram_tensor("minus_ones", [1, HA, T], BF16).ap()
        s = Phase(nc, "load")
        casting = ExitStack()
        constb_f = casting.enter_context(nc.sbuf_tensor("constb_f", [P, CONSTB_COLS + SPREAD_COLS], F32))
        minus = casting.enter_context(nc.sbuf_tensor("minus", [HA, T], BF16))
        zero = casting.enter_context(nc.sbuf_tensor("zero", [P, 1], F32))
        block = nc.Block()
        with block:
            @block.vector
            def _(dve):
                nc.vector.memset(minus[:, :], -1.0).then_inc(s("minus"), 1)
                nc.vector.memset(zero[:, :], 0.0).then_inc(s("zero"), 1)
                dve.wait_ge(s("zero"), 1)
                for part in (HH, HL):
                    for n in range(NB):
                        nc.vector.tensor_copy(part[64:P, n, 0:1], zero[64:P, :]).then_inc(s("first_tokens"), 1)
                dve.wait_ge(s("tables"), 16)
                nc.vector.tensor_copy(constb[:, :], constb_f[:, 0:CONSTB_COLS]).then_inc(s("tables_cast"), 1)
                nc.vector.tensor_copy(spread_w[:, :], constb_f[:, CONSTB_COLS:]).then_inc(s("tables_cast"), 1)

            @block.sync
            def _(sp):
                n = 0
                sp.dma_start(constb_f[:, :], a["constb"]).then_inc(s("tables"), 16)
                sp.wait_ge(s("minus"), 1)
                sp.dma_start(minus_ones[0], minus[:, :]).then_inc(s("loaded"), 16)
                n += 16
                for dst, src in (
                    (const[:, 0:TABLES], a["const"][:, 0:TABLES]),
                    (wa[:, :], a["L0_attn_a_w_qkv"]), (wpa[:, :], a["L0_attn_a_w_proj"]),
                    *((bqk[:, i:i + 1], column(a["L0_attn_a_b_qkv"][P * i:P * i + P])) for i in range(3)),
                    (bpa[:, :], column(a["L0_attn_a_b_proj"])),
                ):
                    sp.dma_start(dst, src).then_inc(s("loaded"), 16)
                    n += 16
                sp.wait_ge(s("loaded"), n)

            @block.gpsimd
            def _(pool):
                nc.gpsimd.memset(eps[:, :], LN_EPS).then_inc(s("eps"), 1)
                pool.wait_ge(s("eps"), 1)
        s.close()
        casting.close()

        g = Kept()
        g.psum, g.X, g.Y, g.eps, g.cst = psum, X, Y, eps, cst
        g.cstb, g.ident, g.x_d, g.wa, g.wpa = cstb, ident, x_d, wa, wpa
        g.bqk, g.bpa, g.wq_b, g.bq_b, g.wd_b, g.bd_b = bqk, bpa, wq_b, bq_b, wd_b, bd_b
        g.wu_b, g.wo_b, g.bo_b, g.wo, g.w1 = wu_b, wo_b, bo_b, wo, w1
        g.w2, g.b1, g.vecs, g.qks, g.load_layer = w2, b1, vecs, qks, load_layer
        g.HH, g.HL, g.wqkv_h, g.wqkv_l, g.wqkv_of = HH, HL, wqkv_h, wqkv_l, wqkv_of
        g.tables_and_weights_b, g.attention_scales = tables_and_weights_b, attention_scales
        g.parts_d, g.minus_ones, g.spread_w = parts_d, minus_ones, spread_w
        g.LATE_WEIGHTS = 16 * 13
        with nc.Fori(0, B // NB) as pair:
            attention_a(nc, a, g, pair)
            with nc.Fori(0, 2) as layer:
                feed_forward(nc, g, layer, 0)
            attention_b(nc, g)
            with nc.Fori(0, 2) as layer:
                feed_forward(nc, g, layer, 1)
            store(nc, g, out, pair)


SHIFTED = [(slice(0, 64), slice(0, T), slice(0, T)), (slice(64, P), slice(1, T), slice(0, T - 1))]


def shift_high(nc, s, g, n, tag=""):
    for rows, to, of in SHIFTED:
        last = nc.vector.tensor_copy(g.HH[rows, n, to], g.Y[rows, n, of])
    last.then_inc(s(tag + "shift_high"), 1)


def shift_low(engine, wait_ge, s, g, n, tag="", one_at_a_time=False):
    wait_ge(s(tag + "shift_high"), 1)
    for i, (rows, to, of) in enumerate(SHIFTED):
        engine.tensor_tensor(g.HL[rows, n, to], g.Y[rows, n, of], g.HH[rows, n, to].bitcast(F32),
                             ALU.subtract).then_inc(s(tag + "shifted"), 1)
        if one_at_a_time:
            wait_ge(s(tag + "shifted"), i + 1)


def attention_a(nc, a, g, pair):
    psum, X, Y, ident = g.psum, g.X, g.Y, g.ident
    wa, wpa, bqk, bpa, x_d, parts_d = g.wa, g.wpa, g.bqk, g.bpa, g.x_d, g.parts_d
    with ExitStack() as ctx:
        def sb(name, shape, dt=F32):
            return ctx.enter_context(nc.sbuf_tensor(name, shape, dt))

        QS = sb("QS", [P, NB, HA, T], BF16)
        KS = sb("KS", [P, NB, HA, T], BF16)
        VA = sb("VA", [P, NB, 4, HA, VCOLS])
        OC = sb("OC", [P, NB, 4, T])

        STACKING = 16 * (2 * len(RUNS) + 1)

        def stack_up(sp, n, sem):
            for w, stack in ((0, QS), (1, KS)):
                slot = 0
                for first, last in RUNS:
                    count = last - first + 1
                    lo = first if w == 0 else 2 - last
                    src = parts_d[n, w, :, lo:lo + count].rearrange("h c d t -> (c d) h t")
                    sp.dma_start(stack[DA * slot:DA * (slot + count), n, :, :], src).then_inc(sem, 16)
                    slot += count
            sp.dma_start(KS[GUARD_ROW:GUARD_ROW + 1, n, :, :], g.minus_ones).then_inc(sem, 16)

        with ExitStack() as prep:
            def sp_(name, shape, dt=F32):
                return prep.enter_context(nc.sbuf_tensor(name, shape, dt))
            XT = sp_("XT", [P, NB, 4, P])
            XC = sp_("XC", [P, NB, T])
            bufs = ln_buffers(sp_)
            QF = sp_("QF", [P, NB, 2, T])
            PRT = sp_("PRT", [P, NB, 2, 3, T], BF16)
            R1 = sp_("R1", [P, NB, 2, T])
            s = Phase(nc, "a1")
            next_s = Phase(nc, "a2")
            block = nc.Block()
            with block:
                @block.sync
                def _(sp):
                    for n in range(NB):
                        src = x_d[bass.ds(pair * NB + n, 1)].rearrange("a (t p) d -> p (a t) d", p=P)
                        sp.dma_start(XT[:, n, :, :], src).then_inc(s(f"x_loaded{n}"), 16)
                    sp.wait_ge(s("parts_out0"), 6 * 16)
                    sp.wait_ge(s("stacks_zero"), NB)
                    stack_up(sp, 0, next_s("stacked0"))
                    sp.wait_ge(s("parts_out1"), 6 * 16)

                @block.gpsimd
                def _(pool):
                    for i, stack in enumerate((QS, KS)):
                        rows = stack[64:P, :, :, :].rearrange("p n h t -> p (n h t)").bitcast(F32)
                        nc.gpsimd.memset(rows, 0.0).then_inc(s("stacks_zero"), 1)
                        pool.wait_ge(s("stacks_zero"), i + 1)
                    for n in range(NB):
                        nc.gpsimd.memset(VA[:, n, :, :, :], 0.0).then_inc(s("v_zero"), 1)
                        pool.wait_ge(s("v_zero"), n + 1)
                    for n in range(NB):
                        nc.gpsimd.memset(VA[:, n, :, :, DA:DA + 1], 1.0).then_inc(s("v_ones"), 1)
                    pool.wait_ge(s("v_ones"), NB)

                @block.tensor
                def _(pe):
                    for n in range(NB):
                        pe.wait_ge(s(f"x_loaded{n}"), 16)
                        for t in range(4):
                            last = nc.tensor.transpose(psum[:, 4 * n, P * t:P * t + P], XT[:, n, t, :], ident)
                        last.then_inc(s("x_turned"), 1)
                    norm_pe(nc, pe, s, g, bufs)
                    for n in range(NB):
                        pe.wait_ge(s("y_new"), n + 1)
                        for w in range(2):
                            nc.tensor.matmul(psum[:, 4 * n + w, :], wa[:, P * w:P * w + P], XC[:, n, :],
                                             start=True, stop=True).then_inc(s("qk"), 1)
                        for t in range(4):
                            last = nc.tensor.matmul(psum[:, 4 * n + 3, P * t:P * t + P], XC[:, n, P * t:P * t + P],
                                                    wa[:, 2 * P:3 * P], start=True, stop=True)
                        last.then_inc(s("v"), 1)

                @block.scalar
                def _(act):
                    for n in range(NB):
                        act.wait_ge(s("x_turned"), n + 1)
                        nc.scalar.activation(X[:, n, :], psum[:, 4 * n, :], ACT.Copy).then_inc(s("x_new"), 1)
                    norm_act(nc, act, s, g, bufs)
                    nc.scalar.preload_act_table_set(EXP_AND_LN)
                    for n in range(NB):
                        for w in range(2):
                            act.wait_ge(s("qk"), 2 * n + w + 1)
                            nc.scalar.activation(QF[:, n, w, :], psum[:, 4 * n + w, :], ACT.Identity,
                                                 bias=bqk[:, w:w + 1]).then_inc(s("qk_biased"), 1)
                        act.wait_ge(s("v"), n + 1)
                        act.wait_ge(s("v_ones"), NB)
                        nc.scalar.activation(VA[:, n, :, :, 0:DA],
                                             psum[:, 4 * n + 3, :].rearrange("p (t h d) -> p t h d", t=4, d=DA),
                                             ACT.Copy).then_inc(s("v_copied"), 1)
                    for n in range(NB):
                        for w in range(2):
                            for part in range(3):
                                act.wait_ge(s(("hi", "mid", "split")[part]), 2 * n + w + 1)
                                place = part if w == 0 else 2 - part
                                act.dma_start(parts_d[n, w, :, place], PRT[:, n, w, part, :])\
                                   .then_inc(s(f"parts_out{n}"), 16)

                @block.vector
                def _(dve):
                    norm_dve(nc, dve, s, g, bufs, XC)
                    for n in range(NB):
                        for w in range(2):
                            i = 2 * n + w
                            dve.wait_ge(s("qk_biased"), i + 1)
                            nc.vector.tensor_copy(PRT[:, n, w, 0, :], QF[:, n, w, :]).then_inc(s("hi"), 1)
                            dve.wait_ge(s("hi"), i + 1)
                            nc.vector.tensor_tensor(R1[:, n, w, :], QF[:, n, w, :], PRT[:, n, w, 0, :],
                                                    ALU.subtract).then_inc(s("rest"), 1)
                            dve.wait_ge(s("rest"), i + 1)
                            nc.vector.tensor_copy(PRT[:, n, w, 1, :], R1[:, n, w, :]).then_inc(s("mid"), 1)
                            dve.wait_ge(s("mid"), i + 1)
                            nc.vector.tensor_tensor(PRT[:, n, w, 2, :], R1[:, n, w, :], PRT[:, n, w, 1, :],
                                                    ALU.subtract).then_inc(s("split"), 1)
            s.close()

        with ExitStack() as main:
            def sm(name, shape, dt=F32):
                return main.enter_context(nc.sbuf_tensor(name, shape, dt))
            PT = sm("PT", [P, 8, 4, T])
            M = sm("M", [P, 4, 2, 4])
            MROW = sm("MROW", [2, ROWS, T], BF16)
            s = next_s
            UNITS = NB * HA // 2
            SLOT = [(2, 3), (4, 5)]
            O_BANK = 6
            TURN_AFTER = 2

            ring = []
            for u in range(UNITS + 1):
                for k in range(8):
                    if k == TURN_AFTER and u:
                        ring.append(("row", u - 1))
                    if u < UNITS:
                        ring.append(("tile", 8 * u + k))
            at = {use: i for i, use in enumerate(ring)}

            def bank(*use):
                return (0, 1, 7)[at[use] % 3]

            def where(unit):
                return unit // (HA // 2), 2 * (unit % (HA // 2))

            block = nc.Block()
            with block:
                @block.tensor
                def _(pe):
                    def take(*use):
                        if at[use] >= 3:
                            kind, i = ring[at[use] - 3]
                            pe.wait_ge(s("maxed" if kind == "tile" else "row_made"), i + 1)
                        return bank(*use)

                    def scores(unit, k):
                        n, h = where(unit)
                        if h == 0 and k == 0:
                            pe.wait_ge(s(f"stacked{n}"), STACKING)
                        qt = k % 4
                        nc.tensor.matmul(psum[:, take("tile", 8 * unit + k), :],
                                         QS[:, n, h + k // 4, P * qt:P * qt + P],
                                         KS[:, n, h + k // 4, :], start=True, stop=True)\
                          .then_inc(s("scored"), 1)

                    def turn_maxima(unit):
                        dst = take("row", unit)
                        pe.wait_ge(s("maxed"), 8 * (unit + 1))
                        for qt in range(4):
                            last = nc.tensor.transpose(psum[0:2, dst, P * qt:P * qt + P],
                                                       M[:, unit % 4, :, qt], ident)
                        last.then_inc(s("turned"), 1)

                    def scores_by_key(unit, k):
                        n, h = where(unit)
                        j, kt = k // 4, k % 4
                        if k == 0:
                            pe.wait_ge(s(f"row_in{unit % ROWS}"), 32 * (unit // ROWS + 1))
                        i = (2 * unit + j) * 2 + kt // 2
                        if i >= 2 and kt % 2 == 0:
                            pe.wait_ge(s("exped"), i - 1)
                        last = nc.tensor.matmul(psum[:, SLOT[i % 2][kt % 2], :],
                                                KS[:, n, h + j, P * kt:P * kt + P],
                                                QS[:, n, h + j, :], start=True, stop=True)
                        if kt % 2:
                            last.then_inc(s("scored_by_key"), 1)

                    def weighted_sums(group, kt):
                        n, quad = group // 4, group % 4
                        if kt == 0:
                            pe.wait_ge(s("exped"), 8 * (group + 1))
                            if group:
                                pe.wait_ge(s("o_copied"), group)
                            else:
                                pe.wait_ge(s("o_zeroed"), 1)
                        for j in range(4):
                            last = nc.tensor.matmul(psum[32 * j:32 * j + VCOLS, O_BANK, :],
                                                    VA[:, n, kt, 4 * quad + j, :], PT[:, (4 * group + j) % 8, kt, :],
                                                    start=(kt == 0), stop=(kt == 3))
                        if kt == 3:
                            last.then_inc(s("summed"), 1)

                    for u in range(LAG):
                        for k in range(8):
                            if k == TURN_AFTER and u:
                                turn_maxima(u - 1)
                            scores(u, k)
                    for u in range(UNITS):
                        for k in range(8):
                            if k == TURN_AFTER and u + LAG <= UNITS:
                                turn_maxima(u + LAG - 1)
                            if u + LAG < UNITS:
                                scores(u + LAG, k)
                            scores_by_key(u, k)
                            if k % 4 == 3 and u >= 2:
                                weighted_sums(u // 2 - 1, 2 * (u % 2) + k // 4)
                    for kt in range(4):
                        weighted_sums(UNITS // 2 - 1, kt)

                @block.vector
                def _(dve):
                    nc.vector.memset(psum[:, O_BANK, :], 0.0).then_inc(s("o_zeroed"), 1)
                    for u in range(UNITS):
                        for k in range(8):
                            i = 8 * u + k
                            dve.wait_ge(s("scored"), i + 1)
                            if u >= 4 and k == 0:
                                dve.wait_ge(s("turned"), u - 3)
                            nc.vector.tensor_reduce(M[:, u % 4, k // 4, k % 4:k % 4 + 1],
                                                    psum[:, bank("tile", i), :], AX_X, ALU.max)\
                              .then_inc(s("maxed"), 1)

                @block.sync
                def _(sp):
                    stack_up(sp, 1, s("stacked1"))
                    pieces = g.attention_scales(0) + g.tables_and_weights_b()
                    todo = list(pieces)
                    for u in range(UNITS):
                        n, h = where(u)
                        sp.wait_ge(s("row_made"), u + 1)
                        for j in range(2):
                            sp.dma_start(QS[GUARD_ROW:GUARD_ROW + 1, n, h + j, :], MROW[j:j + 1, u % ROWS, :])\
                              .then_inc(s(f"row_in{u % ROWS}"), 16)
                        for dst, src in todo[:3]:
                            sp.dma_start(dst, src).then_inc(s("weights"), 16)
                        todo = todo[3:]
                    assert not todo
                    sp.wait_ge(s("weights"), 16 * len(pieces))

                @block.scalar
                def _(act):
                    def copy_sums(group):
                        act.wait_ge(s("summed"), group + 1)
                        nc.scalar.activation(OC[:, group // 4, group % 4, :], psum[:, O_BANK, :], ACT.Copy)\
                          .then_inc(s("o_copied"), 1)

                    def make_row(unit):
                        act.wait_ge(s("turned"), unit + 1)
                        if unit >= ROWS:
                            act.wait_ge(s(f"row_in{unit % ROWS}"), 32 * (unit // ROWS))
                        nc.scalar.activation(MROW[:, unit % ROWS, :], psum[0:2, bank("row", unit), :], ACT.Copy)\
                          .then_inc(s("row_made"), 1)

                    nc.scalar.preload_act_table_set(EXP_AND_LN)
                    for u in range(LAG - 1):
                        make_row(u)
                    for u in range(UNITS):
                        for half in range(4):
                            head = 2 * u + half // 2
                            if head >= 8 and head % 4 == 0 and half % 2 == 0:
                                act.wait_ge(s("summed"), head // 4 - 1)
                            i = 4 * u + half
                            act.wait_ge(s("scored_by_key"), i + 1)
                            nc.scalar.activation(PT[:, head % 8, 2 * (half % 2):2 * (half % 2) + 2, :],
                                                 psum[:, SLOT[i % 2][0]:SLOT[i % 2][1] + 1, :], ACT.Exp,
                                                 scale=float(DA) ** -0.5).then_inc(s("exped"), 1)
                            if half == 0 and u + LAG <= UNITS:
                                make_row(u + LAG - 1)
                        if u % 2 and u > 2:
                            copy_sums(u // 2 - 1)
                    copy_sums(UNITS // 2 - 1)
            s.close()

        with ExitStack() as tail:
            def st(name, shape, dt=F32):
                return tail.enter_context(nc.sbuf_tensor(name, shape, dt))
            raw = st("raw", [P, 3 * T])
            RD = st("RD", [P, NB, 4, HA])
            OT = st("OT", [P, NB, 4, HA, DA])
            ON = st("ON", [P, NB, T])
            bufs = ln_buffers(lambda name, *rest: st("tail_" + name, *rest))
            s = Phase(nc, "a3")
            block = nc.Block()
            with block:
                @block.sync
                def _(sp):
                    sp.dma_start(raw[:, :], g.wqkv_of(0)).then_inc(s("raw"), 16)

                @block.gpsimd
                def _(pool):
                    for i in range(3):
                        cols = slice(T * i, T * i + T)
                        pool.wait_ge(s("weights_high"), i + 1)
                        nc.gpsimd.tensor_tensor(g.wqkv_l[:, cols], raw[:, cols], g.wqkv_h[:, cols].bitcast(F32),
                                                ALU.subtract).then_inc(s("weights_low"), 1)
                    pool.wait_ge(s("weights_low"), 3)

                @block.tensor
                def _(pe):
                    for n in range(NB):
                        for t in range(4):
                            for quad in range(4):
                                last = nc.tensor.transpose(psum[:, 4 * n + t, P * quad:P * quad + P],
                                                           OC[:, n, quad, P * t:P * t + P], ident)
                        last.then_inc(s("by_token"), 1)
                    for n in range(NB):
                        pe.wait_ge(s("o_div"), n + 1)
                        for t in range(4):
                            last = nc.tensor.transpose(psum[:, 4 * n, P * t:P * t + P],
                                                       OT[:, n, t, :, :].rearrange("p h d -> p (h d)"), ident)
                        last.then_inc(s("by_feature"), 1)
                    for n in range(NB):
                        pe.wait_ge(s("o_ready"), n + 1)
                        nc.tensor.matmul(psum[:, 4 * n + 2, :], wpa[:, :], ON[:, n, :], start=True, stop=True)\
                          .then_inc(s("projected"), 1)
                    norm_pe(nc, pe, s, g, bufs)

                @block.scalar
                def _(act):
                    act.wait_ge(s("raw"), 16)
                    for i in range(3):
                        cols = slice(T * i, T * i + T)
                        nc.scalar.activation(g.wqkv_h[:, cols], raw[:, cols], ACT.Copy).then_inc(s("weights_high"), 1)
                    for n in range(NB):
                        act.wait_ge(s("by_feature"), n + 1)
                        nc.scalar.activation(ON[:, n, :], psum[:, 4 * n, :], ACT.Identity, bias=bqk[:, 2:3])\
                          .then_inc(s("o_ready"), 1)
                    norm_act(nc, act, s, g, bufs)

                @block.vector
                def _(dve):
                    for n in range(NB):
                        dve.wait_ge(s("by_token"), n + 1)
                        heads = psum[:, 4 * n:4 * n + 4, :].rearrange("p t (h c) -> p t h c", c=32)
                        nc.vector.reciprocal(RD[:, n, :, :], heads[:, :, :, DA]).then_inc(s("rden"), 1)
                        dve.wait_ge(s("rden"), n + 1)
                        nc.vector.tensor_tensor(OT[:, n, :, :, :], heads[:, :, :, 0:DA],
                                                RD[:, n, :, :, None].to_broadcast([P, 4, HA, DA]), ALU.mult)\
                          .then_inc(s("o_div"), 1)
                    for n in range(NB):
                        dve.wait_ge(s("projected"), n + 1)
                        nc.vector.scalar_tensor_tensor(out=X[:, n, :], in0=psum[:, 4 * n + 2, :],
                                                       scalar=bpa[:, 0:1], in1=X[:, n, :],
                                                       op0=ALU.add, op1=ALU.add).then_inc(s("x_new"), 1)
                    norm_dve(nc, dve, s, g, bufs, Y)
                    dve.wait_ge(s("y_new"), 1)
                    shift_high(nc, s, g, 0)
                    shift_low(nc.vector, dve.wait_ge, s, g, 0)
            s.close()


def ln_buffers(alloc):
    b = {k: alloc("ln_" + k, [P, NB, T]) for k in ("centered", "squared")}
    b["recip"] = alloc("ln_recip", [P, NB, 4])
    b["diag"] = alloc("ln_diag", [P, NB, 4, P])
    return b


def variance_pe(nc, out, squared, mean):
    for t in range(4):
        last = nc.tensor.matmul(out[:, t:t + 1], squared[:, P * t:P * t + P], mean, start=True, stop=True)
    return last


def diagonals(nc, g, out, recip):
    return nc.vector.tensor_tensor(out, g.ident[:, None, :].to_broadcast([P, 4, P]),
                                   recip[:, :, None].to_broadcast([P, 4, P]), ALU.mult)


def norm_pe(nc, pe, s, g, b, tag=""):
    psum, X = g.psum, g.X
    for n in range(NB):
        pe.wait_ge(s(tag + "x_new"), n + 1)
        nc.tensor.matmul(psum[:, 4 * n, :], g.cst("center"), X[:, n, :], start=True, stop=True)\
          .then_inc(s(tag + "ln_centered"), 1)
    for n in range(NB):
        pe.wait_ge(s(tag + "ln_squared"), n + 1)
        variance_pe(nc, psum[:, 4 * n + 3, :], b["squared"][:, n, :], g.cst("mean")).then_inc(s(tag + "ln_var"), 1)
    for n in range(NB):
        pe.wait_ge(s(tag + "ln_diag"), n + 1)
        nc.tensor.matmul(psum[:, 4 * n + 1, :], g.cst("ones"), b["diag"][:, n, :, :].rearrange("p t c -> p (t c)"),
                         start=True, stop=True).then_inc(s(tag + "ln_spread"), 1)


def norm_act(nc, act, s, g, b, tag=""):
    psum, eps = g.psum, g.eps
    nc.scalar.preload_act_table_set(SQRT)
    for n in range(NB):
        act.wait_ge(s(tag + "ln_centered"), n + 1)
        nc.scalar.activation(b["squared"][:, n, :], psum[:, 4 * n, :], ACT.Square).then_inc(s(tag + "ln_squared"), 1)
    for n in range(NB):
        act.wait_ge(s(tag + "ln_var"), n + 1)
        nc.scalar.activation(b["recip"][:, n, :], psum[:, 4 * n + 3, 0:4], ACT.Sqrt, bias=eps[:, 0:1])\
          .then_inc(s(tag + "ln_sd"), 1)


def norm_dve(nc, dve, s, g, b, dst, tag=""):
    psum = g.psum
    for n in range(NB):
        dve.wait_ge(s(tag + "ln_squared"), n + 1)
        nc.vector.tensor_copy(b["centered"][:, n, :], psum[:, 4 * n, :]).then_inc(s(tag + "ln_kept"), 1)
    for n in range(NB):
        dve.wait_ge(s(tag + "ln_sd"), n + 1)
        nc.vector.reciprocal(b["recip"][:, n, :], b["recip"][:, n, :]).then_inc(s(tag + "ln_recip"), 1)
        dve.wait_ge(s(tag + "ln_recip"), n + 1)
        diagonals(nc, g, b["diag"][:, n, :, :], b["recip"][:, n, :]).then_inc(s(tag + "ln_diag"), 1)
    for n in range(NB):
        dve.wait_ge(s(tag + "ln_kept"), n + 1)
        dve.wait_ge(s(tag + "ln_spread"), n + 1)
        nc.vector.tensor_tensor(dst[:, n, :], b["centered"][:, n, :], psum[:, 4 * n + 1, :], ALU.mult)\
          .then_inc(s(tag + "y_new"), 1)


def feed_forward_schedule():
    def each(stage, n, items):
        return [(stage, n, i) for i in items]

    plan = each("project", 0, range(2 * PAIRS)) + [("shift", 1), ("value", 0, 0), ("ssq", 0)]
    plan += each("value", 0, (1, 2, 3)) + [("rotate", 0, 0), ("norm", 0), ("rotate", 0, 1)]
    plan += each("project", 1, range(5)) + [("spread", 0, 0), ("cast", 0, 0), ("spread", 0, 1), ("rotate", 0, 2)]
    plan += each("project", 1, (5, 6)) + [("scores", 0), ("cast", 0, 1), ("rotate", 0, 3), ("spread", 0, 2)]
    plan += [("scores", 1), ("cast", 0, 2), ("rotate", 1, 0), ("project", 1, 7), ("by_key", 0), ("spread", 0, 3)]
    plan += [("scores", 2), ("cast", 0, 3), ("by_key", 1), ("rotate", 1, 1), ("ssq", 1), ("zero", 1), ("sums", 0),
             ("divide", 0)]
    plan += [("scores", 3), ("norm", 1), ("value", 1, 0), ("value", 1, 1), ("rotate", 1, 2), ("by_key", 2),
             ("sums", 1), ("divide", 1)]
    plan += each("value", 1, (2, 3)) + [("spread", 1, 0), ("cast", 1, 0), ("by_key", 3), ("rotate", 1, 3),
                                        ("spread", 1, 1), ("cast", 1, 1), ("scores", 4), ("sums", 2), ("divide", 2)]
    plan += [("scores", 5), ("spread", 1, 2), ("cast", 1, 2), ("split", 0), ("by_key", 4), ("sums", 3), ("divide", 3)]
    plan += [("scores", 6), ("spread", 1, 3), ("cast", 1, 3), ("by_key", 5), ("split", 1), ("wo", 0), ("sums", 4),
             ("divide", 4)]
    plan += [("scores", 7), ("center", 0), ("by_key", 6), ("split", 2), ("sums", 5), ("var", 0), ("divide", 5)]
    plan += [("by_key", 7), ("deviation", 0), ("sums", 6), ("divide", 6), ("sums", 7), ("divide", 7)]
    plan += each("w1", 0, (0, 1)) + [("wo", 1), ("w1", 0, 2), ("center", 1), ("w2", 0), ("var", 1), ("deviation", 1),
                                  ("next_shift", 0)]
    plan += each("w1", 1, range(3)) + [("w2", 1)]
    return plan


def feed_forward(nc, g, layer, call):
    psum, Y, eps, cst, cstb = g.psum, g.Y, g.eps, g.cst, g.cstb
    HH, HL, wqkv_h, wqkv_l = g.HH, g.HL, g.wqkv_h, g.wqkv_l
    wo, w1, w2, b1, vecs, qks = g.wo, g.w1, g.w2, g.b1, g.vecs, g.qks
    BLOCKS = 2 * PAIRS
    SWAPS = 4
    CASTS = 4
    plan = feed_forward_schedule()

    order = []
    for stage, *i in plan:
        if stage == "project":
            order += [("project", *i)]
        elif stage == "ssq":
            order += [("ssq", i[0])]
        elif stage in ("value", "wo", "center", "var", "deviation", "w2"):
            order += [(stage, *i)]
        elif stage == "spread":
            order += [("spread", i[0], 2 * i[1] + w) for w in range(2)]
        elif stage in ("scores", "by_key"):
            order += [(stage, *i, j, half) for j in range(2) for half in range(2)]
        elif stage == "sums":
            order += [("den", *i), ("num", *i)]
        elif stage == "w1":
            order += [("gate", *i), ("up", *i)]
    at = {use: i for i, use in enumerate(order)}

    def bank(*use):
        return at[use] % BANKS

    def last_read(use):
        kind, *i = use
        if kind == "project":
            return ("squares_of_second", i[1] + 1) if i[0] else ("projected", i[1] + 1)
        if kind == "value":
            return "v_copied", 4 * i[0] + i[1] + 1
        if kind == "spread":
            return "qk_ready", BLOCKS * i[0] + i[1] + 1
        if kind in ("scores", "by_key"):
            return "maxed" if kind == "scores" else "exped", 4 * i[0] + 2 * i[1] + i[2] + 1
        if kind in ("gate", "up"):
            return "hidden", 3 * i[0] + i[1] + 1
        return {"ssq": "sd", "den": "den_refined", "num": "o_ready", "wo": "y_mid", "center": "ln_kept",
                "var": "ln_sd", "deviation": "ln_scaled", "w2": "y_new"}[kind], i[0] + 1

    with ExitStack() as ctx:
        def sb(name, shape, dt=F32):
            return ctx.enter_context(nc.sbuf_tensor(f"f{call}_{name}", shape, dt))

        QK = sb("QK", [P, NB, PAIRS, 2, T])
        SINK = sb("SINK", [P, T])
        SWAP = sb("SWAP", [P, SWAPS, 2, T])
        QZ = sb("QZ", [P, NB, HW, T])
        QB = sb("QB", [P, CASTS, 2, T], BF16)
        KB = sb("KB", [P, CASTS, WIN + T], BF16)
        V = sb("V", [P, NB, 4, T])
        SQ = sb("SQ", [P, BLOCKS, T])
        R = sb("R", [P, T])
        RH = sb("RH", [P, T], F32R)
        RL = sb("RL", [P, T], F32R)
        PT = sb("PT", [P, 4, 4 * SPAN])
        M = sb("M", [P, 4, 4])
        D = sb("D", [P, 4, 4, P], BF16)
        LR = sb("LR", [P, NB, 4])
        RD = sb("RD", [P, 2, T])

        raw = SQ[:, 0:3, :].rearrange("p a t -> p (a t)")

        def centered(n):
            return QK[:, n, 0, 1, :]

        def ln_squared(n):
            return QK[:, n, 1, 1, :]

        def mid(n):
            return QK[:, n, 3, 1, :]

        def ln_diag(n):
            return QK[:, n, 2, 1, :]

        def hidden(n, part, blk):
            return QZ[:, n, 3 * part + blk, :]

        s = Phase(nc, f"f{call}")

        block = nc.Block()
        with block:
            @block.sync
            def _(sp):
                for stage, *i in plan:
                    if stage == "project" and i[1] % 2:
                        pair = PAIRS * i[0] + i[1] // 2
                        sp.wait_ge(s("projected"), 2 * pair + 2)
                        if pair >= SWAPS:
                            sp.wait_ge(s("rotation_added"), 2 * (pair - SWAPS) + 2)
                        for row in range(0, P, 32):
                            sp.dma_start(SWAP[row:row + 32, pair % SWAPS, :, :],
                                         QK[row ^ 32:(row ^ 32) + 32, i[0], i[1] // 2, :, :])\
                              .then_inc(s(f"swapped{pair % SWAPS}"), 16)
                    elif stage == "ssq" and i == [0]:
                        loads = g.load_layer(sp, layer, s("weights"))
                        assert loads == g.LATE_WEIGHTS
                    elif stage == "ssq" and i == [1]:
                        sp.wait_ge(s("ssq"), 2)
                        sp.dma_start(raw, g.wqkv_of(1 - layer)).then_inc(s("raw"), 16)
                sp.wait_ge(s("rotated"), BLOCKS * NB)
                sp.wait_ge(s("k_table"), 1)
                pieces = g.attention_scales(1 - layer)
                for dst, src in pieces:
                    sp.dma_start(dst, src).then_inc(s("next_layer"), 16)
                sp.wait_ge(s("next_layer"), 16 * len(pieces))

            @block.gpsimd
            def _(pool):
                def zero(n):
                    for j in range(2):
                        other = slice(DW * (1 - j), DW * (1 - j) + DW)
                        nc.gpsimd.memset(QZ[other, n, j:HW:2, :], 0.0).then_inc(s("zeroed"), 1)
                        pool.wait_ge(s("zeroed"), 2 * n + j + 1 + (n > 0))

                zero(0)
                nc.gpsimd.memset(KB[:, :, 0:WIN], 0.0).then_inc(s("zeroed"), 1)
                pool.wait_ge(s("zeroed"), 3)
                for stage, *i in plan:
                    if stage == "rotate":
                        n, c = i
                        pair = PAIRS * n + c
                        for w in range(2):
                            if w == 1:
                                pool.wait_ge(s("k_table"), 1)
                                pool.wait_ge(s(f"swapped{pair % SWAPS}"), 64 * (pair // SWAPS + 1))
                                nc.gpsimd.tensor_tensor(SWAP[:, pair % SWAPS, 1, :], SWAP[:, pair % SWAPS, 1, :],
                                                        SINK[:, :], ALU.mult).then_inc(s("k_rotated"), 1)
                                pool.wait_ge(s("k_rotated"), pair + 1)
                            pool.wait_ge(s("rotated"), 2 * pair + w + 1)
                            nc.gpsimd.tensor_tensor(QK[:, n, c, w, :], QK[:, n, c, w, :],
                                                    SWAP[:, pair % SWAPS, w, :], ALU.add)\
                              .then_inc(s("rotation_added"), 1)
                    elif stage == "shift":
                        shift_low(nc.gpsimd, pool.wait_ge, s, g, 1, "start_", True)
                    elif stage == "zero":
                        pool.wait_ge(s("rotation_added"), 2 * (PAIRS + 1) + 2)
                        zero(1)
                    elif stage == "split":
                        cols = slice(T * i[0], T * i[0] + T)
                        pool.wait_ge(s("weights_high"), i[0] + 1)
                        nc.gpsimd.tensor_tensor(wqkv_l[:, cols], raw[:, cols], wqkv_h[:, cols].bitcast(F32),
                                                ALU.subtract).then_inc(s("weights_low"), 1)
                    elif stage == "scores":
                        for j in range(2):
                            head = 2 * i[0] + j
                            pool.wait_ge(s("maxed"), 2 * head + 2)
                            if head >= 4:
                                pool.wait_ge(s("by_key"), 2 * (head - 4) + 2)
                            nc.gpsimd.tensor_tensor(
                                D[:, head % 4, :, :], cstb("ident")[:, None, :].to_broadcast([P, 4, P]),
                                M[:, head % 4, :, None].to_broadcast([P, 4, P]), ALU.mult).then_inc(s("diag"), 1)

            @block.tensor
            def _(pe):
                def take(*use):
                    i = at[use]
                    if i >= BANKS:
                        name, value = last_read(order[i - BANKS])
                        pe.wait_ge(s(name), value)
                    return psum[:, i % BANKS, :]

                def project(n, b):
                    col = P * (PAIRS * (b % 2) + b // 2)
                    if n and b == 0:
                        pe.wait_ge(s("start_shifted"), 2)
                    dst = take("project", n, b)
                    nc.tensor.matmul(dst, wqkv_h[:, col:col + P], HH[:, n, :], start=True, stop=False)
                    nc.tensor.matmul(dst, wqkv_h[:, col:col + P], HL[:, n, :], start=False, stop=False)
                    nc.tensor.matmul(dst, wqkv_l[:, col:col + P], HH[:, n, :], start=False, stop=True)\
                      .then_inc(s("project"), 1)

                def ssq(n):
                    dst = take("ssq", n)
                    pe.wait_ge(s("squares_of_second" if n else "squares_of_first"), BLOCKS)
                    for w in range(2):
                        for c in range(PAIRS):
                            last = nc.tensor.matmul(dst[32 * c:32 * c + 32, :], cst("head_sum", 32 * w, 32),
                                                    SQ[:, 2 * c + w, :], start=(w == 0), stop=(w == 1))
                    last.then_inc(s("ssq"), 1)

                def value(n, t):
                    dst, cols = take("value", n, t), slice(P * t, P * t + P)
                    nc.tensor.matmul(dst, HH[:, n, cols], wqkv_h[:, 2 * T:3 * T], start=True, stop=False)
                    nc.tensor.matmul(dst, HH[:, n, cols], wqkv_l[:, 2 * T:3 * T], start=False, stop=False)
                    nc.tensor.matmul(dst, HL[:, n, cols], wqkv_h[:, 2 * T:3 * T], start=False, stop=True)\
                      .then_inc(s("value"), 1)

                def spread(n, c):
                    pe.wait_ge(s("norm_split"), n + 1)
                    for w in range(2):
                        dst = take("spread", n, 2 * c + w)
                        rows = g.spread_w[:, P * (2 * c + w):P * (2 * c + w) + P]
                        nc.tensor.matmul(dst, rows, RH[:, :], start=True, stop=False)
                        nc.tensor.matmul(dst, rows, RL[:, :], start=False, stop=True).then_inc(s("spread"), 1)

                def scores(i):
                    n, c = i // PAIRS, i % PAIRS
                    pe.wait_ge(s("cast"), BLOCKS * n + 2 * c + 2)
                    for j in range(2):
                        for half in range(2):
                            dst = take("scores", i, j, half)
                            for k in range(2):
                                tile = 2 * half + k
                                part = dst[:, SPAN * k:SPAN * k + SPAN]
                                nc.tensor.matmul(part, QB[:, i % CASTS, j, P * tile:P * tile + P],
                                                 KB[:, i % CASTS, P * tile:P * tile + SPAN], start=True, stop=False)
                                last = nc.tensor.matmul(part, cstb("ident"), cstb("mask_q" if tile else "mask_first"),
                                                        start=False, stop=True)
                            last.then_inc(s("scores"), 1)

                def by_key(i):
                    n, c = i // PAIRS, i % PAIRS
                    for j in range(2):
                        head = 2 * i + j
                        pe.wait_ge(s("diag"), head + 1)
                        for half in range(2):
                            dst = take("by_key", i, j, half)
                            for k in range(2):
                                tile = 2 * half + k
                                width = min(SPAN, T - P * tile)
                                part = dst[:, SPAN * k:SPAN * k + width]
                                nc.tensor.matmul(part, QK[:, n, c, 1, P * tile:P * tile + P],
                                                 QZ[:, n, 2 * c + j, P * tile:P * tile + width],
                                                 start=True, stop=False)
                                nc.tensor.matmul(part, cstb("ident"), cstb("mask_k", 0, width),
                                                 start=False, stop=False)
                                diag = D[:, head % 4, :, :].rearrange("p a b -> p (a b)")
                                last = nc.tensor.matmul(part, cstb("minus1"), diag[:, P * tile:P * tile + width],
                                                        start=False, stop=True)
                            last.then_inc(s("by_key"), 1)

                def sums(i):
                    n, c = i // PAIRS, i % PAIRS
                    pe.wait_ge(s("exped"), 4 * i + 4)
                    for kind in ("den", "num"):
                        dst = take(kind, i)
                        for tile in range(4):
                            width = min(SPAN, T - P * tile)
                            for j in range(2):
                                weights = (V[:, n, tile, DW * (2 * c + j):DW * (2 * c + j) + DW] if kind == "num"
                                           else cst("ones", 0, DW))
                                last = nc.tensor.matmul(
                                    dst[DW * j:DW * j + DW, P * tile:P * tile + width], weights,
                                    PT[:, (2 * i + j) % 4, SPAN * tile:SPAN * tile + width],
                                    start=(tile == 0), stop=(tile == 3), skip_group_check=True)
                        last.then_inc(s(kind), 1)

                for stage, *i in plan:
                    if stage == "project":
                        project(*i)
                    elif stage == "ssq":
                        ssq(*i)
                    elif stage == "value":
                        value(*i)
                    elif stage == "spread":
                        spread(*i)
                    elif stage == "scores":
                        scores(*i)
                    elif stage == "by_key":
                        by_key(*i)
                    elif stage == "sums":
                        sums(*i)
                    elif stage == "wo":
                        n = i[0]
                        pe.wait_ge(s("weights"), g.LATE_WEIGHTS)
                        pe.wait_ge(s("o_ready"), PAIRS * (n + 1))
                        dst = take("wo", n)
                        for c in range(PAIRS):
                            last = nc.tensor.matmul(dst, wo[:, c, :], QK[:, n, c, 0, :], start=(c == 0),
                                                    stop=(c == PAIRS - 1))
                        last.then_inc(s("wo"), 1)
                    elif stage == "center":
                        n = i[0]
                        pe.wait_ge(s("shifted_mid"), n + 1)
                        nc.tensor.matmul(take("center", n), cst("center"), mid(n), start=True, stop=True)\
                          .then_inc(s("center"), 1)
                    elif stage == "var":
                        n = i[0]
                        pe.wait_ge(s("ln_squared"), n + 1)
                        variance_pe(nc, take("var", n), ln_squared(n), cst("mean")).then_inc(s("var"), 1)
                    elif stage == "deviation":
                        n = i[0]
                        pe.wait_ge(s("ln_diag"), n + 1)
                        nc.tensor.matmul(take("deviation", n), cst("ones"), ln_diag(n), start=True, stop=True)\
                          .then_inc(s("deviation"), 1)
                    elif stage == "w1":
                        n, blk = i
                        lo, w = HID_BLOCKS[blk]
                        pe.wait_ge(s("ln_done"), n + 1)
                        for kind, first in (("gate", HID), ("up", 0)):
                            nc.tensor.matmul(take(kind, n, blk)[0:w, :], w1[:, first + lo:first + lo + w],
                                             mid(n), start=True, stop=True).then_inc(s(kind), 1)
                    elif stage == "w2":
                        n = i[0]
                        dst = take("w2", n)
                        for blk, (lo, w) in enumerate(HID_BLOCKS):
                            pe.wait_ge(s("hidden"), 3 * n + blk + 1)
                            last = nc.tensor.matmul(dst, w2[0:w, blk, :], hidden(n, 1, blk)[0:w, :],
                                                    start=(blk == 0), stop=(blk == 2))
                        last.then_inc(s("w2"), 1)

            @block.scalar
            def _(act):
                for stage, *i in plan:
                    if stage == "project":
                        n, b = i
                        c, w = b // 2, b % 2
                        act.wait_ge(s("project"), BLOCKS * n + b + 1)
                        nc.scalar.activation(QK[:, n, c, w, :], psum[:, bank("project", n, b), :], ACT.Copy)\
                          .then_inc(s("projected"), 1)
                        if n:
                            act.wait_ge(s("ssq"), 1)
                            nc.scalar.activation(SQ[:, b, :], psum[:, bank("project", n, b), :], ACT.Square)\
                              .then_inc(s("squares_of_second"), 1)
                    elif stage == "ssq":
                        n = i[0]
                        nc.scalar.preload_act_table_set(SQRT)
                        act.wait_ge(s("ssq"), n + 1)
                        if n:
                            act.wait_ge(s("norm_split"), n)
                        nc.scalar.activation(R[:, :], psum[:, bank("ssq", n), :], ACT.Sqrt).then_inc(s("sd"), 1)
                        nc.scalar.preload_act_table_set(EXP_AND_LN)
                    elif stage == "value":
                        n, t = i
                        act.wait_ge(s("value"), 4 * n + t + 1)
                        nc.scalar.activation(V[:, n, t, :], psum[:, bank("value", n, t), :], ACT.Copy)\
                          .then_inc(s("v_copied"), 1)
                    elif stage == "split":
                        cols = slice(T * i[0], T * i[0] + T)
                        act.wait_ge(s("raw"), 16)
                        act.wait_ge(s("value"), 4 * NB)
                        nc.scalar.activation(wqkv_h[:, cols], raw[:, cols], ACT.Copy).then_inc(s("weights_high"), 1)
                    elif stage == "cast":
                        n, c = i
                        pair = PAIRS * n + c
                        if pair >= CASTS:
                            act.wait_ge(s("scores"), 4 * (pair - CASTS) + 4)
                        act.wait_ge(s("qk_ready"), BLOCKS * n + 2 * c + 1)
                        nc.scalar.activation(QB[:, pair % CASTS, :, :], QZ[:, n, 2 * c:2 * c + 2, :], ACT.Copy)\
                          .then_inc(s("cast"), 1)
                        act.wait_ge(s("qk_ready"), BLOCKS * n + 2 * c + 2)
                        nc.scalar.activation(KB[:, pair % CASTS, WIN:WIN + T], QK[:, n, c, 1, :], ACT.Copy)\
                          .then_inc(s("cast"), 1)
                    elif stage == "by_key":
                        i = i[0]
                        for j in range(2):
                            if i >= 2:
                                act.wait_ge(s("num"), i - 1)
                            for half in range(2):
                                act.wait_ge(s("by_key"), 4 * i + 2 * j + half + 1)
                                width = SPAN + min(SPAN, T - P * (2 * half + 1))
                                nc.scalar.activation(
                                    PT[:, (2 * i + j) % 4, 2 * SPAN * half:2 * SPAN * half + width],
                                    psum[:, bank("by_key", i, j, half), 0:width], ACT.Exp, scale=8.0)\
                                  .then_inc(s("exped"), 1)
                    elif stage == "sums":
                        i = i[0]
                        act.wait_ge(s("den"), i + 1)
                        if i >= 2:
                            act.wait_ge(s("o_ready"), i - 1)
                        nc.scalar.activation(RD[:, i % 2, :], psum[:, bank("den", i), :], ACT.Ln)\
                          .then_inc(s("den_log"), 1)
                        act.wait_ge(s("den_log"), i + 1)
                        nc.scalar.activation(RD[:, i % 2, :], RD[:, i % 2, :], ACT.Exp, scale=-1.0)\
                          .then_inc(s("den_recip"), 1)
                    elif stage == "center":
                        n = i[0]
                        act.wait_ge(s("center"), n + 1)
                        nc.scalar.activation(ln_squared(n), psum[:, bank("center", n), :], ACT.Square)\
                          .then_inc(s("ln_squared"), 1)
                    elif stage == "var":
                        n = i[0]
                        nc.scalar.preload_act_table_set(SQRT)
                        act.wait_ge(s("var"), n + 1)
                        nc.scalar.activation(LR[:, n, :], psum[:, bank("var", n), 0:4], ACT.Sqrt,
                                             bias=eps[:, 0:1]).then_inc(s("ln_sd"), 1)
                        nc.scalar.preload_act_table_set(GELU if n else EXP_AND_LN)
                    elif stage == "w1":
                        n, blk = i
                        w = HID_BLOCKS[blk][1]
                        if n == 0 and blk == 0:
                            nc.scalar.preload_act_table_set(GELU)
                        act.wait_ge(s("weights"), g.LATE_WEIGHTS)
                        act.wait_ge(s("gate"), 3 * n + blk + 1)
                        nc.scalar.activation(hidden(n, 0, blk)[0:w, :], psum[0:w, bank("gate", n, blk), :],
                                             ACT.Gelu, bias=b1[0:w, 3 + blk:4 + blk]).then_inc(s("gated"), 1)

            @block.vector
            def _(dve):
                def rotate(n, c):
                    pair = PAIRS * n + c
                    dve.wait_ge(s("projected"), 2 * pair + 2)
                    dve.wait_ge(s(f"swapped{pair % SWAPS}"), 64 * (pair // SWAPS + 1))
                    for x, column, table in ((QK[:, n, c, 0, :], 0, "cosq"),
                                                (SWAP[:, pair % SWAPS, 0, :], 2, "sinq"),
                                                (QK[:, n, c, 1, :], 1, "cosk")):
                        last = nc.vector.scalar_tensor_tensor(out=x, in0=x, scalar=qks[:, column:column + 1],
                                                              in1=cst(table), op0=ALU.mult, op1=ALU.mult)
                        if table != "cosq":
                            last.then_inc(s("rotated"), 1)

                def norm(n):
                    dve.wait_ge(s("sd"), n + 1)
                    nc.vector.tensor_scalar(R[:, :], R[:, :], 1e-12, None, ALU.max).then_inc(s("clipped"), 1)
                    dve.wait_ge(s("clipped"), n + 1)
                    nc.vector.reciprocal(R[:, :], R[:, :]).then_inc(s("norm_recip"), 1)
                    dve.wait_ge(s("norm_recip"), n + 1)
                    if n:
                        dve.wait_ge(s("spread"), BLOCKS * n)
                    nc.vector.tensor_copy(RH[:, :], R[:, :]).then_inc(s("norm_high"), 1)
                    dve.wait_ge(s("norm_high"), n + 1)
                    nc.vector.tensor_tensor(RL[:, :], R[:, :], RH[:, :].bitcast(F32), ALU.subtract)\
                      .then_inc(s("norm_split"), 1)

                def normalise(n, c):
                    for w in range(2):
                        i = BLOCKS * n + 2 * c + w
                        dve.wait_ge(s("spread"), i + 1)
                        dve.wait_ge(s("rotation_added"), i + 1)
                        if i == 0:
                            dve.wait_ge(s("zeroed"), 3)
                        if i == BLOCKS:
                            dve.wait_ge(s("zeroed"), 5)
                        r = psum[:, bank("spread", n, 2 * c + w), :]
                        if w == 0:
                            nc.vector.tensor_tensor(QZ[0:DW, n, 2 * c, :], QK[0:DW, n, c, 0, :], r[0:DW, :], ALU.mult)
                            nc.vector.tensor_tensor(QZ[DW:P, n, 2 * c + 1, :], QK[DW:P, n, c, 0, :], r[DW:P, :],
                                                    ALU.mult).then_inc(s("qk_ready"), 1)
                        else:
                            nc.vector.tensor_tensor(QK[:, n, c, 1, :], QK[:, n, c, 1, :], r, ALU.mult)\
                              .then_inc(s("qk_ready"), 1)

                def maxima(i):
                    for j in range(2):
                        head = 2 * i + j
                        if head >= 4:
                            dve.wait_ge(s("diag"), head - 3)
                        for half in range(2):
                            dve.wait_ge(s("scores"), 2 * head + half + 1)
                            nc.vector.tensor_reduce(
                                M[:, head % 4, 2 * half:2 * half + 2],
                                psum[:, bank("scores", i, j, half), 0:2 * SPAN].rearrange("p (k x) -> p k x", k=2),
                                AX_X, ALU.max).then_inc(s("maxed"), 1)

                def divide(i):
                    n, c = i // PAIRS, i % PAIRS
                    dve.wait_ge(s("den_recip"), i + 1)
                    nc.vector.tensor_tensor(QK[:, n, c, 0, :], psum[:, bank("den", i), :], RD[:, i % 2, :],
                                            ALU.mult).then_inc(s("den_refined"), 1)
                    dve.wait_ge(s("den_refined"), i + 1)
                    nc.vector.scalar_tensor_tensor(out=RD[:, i % 2, :], in0=QK[:, n, c, 0, :], scalar=-2.0,
                                                   in1=RD[:, i % 2, :], op0=ALU.add, op1=ALU.mult)\
                      .then_inc(s("minus_recip"), 1)
                    dve.wait_ge(s("minus_recip"), i + 1)
                    dve.wait_ge(s("num"), i + 1)
                    nc.vector.tensor_tensor(QK[:, n, c, 0, :], psum[:, bank("num", i), :], RD[:, i % 2, :],
                                            ALU.mult).then_inc(s("o_ready"), 1)

                nc.vector.tensor_scalar(SINK[:, :], cst("sink"), qks[:, 3:4], None, ALU.mult).then_inc(s("k_table"), 1)
                for stage, *i in plan:
                    if stage == "project" and i[0] == 0:
                        b = i[1]
                        dve.wait_ge(s("projected"), b + 1)
                        q = QK[:, 0, b // 2, b % 2, :]
                        nc.vector.tensor_tensor(SQ[:, b, :], q, q, ALU.mult).then_inc(s("squares_of_first"), 1)
                    elif stage == "shift":
                        shift_high(nc, s, g, 1, "start_")
                    elif stage == "next_shift":
                        dve.wait_ge(s("y_new"), 1)
                        shift_high(nc, s, g, 0)
                        shift_low(nc.vector, dve.wait_ge, s, g, 0)
                    elif stage == "rotate":
                        rotate(*i)
                    elif stage == "norm":
                        norm(*i)
                    elif stage == "spread":
                        normalise(*i)
                    elif stage == "scores":
                        maxima(*i)
                    elif stage == "divide":
                        divide(*i)
                    elif stage == "wo":
                        n = i[0]
                        dve.wait_ge(s("wo"), n + 1)
                        nc.vector.tensor_tensor(Y[:, n, :], Y[:, n, :], psum[:, bank("wo", n), :], ALU.subtract)\
                          .then_inc(s("y_mid"), 1)
                        dve.wait_ge(s("y_mid"), n + 1)
                        nc.vector.tensor_copy(mid(n)[0:64, :], Y[0:64, n, :])
                        nc.vector.tensor_copy(mid(n)[64:P, 1:T], Y[64:P, n, 0:T - 1])
                        nc.vector.memset(mid(n)[64:P, 0:1], 0.0).then_inc(s("shifted_mid"), 1)
                    elif stage == "center":
                        n = i[0]
                        dve.wait_ge(s("ln_squared"), n + 1)
                        nc.vector.tensor_copy(centered(n), psum[:, bank("center", n), :]).then_inc(s("ln_kept"), 1)
                    elif stage == "var":
                        n = i[0]
                        dve.wait_ge(s("ln_sd"), n + 1)
                        nc.vector.reciprocal(LR[:, n, :], LR[:, n, :]).then_inc(s("ln_recip"), 1)
                        dve.wait_ge(s("ln_recip"), n + 1)
                        diagonals(nc, g, ln_diag(n).rearrange("p (t c) -> p t c", t=4), LR[:, n, :])\
                          .then_inc(s("ln_diag"), 1)
                    elif stage == "deviation":
                        n = i[0]
                        dve.wait_ge(s("weights"), g.LATE_WEIGHTS)
                        dve.wait_ge(s("ln_kept"), n + 1)
                        dve.wait_ge(s("deviation"), n + 1)
                        nc.vector.scalar_tensor_tensor(out=mid(n), in0=centered(n), scalar=vecs[:, 0:1],
                                                       in1=psum[:, bank("deviation", n), :],
                                                       op0=ALU.mult, op1=ALU.mult).then_inc(s("ln_scaled"), 1)
                        dve.wait_ge(s("ln_scaled"), n + 1)
                        nc.vector.tensor_scalar(mid(n), mid(n), vecs[:, 1:2], None, ALU.add)\
                          .then_inc(s("ln_done"), 1)
                    elif stage == "w1":
                        n, blk = i
                        w = HID_BLOCKS[blk][1]
                        dve.wait_ge(s("up"), 3 * n + blk + 1)
                        dve.wait_ge(s("gated"), 3 * n + blk + 1)
                        nc.vector.scalar_tensor_tensor(
                            out=hidden(n, 1, blk)[0:w, :], in0=psum[0:w, bank("up", n, blk), :],
                            scalar=b1[0:w, blk:blk + 1], in1=hidden(n, 0, blk)[0:w, :],
                            op0=ALU.add, op1=ALU.mult).then_inc(s("hidden"), 1)
                    elif stage == "w2":
                        n = i[0]
                        dve.wait_ge(s("w2"), n + 1)
                        nc.vector.scalar_tensor_tensor(out=Y[:, n, :], in0=psum[:, bank("w2", n), :],
                                                       scalar=vecs[:, 2:3], in1=Y[:, n, :],
                                                       op0=ALU.add, op1=ALU.add).then_inc(s("y_new"), 1)
        s.close()


def attention_b(nc, g):
    psum, X, Y, cst, ident = g.psum, g.X, g.Y, g.cst, g.ident
    with ExitStack() as ctx:
        def sb(name, shape, dt=F32):
            return ctx.enter_context(nc.sbuf_tensor("b_" + name, shape, dt))

        first = ln_buffers(lambda name, *rest: sb("1" + name, *rest))
        second = ln_buffers(lambda name, *rest: sb("2" + name, *rest))
        Q = sb("Q", [P, NB, T])
        NEG = sb("NEG", [P, NB, T])
        E = sb("E", [P, NB, T])
        LAT = sb("LAT", [33, NB, T])
        KT = sb("KT", [P, NB, 4, P])
        NEGK = sb("NEGK", [P, NB, 4, P])
        EK = sb("EK", [P, NB, 4, P])
        VT = sb("VT", [P, NB, 4, P + HA])
        CTX = sb("CTX", [P, NB, P + HA])
        DEN = sb("DEN", [P, NB, 4, HA])
        OT = sb("OT", [P, NB, 4, HA, DA])
        ON = sb("ON", [P, NB, T])
        s = Phase(nc, "b")

        def halves(n):
            return psum[:, 4 * n + 2:4 * n + 4, :].rearrange("p b (u x) -> p (b u) x", u=2)

        block = nc.Block()
        with block:
            @block.gpsimd
            def _(pool):
                for n in range(NB):
                    nc.gpsimd.memset(LAT[32:33, n, :], 1.0).then_inc(s("ones"), 1)
                    pool.wait_ge(s("ones"), 2 * n + 1)
                    nc.gpsimd.memset(VT[:, n, :, P:P + HA], 1.0).then_inc(s("ones"), 1)
                    pool.wait_ge(s("ones"), 2 * n + 2)

            @block.tensor
            def _(pe):
                norm_pe(nc, pe, s, g, first)
                for n in range(NB):
                    pe.wait_ge(s("y_new"), n + 1)
                    nc.tensor.matmul(psum[0:32, 4 * n + 1, :], g.wd_b[:, :], Y[:, n, :], start=True, stop=True)\
                      .then_inc(s("latent"), 1)
                    nc.tensor.matmul(psum[:, 4 * n, :], g.wq_b[:, :], Y[:, n, :], start=True, stop=True)\
                      .then_inc(s("q"), 1)
                pe.wait_ge(s("ones"), 2 * NB)
                for n in range(NB):
                    pe.wait_ge(s("latent_ready"), n + 1)
                    for t in range(4):
                        last = nc.tensor.matmul(psum[:, 4 * n + 2 + t // 2, 256 * (t % 2):256 * (t % 2) + 256],
                                                LAT[:, n, P * t:P * t + P], g.wu_b[:, :], start=True, stop=True)
                        if t % 2:
                            last.then_inc(s("kv"), 1)
                for n in range(NB):
                    pe.wait_ge(s("k_ready"), 2 * n + 2)
                    pe.wait_ge(s("v_ready"), 2 * n + 2)
                    pe.wait_ge(s("q_ready"), n + 1)
                    for t in range(4):
                        last = nc.tensor.matmul(psum[:, 4 * n, 0:P + HA], KT[:, n, t, :], VT[:, n, t, :],
                                                start=(t == 0), stop=(t == 3))
                    last.then_inc(s("context"), 1)
                for n in range(NB):
                    pe.wait_ge(s("context_ready"), n + 1)
                    for t in range(4):
                        last = nc.tensor.matmul(halves(n)[:, t, 0:P + HA], Q[:, n, P * t:P * t + P], CTX[:, n, :],
                                                start=True, stop=True)
                    last.then_inc(s("by_token"), 1)
                for n in range(NB):
                    pe.wait_ge(s("o_div"), n + 1)
                    for t in range(4):
                        last = nc.tensor.transpose(psum[:, 4 * n + 1, P * t:P * t + P],
                                                   OT[:, n, t, :, :].rearrange("p h d -> p (h d)"), ident)
                    last.then_inc(s("by_feature"), 1)
                for n in range(NB):
                    pe.wait_ge(s("o_ready"), n + 1)
                    nc.tensor.matmul(psum[:, 4 * n, :], g.wo_b[:, :], ON[:, n, :], start=True, stop=True)\
                      .then_inc(s("projected"), 1)
                norm_pe(nc, pe, s, g, second, "2")

            @block.scalar
            def _(act):
                norm_act(nc, act, s, g, first)
                nc.scalar.preload_act_table_set(EXP_AND_LN)
                for n in range(NB):
                    act.wait_ge(s("latent"), n + 1)
                    nc.scalar.activation(LAT[0:32, n, :], psum[0:32, 4 * n + 1, :], ACT.Identity,
                                         bias=g.bd_b[:, 0:1]).then_inc(s("latent_ready"), 1)
                for n in range(NB):
                    act.wait_ge(s("q_neg"), n + 1)
                    nc.scalar.activation(E[:, n, :], NEG[:, n, :], ACT.Exp).then_inc(s("q_exp"), 1)
                for n in range(NB):
                    for half in range(2):
                        i = 2 * n + half
                        act.wait_ge(s("k_neg"), i + 1)
                        nc.scalar.activation(VT[:, n, 2 * half:2 * half + 2, 0:P],
                                             halves(n)[:, 2 * half:2 * half + 2, P:2 * P],
                                             ACT.Copy).then_inc(s("v_ready"), 1)
                        nc.scalar.activation(EK[:, n, 2 * half:2 * half + 2, :],
                                             NEGK[:, n, 2 * half:2 * half + 2, :], ACT.Exp)\
                          .then_inc(s("k_exp"), 1)
                for n in range(NB):
                    act.wait_ge(s("by_feature"), n + 1)
                    nc.scalar.activation(ON[:, n, :], psum[:, 4 * n + 1, :], ACT.Copy).then_inc(s("o_ready"), 1)
                norm_act(nc, act, s, g, second, "2")

            @block.vector
            def _(dve):
                for n in range(NB):
                    nc.vector.tensor_tensor(X[:, n, :], X[:, n, :], Y[:, n, :], ALU.add).then_inc(s("x_new"), 1)
                dve.wait_ge(s("x_new"), NB)
                norm_dve(nc, dve, s, g, first, Y)
                for n in range(NB):
                    dve.wait_ge(s("q"), n + 1)
                    nc.vector.tensor_scalar(NEG[:, n, :], psum[:, 4 * n, :], g.bq_b[:, 0:1], 0.0,
                                            ALU.add, ALU.min).then_inc(s("q_neg"), 1)
                    nc.vector.tensor_scalar(Q[:, n, :], psum[:, 4 * n, :], g.bq_b[:, 0:1], 0.0,
                                            ALU.add, ALU.max).then_inc(s("q_pos"), 1)
                for n in range(NB):
                    dve.wait_ge(s("q_pos"), n + 1)
                    dve.wait_ge(s("q_exp"), n + 1)
                    nc.vector.tensor_tensor(Q[:, n, :], Q[:, n, :], E[:, n, :], ALU.add).then_inc(s("q_ready"), 1)
                for n in range(NB):
                    for half in range(2):
                        i = 2 * n + half
                        dve.wait_ge(s("kv"), i + 1)
                        nc.vector.tensor_scalar(NEGK[:, n, 2 * half:2 * half + 2, :],
                                                halves(n)[:, 2 * half:2 * half + 2, 0:P], 0.0, None,
                                                ALU.min).then_inc(s("k_neg"), 1)
                for n in range(NB):
                    for half in range(2):
                        i = 2 * n + half
                        dve.wait_ge(s("k_exp"), i + 1)
                        nc.vector.scalar_tensor_tensor(out=KT[:, n, 2 * half:2 * half + 2, :],
                                                       in0=halves(n)[:, 2 * half:2 * half + 2, 0:P], scalar=0.0,
                                                       in1=EK[:, n, 2 * half:2 * half + 2, :],
                                                       op0=ALU.max, op1=ALU.add).then_inc(s("k_ready"), 1)
                for n in range(NB):
                    dve.wait_ge(s("context"), n + 1)
                    nc.vector.tensor_tensor(CTX[:, n, :], psum[:, 4 * n, 0:P + HA], cst("block8"), ALU.mult)\
                      .then_inc(s("context_ready"), 1)
                for n in range(NB):
                    dve.wait_ge(s("by_token"), n + 1)
                    nc.vector.tensor_scalar(DEN[:, n, :, :], halves(n)[:, :, P:P + HA], 1e-6, None, ALU.add)\
                      .then_inc(s("den_ready"), 1)
                    dve.wait_ge(s("den_ready"), n + 1)
                    nc.vector.reciprocal(DEN[:, n, :, :], DEN[:, n, :, :]).then_inc(s("den_recip"), 1)
                    dve.wait_ge(s("den_recip"), n + 1)
                    nc.vector.tensor_tensor(OT[:, n, :, :, :],
                                            halves(n)[:, :, 0:P].rearrange("p t (h d) -> p t h d", d=DA),
                                            DEN[:, n, :, :, None].to_broadcast([P, 4, HA, DA]), ALU.mult)\
                      .then_inc(s("o_div"), 1)
                for n in range(NB):
                    dve.wait_ge(s("projected"), n + 1)
                    nc.vector.scalar_tensor_tensor(out=X[:, n, :], in0=psum[:, 4 * n, :], scalar=g.bo_b[:, 0:1],
                                                   in1=X[:, n, :], op0=ALU.add, op1=ALU.add).then_inc(s("2x_new"), 1)
                norm_dve(nc, dve, s, g, second, Y, "2")
                dve.wait_ge(s("2y_new"), 1)
                shift_high(nc, s, g, 0)
                shift_low(nc.vector, dve.wait_ge, s, g, 0)
        s.close()


def store(nc, g, out, pair):
    psum, X, Y = g.psum, g.X, g.Y
    with ExitStack() as ctx:
        OUT = ctx.enter_context(nc.sbuf_tensor("OUT", [P, NB, 4, P], F32))
        s = Phase(nc, "out")
        block = nc.Block()
        with block:
            @block.vector
            def _(dve):
                for n in range(NB):
                    nc.vector.tensor_tensor(X[:, n, :], X[:, n, :], Y[:, n, :], ALU.add).then_inc(s("x_new"), 1)

            @block.tensor
            def _(pe):
                for n in range(NB):
                    pe.wait_ge(s("x_new"), n + 1)
                    for t in range(4):
                        last = nc.tensor.transpose(psum[:, n, P * t:P * t + P], X[:, n, P * t:P * t + P], g.ident)
                    last.then_inc(s("turned"), 1)

            @block.scalar
            def _(act):
                for n in range(NB):
                    act.wait_ge(s("turned"), n + 1)
                    nc.scalar.activation(OUT[:, n, :, :].rearrange("p t d -> p (t d)"), psum[:, n, :], ACT.Copy)\
                      .then_inc(s("copied"), 1)

            @block.sync
            def _(sp):
                for n in range(NB):
                    sp.wait_ge(s("copied"), n + 1)
                    dst = out[bass.ds(pair * NB + n, 1)].rearrange("a (t p) d -> p (a t) d", p=P)
                    sp.dma_start(dst, OUT[:, n, :, :]).then_inc(s("stored"), 16)
                sp.wait_ge(s("stored"), 16 * NB)
        s.close()


def kernel(**inputs):
    import concourse.bacc as bacc
    from concourse.bass_utils import run_bass_kernel_spmd

    nc = bacc.Bacc("TRN2", target_bir_lowering=False, num_devices=1)
    arrays = {name: np.ascontiguousarray(a) for name, a in inputs.items()}
    c, b = constants()
    arrays["const"] = c
    arrays["constb"] = b
    args = {name: nc.dram_tensor(name + "_dram", a.shape, mybir.dt.from_np(a.dtype), kind="ExternalInput").ap()
            for name, a in arrays.items()}
    shape = inputs["L0_attn_a_x"].shape
    out = nc.dram_tensor("out_dram", shape, F32, kind="ExternalOutput").ap()
    build(nc, args, out)
    r = run_bass_kernel_spmd(nc, [{name + "_dram": a for name, a in arrays.items()}], core_ids=[0])
    return r.results[0]["out_dram"]
```
